# Optimizing a Trainium2 kernel written in Bass

```python
import numpy as np
import jax
import jax.numpy as jnp

def _softmax(x, axis=-1):
    return jax.nn.softmax(x, axis=axis)

def _gelu(x):
    return jax.nn.gelu(x, approximate=True)

def _silu(x):
    return jax.nn.silu(x)

def _sigmoid(x):
    return jax.nn.sigmoid(x)

def _layernorm(x, axis=-1, eps=1e-05):
    m = jnp.mean(x, axis=axis, keepdims=True)
    v = jnp.var(x, axis=axis, keepdims=True)
    return (x - m) / jnp.sqrt(v + eps)

def _scatter_add(tgt, idx, src, axis=0):
    return tgt.at[idx].add(src)

def _segment_sum(src, seg, n):
    return jax.ops.segment_sum(src, seg, n)
kernel_name = 'mk_seq_postln_d2_jaxref_r8_633dff'

def setup_inputs(seed: int=0):
    np.random.seed(seed)
    _w = jnp.asarray

    def _L0_attn_setup():
        import jax, jax.numpy as jnp
        import numpy as np
        B, T, C = (8, 128, 256)

        def _wkv(time_decay, time_first, k, v):
            w = -jnp.exp(time_decay.astype(jnp.float32))
            u = time_first.astype(jnp.float32)
            kf = k.astype(jnp.float32)
            vf = v.astype(jnp.float32)

            def step(carry, kv):
                num, den, mx = carry
                kt, vt = kv
                max_out = jnp.maximum(mx, kt + u)
                e1 = jnp.exp(mx - max_out)
                e2 = jnp.exp(kt + u - max_out)
                out = (e1 * num + e2 * vt) / (e1 * den + e2)
                max_st = jnp.maximum(mx + w, kt)
                e1s = jnp.exp(mx + w - max_st)
                e2s = jnp.exp(kt - max_st)
                return ((e1s * num + e2s * vt, e1s * den + e2s, max_st), out)
            Bn, Tn, Cn = k.shape
            init = (jnp.zeros((Bn, Cn), jnp.float32), jnp.zeros((Bn, Cn), jnp.float32), jnp.full((Bn, Cn), -1e+38, jnp.float32))
            kT = jnp.swapaxes(kf, 0, 1)
            vT = jnp.swapaxes(vf, 0, 1)
            _, outs = jax.lax.scan(step, init, (kT, vT))
            return jnp.swapaxes(outs, 0, 1).astype(k.dtype)
        key = jax.random.key(seed)
        ks = jax.random.split(key, 10)
        inp = {'x': jax.random.normal(ks[0], (B, T, C), dtype=jnp.float32), 'time_decay': jax.random.normal(ks[1], (C,), dtype=jnp.float32), 'time_first': jax.random.normal(ks[2], (C,), dtype=jnp.float32), 'time_mix_k': jax.random.uniform(ks[3], (C,), dtype=jnp.float32), 'time_mix_v': jax.random.uniform(ks[4], (C,), dtype=jnp.float32), 'time_mix_r': jax.random.uniform(ks[5], (C,), dtype=jnp.float32), 'Wk': jax.random.normal(ks[6], (C, C), dtype=jnp.float32) / np.sqrt(C), 'Wv': jax.random.normal(ks[7], (C, C), dtype=jnp.float32) / np.sqrt(C), 'Wr': jax.random.normal(ks[8], (C, C), dtype=jnp.float32) / np.sqrt(C), 'Wo': jax.random.normal(ks[9], (C, C), dtype=jnp.float32) / np.sqrt(C)}
        return inp
    _L0_attn_in = _L0_attn_setup()

    def _L0_ffn_setup():
        import jax, jax.numpy as jnp
        import numpy as np
        B, T, D = (1, 128, 256)
        F_DIM = 176
        E = 8
        TOPK = 2
        key = jax.random.key(seed)
        ks = jax.random.split(key, 5)
        x = jax.random.normal(ks[0], (B, T, D), dtype=jnp.float32)
        gate_w = jax.random.normal(ks[1], (E, D), dtype=jnp.float32) * 0.02
        gate_proj = jax.random.normal(ks[2], (E, F_DIM, D), dtype=jnp.float32) * 0.02
        up_proj = jax.random.normal(ks[3], (E, F_DIM, D), dtype=jnp.float32) * 0.02
        down_proj = jax.random.normal(ks[4], (E, D, F_DIM), dtype=jnp.float32) * 0.02
        return {'x': x, 'gate_w': gate_w, 'gate_proj': gate_proj, 'up_proj': up_proj, 'down_proj': down_proj}
    _L0_ffn_in = _L0_ffn_setup()

    def _L1_attn_setup():
        import jax, jax.numpy as jnp
        import numpy as np
        HID = 256
        HEADS = 16
        HD = HID // HEADS
        EPS = 1e-06

        def _heads(x, b, s):
            return x.reshape(b, s, HEADS, HD).transpose(0, 2, 1, 3)
        key = jax.random.key(seed)
        ks = jax.random.split(key, 9)
        s = 1.0 / np.sqrt(HID)
        return {'hidden_states': jax.random.normal(ks[0], (4, 512, HID), jnp.float32), 'q_w': jax.random.normal(ks[1], (HID, HID), jnp.float32) * s, 'q_b': jnp.zeros((HID,), jnp.float32), 'k_w': jax.random.normal(ks[2], (HID, HID), jnp.float32) * s, 'k_b': jnp.zeros((HID,), jnp.float32), 'v_w': jax.random.normal(ks[3], (HID, HID), jnp.float32) * s, 'v_b': jnp.zeros((HID,), jnp.float32), 'o_w': jax.random.normal(ks[4], (HID, HID), jnp.float32) * s, 'o_b': jnp.zeros((HID,), jnp.float32)}
    _L1_attn_in = _L1_attn_setup()

    def _L1_ffn_setup():
        import jax, jax.numpy as jnp
        import numpy as np
        EPS = 1e-08

        def _quantize(w):
            gamma = jnp.mean(jnp.abs(w))
            return jnp.clip(jnp.round(w / (gamma + EPS)), -1.0, 1.0)

        def _bitlinear(x, w):
            return jnp.matmul(x, _quantize(w).T)
        key = jax.random.key(seed)
        k1, k2, k3, k4 = jax.random.split(key, 4)
        d, h = (256, 704)
        x = jax.random.normal(k1, (4, 256, d), dtype=jnp.float32)
        w1 = jax.random.normal(k2, (h, d), dtype=jnp.float32)
        w2 = jax.random.normal(k3, (h, d), dtype=jnp.float32)
        w3 = jax.random.normal(k4, (d, h), dtype=jnp.float32)
        return {'x': x, 'w1': w1, 'w2': w2, 'w3': w3}
    _L1_ffn_in = _L1_ffn_setup()
    _d = {'L0_attn_x': _L0_attn_in['x'], 'L0_attn_time_decay': _L0_attn_in['time_decay'], 'L0_attn_time_first': _L0_attn_in['time_first'], 'L0_attn_time_mix_k': _L0_attn_in['time_mix_k'], 'L0_attn_time_mix_v': _L0_attn_in['time_mix_v'], 'L0_attn_time_mix_r': _L0_attn_in['time_mix_r'], 'L0_attn_Wk': _L0_attn_in['Wk'], 'L0_attn_Wv': _L0_attn_in['Wv'], 'L0_attn_Wr': _L0_attn_in['Wr'], 'L0_attn_Wo': _L0_attn_in['Wo'], 'L0_ffn_gate_w': _L0_ffn_in['gate_w'], 'L0_ffn_gate_proj': _L0_ffn_in['gate_proj'], 'L0_ffn_up_proj': _L0_ffn_in['up_proj'], 'L0_ffn_down_proj': _L0_ffn_in['down_proj'], 'L1_attn_q_w': _L1_attn_in['q_w'], 'L1_attn_q_b': _L1_attn_in['q_b'], 'L1_attn_k_w': _L1_attn_in['k_w'], 'L1_attn_k_b': _L1_attn_in['k_b'], 'L1_attn_v_w': _L1_attn_in['v_w'], 'L1_attn_v_b': _L1_attn_in['v_b'], 'L1_attn_o_w': _L1_attn_in['o_w'], 'L1_attn_o_b': _L1_attn_in['o_b'], 'L1_ffn_w1': _L1_ffn_in['w1'], 'L1_ffn_w2': _L1_ffn_in['w2'], 'L1_ffn_w3': _L1_ffn_in['w3']}
    _x0 = _d['L0_attn_x']
    _d['L0_attn_x'] = jax.random.normal(jax.random.fold_in(jax.random.key(seed), 1), (8, 256, 256), dtype=_x0.dtype)
    del _x0
    return _d

def reference(L0_attn_x, L0_attn_time_decay, L0_attn_time_first, L0_attn_time_mix_k, L0_attn_time_mix_v, L0_attn_time_mix_r, L0_attn_Wk, L0_attn_Wv, L0_attn_Wr, L0_attn_Wo, L0_ffn_gate_w, L0_ffn_gate_proj, L0_ffn_up_proj, L0_ffn_down_proj, L1_attn_q_w, L1_attn_q_b, L1_attn_k_w, L1_attn_k_b, L1_attn_v_w, L1_attn_v_b, L1_attn_o_w, L1_attn_o_b, L1_ffn_w1, L1_ffn_w2, L1_ffn_w3):

    def _L0_attn_ref(x, time_decay, time_first, time_mix_k, time_mix_v, time_mix_r, Wk, Wv, Wr, Wo):
        import jax, jax.numpy as jnp
        import numpy as np
        B, T, C = (8, 128, 256)

        def _wkv(time_decay, time_first, k, v):
            w = -jnp.exp(time_decay.astype(jnp.float32))
            u = time_first.astype(jnp.float32)
            kf = k.astype(jnp.float32)
            vf = v.astype(jnp.float32)

            def step(carry, kv):
                num, den, mx = carry
                kt, vt = kv
                max_out = jnp.maximum(mx, kt + u)
                e1 = jnp.exp(mx - max_out)
                e2 = jnp.exp(kt + u - max_out)
                out = (e1 * num + e2 * vt) / (e1 * den + e2)
                max_st = jnp.maximum(mx + w, kt)
                e1s = jnp.exp(mx + w - max_st)
                e2s = jnp.exp(kt - max_st)
                return ((e1s * num + e2s * vt, e1s * den + e2s, max_st), out)
            Bn, Tn, Cn = k.shape
            init = (jnp.zeros((Bn, Cn), jnp.float32), jnp.zeros((Bn, Cn), jnp.float32), jnp.full((Bn, Cn), -1e+38, jnp.float32))
            kT = jnp.swapaxes(kf, 0, 1)
            vT = jnp.swapaxes(vf, 0, 1)
            _, outs = jax.lax.scan(step, init, (kT, vT))
            return jnp.swapaxes(outs, 0, 1).astype(k.dtype)
        shifted = jnp.pad(x, ((0, 0), (1, 0), (0, 0)))[:, :-1]
        xk = x * time_mix_k + shifted * (1.0 - time_mix_k)
        xv = x * time_mix_v + shifted * (1.0 - time_mix_v)
        xr = x * time_mix_r + shifted * (1.0 - time_mix_r)
        k = jnp.einsum('btc,dc->btd', xk, Wk)
        v = jnp.einsum('btc,dc->btd', xv, Wv)
        r = jnp.einsum('btc,dc->btd', xr, Wr)
        sr = jax.nn.sigmoid(r)
        rwkv = _wkv(time_decay, time_first, k, v)
        return jnp.einsum('btd,cd->btc', sr * rwkv, Wo)

    def _L0_ffn_ref(x, gate_w, gate_proj, up_proj, down_proj):
        import jax, jax.numpy as jnp
        import numpy as np
        B, T, D = (1, 128, 256)
        F_DIM = 176
        E = 8
        TOPK = 2
        b, t, d = x.shape
        x_flat = x.reshape(-1, d)
        n = x_flat.shape[0]
        router_logits = x_flat @ gate_w.T
        top_w, sel = jax.lax.top_k(router_logits, TOPK)
        top_w = jax.nn.softmax(top_w, axis=-1)
        tok_ids = jnp.arange(n)[:, None]
        tw = jnp.zeros((n, E), dtype=x.dtype).at[tok_ids, sel].add(top_w)
        g = jnp.einsum('nd,efd->enf', x_flat, gate_proj)
        u = jnp.einsum('nd,efd->enf', x_flat, up_proj)
        h = jax.nn.silu(g) * u
        eo = jnp.einsum('enf,edf->end', h, down_proj)
        out = jnp.einsum('end,ne->nd', eo, tw)
        return out.reshape(b, t, d)

    def _L1_attn_ref(hidden_states, q_w, q_b, k_w, k_b, v_w, v_b, o_w, o_b):
        import jax, jax.numpy as jnp
        import numpy as np
        HID = 256
        HEADS = 16
        HD = HID // HEADS
        EPS = 1e-06

        def _heads(x, b, s):
            return x.reshape(b, s, HEADS, HD).transpose(0, 2, 1, 3)
        b, s, _ = hidden_states.shape
        q = _heads(hidden_states @ q_w.T + q_b, b, s)
        k = _heads(hidden_states @ k_w.T + k_b, b, s)
        v = _heads(hidden_states @ v_w.T + v_b, b, s)
        qp = jax.nn.elu(q) + 1.0
        kp = jax.nn.elu(k) + 1.0
        kv = jnp.einsum('bhsd,bhse->bhde', kp, v)
        z = jnp.einsum('bhsd,bhd->bhs', qp, kp.sum(axis=2))[..., None]
        attn = jnp.einsum('bhsd,bhde->bhse', qp, kv) / (z + EPS)
        out = attn.transpose(0, 2, 1, 3).reshape(b, s, HID)
        return out @ o_w.T + o_b

    def _L1_ffn_ref(x, w1, w2, w3):
        import jax, jax.numpy as jnp
        import numpy as np
        EPS = 1e-08

        def _quantize(w):
            gamma = jnp.mean(jnp.abs(w))
            return jnp.clip(jnp.round(w / (gamma + EPS)), -1.0, 1.0)

        def _bitlinear(x, w):
            return jnp.matmul(x, _quantize(w).T)
        x1 = _bitlinear(x, w1)
        x2 = _bitlinear(x, w2)
        hidden = jax.nn.sigmoid(x1) * x2
        return _bitlinear(hidden, w3)
    x = L0_attn_x
    x = _layernorm(x + _L0_attn_ref(x, L0_attn_time_decay, L0_attn_time_first, L0_attn_time_mix_k, L0_attn_time_mix_v, L0_attn_time_mix_r, L0_attn_Wk, L0_attn_Wv, L0_attn_Wr, L0_attn_Wo), axis=-1)
    x = _layernorm(x + _L0_ffn_ref(x, L0_ffn_gate_w, L0_ffn_gate_proj, L0_ffn_up_proj, L0_ffn_down_proj), axis=-1)
    x = _layernorm(x + _L1_attn_ref(x, L1_attn_q_w, L1_attn_q_b, L1_attn_k_w, L1_attn_k_b, L1_attn_v_w, L1_attn_v_b, L1_attn_o_w, L1_attn_o_b), axis=-1)
    x = _layernorm(x + _L1_ffn_ref(x, L1_ffn_w1, L1_ffn_w2, L1_ffn_w3), axis=-1)
    return x

_drawn_inputs = setup_inputs


def setup_inputs(seed=0):
    import zlib

    import numpy as np

    out = dict(_drawn_inputs(seed))
    spreads = {'L1_attn_q_b': (0.0, 0.8),
     'L1_attn_k_b': (0.0, 0.8),
     'L1_attn_v_b': (0.0, 0.1),
     'L1_attn_o_b': (0.0, 0.1)}
    factors = {'L0_ffn_gate_w': 3.866,
     'L0_ffn_gate_proj': 3.408,
     'L0_ffn_up_proj': 3.378,
     'L0_ffn_down_proj': 3.377,
     'L1_attn_q_w': 3.44}
    for name, (base, spread) in spreads.items():
        noise = np.random.default_rng([zlib.crc32(name.encode()), seed]).standard_normal(out[name].shape)
        drawn = base * np.exp(spread * noise) if base else spread * noise
        out[name] = jnp.asarray(drawn.astype(out[name].dtype))
    for name, factor in factors.items():
        out[name] = (out[name] * factor).astype(out[name].dtype)
    return out
```

```python
from contextlib import ExitStack

import concourse.bass as bass
from concourse import mybir

P = 128
F32 = mybir.dt.float32
F32R = mybir.dt.float32r
U32 = mybir.dt.uint32
ALU = mybir.AluOpType
ACT = mybir.ActivationFunctionType
AX_X = mybir.AxisListType.X

B, T, C = 8, 256, 256
KC = C // P
NT = T // P
E, F = 8, 176
FE = P // E
NCH = F // FE
HID = 704
NF = -(-HID // P)
HEAD = 16
NH = C // HEAD
LN_EPS = 1e-5
Z_EPS = 1e-6
GAMMA_EPS = 1e-8
LOW = -1e38
MIX, U_COL, TD_COL, QB_COL = 0, 3, 4, 5
NVEC = 6
HDEPTH = 4
SDEPTH = 3


def rotating(c, depth, per_batch=NCH):
    if c >= depth:
        return depth
    back = [x for x in range(per_batch) if x % depth == c % depth][-1]
    return per_batch - back + c


def past(eng, sem, value):
    if isinstance(value, int) and value < 1:
        return
    eng.wait_ge(sem, value)


def build(nc, xT, x, vecs, rows, consts, mask, Wk, Wv, Wr, Wo, gate_w, w_gate, w_up, w_down,
          Wq3, Wk3, Wv3, Wo3, W1, W2, W3, out):
    ctx = ExitStack()
    with ctx:
        def sb(name, shape, dt=F32):
            return ctx.enter_context(nc.sbuf_tensor(name, shape, dt))

        def pb(name, shape):
            return ctx.enter_context(nc.psum_tensor(name, shape, F32))

        def sem(name):
            return ctx.enter_context(nc.semaphore(name))

        wkvr = sb("wkvr", [P, 3, KC, C])
        wo1 = sb("wo1", [P, KC, C])
        wqkv = sb("wqkv", [P, 3, KC, C])
        wo3 = sb("wo3", [P, KC, C])
        gw = sb("gw", [P, KC, E])
        gate_hi = sb("gate_hi", [P, KC, NCH * P], F32R)
        gate_lo = sb("gate_lo", [P, KC, NCH * P], F32R)
        up_hi = sb("up_hi", [P, KC, NCH * P], F32R)
        up_lo = sb("up_lo", [P, KC, NCH * P], F32R)
        down_hi = sb("down_hi", [P, NCH, C], F32R)
        down_lo = sb("down_lo", [P, NCH, C], F32R)
        w1q = sb("w1q", [P, KC, NF * P], F32R)
        w2q = sb("w2q", [P, KC, NF * P], F32R)
        w3q = sb("w3q", [P, NF, C], F32R)
        vec = sb("vec", [P, KC, NVEC])
        wdec = sb("wdec", [P, KC])
        qb1 = sb("qb1", [P, KC])
        bias = sb("bias", [P, 3, C])
        cst = sb("cst", [P, 2, P])
        msk = sb("msk", [P, C])
        ones = sb("ones", [P, P])
        neghalf = sb("neghalf", [P, NT])
        eps = sb("eps", [P, NT])
        ident = cst[:, 0, :]
        expert_of = cst[:, 1, :]

        xs = sb("xs", [P, KC, 1 + T])
        dx = sb("dx", [P, KC, T])
        mix = sb("mix", [P, 3, KC, T])
        kS = sb("kS", [P, KC, T])
        vS = sb("vS", [P, KC, T])
        ra = sb("ra", [P, KC, T])
        rn = sb("rn", [P, KC, T])
        M = sb("M", [P, KC, 1 + T])
        AR = sb("AR", [P, 4, KC, T])
        V2 = sb("V2", [P, 2, KC, T])
        ND = sb("ND", [P, 2, KC, 1 + T])
        y = sb("y", [P, KC, T])
        x1 = sb("x1", [P, NT, C])
        x1k = sb("x1k", [P, NT, C])
        x4 = sb("x4", [P, NT, C])
        x1T = sb("x1T", [P, KC, T])
        x1h = sb("x1h", [P, KC, T], F32R)
        x1l = sb("x1l", [P, KC, T], F32R)
        hb = sb("hb", [P, HDEPTH, T])
        hh = sb("hh", [P, SDEPTH, T], F32R)
        hl = sb("hl", [P, SDEPTH, T], F32R)
        TW = sb("TW", [P, T])
        twt = sb("twt", [P, NT, P])
        twb = sb("twb", [P, NT, P])
        lg = sb("lg", [P, NT, E])
        mx8 = sb("mx8", [P, NT, 8])
        ix8 = sb("ix8", [P, NT, 8], U32)
        sel = sb("sel", [P, NT, 2])
        gap = sb("gap", [P, NT])
        top = sb("top", [P, 2, NT])
        STAGE = KC * NCH * P
        arena = sb("arena", [P, 2 * STAGE])
        stage = [arena[:, i * STAGE:(i + 1) * STAGE] for i in range(2)]
        U = KC * T
        x2 = arena[:, 0:U].rearrange("p (t c) -> p t c", t=NT)
        x3 = arena[:, U:2 * U].rearrange("p (t c) -> p t c", t=NT)
        xT2 = arena[:, 2 * U:3 * U].rearrange("p (k t) -> p k t", k=KC)
        qS = arena[:, 3 * U:4 * U].rearrange("p (k t) -> p k t", k=KC)
        kt = arena[:, 4 * U:5 * U].rearrange("p (t c) -> p t c", t=NT)
        ke = arena[:, 5 * U:6 * U].rearrange("p (t c) -> p t c", t=NT)
        vx = arena[:, 6 * U:6 * U + NT * 3 * P].rearrange("p (t j c) -> p t j c", t=NT, j=3)
        kvm = arena[:, 7 * U + C:8 * U + C].rearrange("p (k c) -> p k c", k=KC)
        an = arena[:, 8 * U + C:9 * U + C].rearrange("p (t c) -> p t c", t=NT)
        anT = arena[:, 9 * U + C:10 * U + C].rearrange("p (k t) -> p k t", k=KC)
        assert 10 * U + C <= 2 * STAGE and 6 * U + NT * 3 * P <= 7 * U + C
        zr = sb("zr", [P, NT, NH])
        x3h = sb("x3h", [P, KC, T], F32R)
        x3l = sb("x3l", [P, KC, T], F32R)
        fb = sb("fb", [P, SDEPTH, T])
        fh = sb("fh", [P, SDEPTH, T], F32R)
        fl = sb("fl", [P, SDEPTH, T], F32R)
        wsum = sb("wsum", [P, 3])
        thr = sb("thr", [P, 2, 3])
        st = sb("st", [P, 4, NT, 6])
        mv = sb("mv", [P, 4, NT, 2])
        ve = sb("ve", [P, 4, NT])
        rs = sb("rs", [P, 4, NT])

        G = pb("G", [P, 2, 2, T])
        D = pb("D", [P, NT, C])
        Tb = pb("Tb", [P, KC, T])
        Q = pb("Q", [P, 3, 2 * T])
        O = pb("O", [P, NT, C])

        in_vec, in_msk, in_wkvr, in_wo1, in_gw, in_xT, in_x = map(sem, ("in_vec", "in_msk", "in_wkvr", "in_wo1", "in_gw", "in_xT", "in_x"))
        in_gate, in_up, in_down, in_w12, in_w3 = map(sem, ("in_gate", "in_up", "in_down", "in_w12", "in_w3"))
        in_wqkv, in_wo3, out_x4 = map(sem, ("in_wqkv", "in_wo3", "out_x4"))
        preset, decay_e, wdec_ok, pads_ok, qb1_ok = map(sem, ("preset", "decay_e", "wdec_ok", "pads_ok", "qb1_ok"))
        gate_hi_ok, gate_lo_ok = sem("gate_hi_ok"), sem("gate_lo_ok")
        up_hi_ok, up_lo_ok = sem("up_hi_ok"), sem("up_lo_ok")
        down_hi_ok, down_lo_ok = sem("down_hi_ok"), sem("down_lo_ok")
        wsum_ok, gamma_ok, thr_ok, w12a_ok, w12q_ok, w3a_ok, w3q_ok = map(
            sem, ("wsum_ok", "gamma_ok", "thr_ok", "w12a_ok", "w12q_ok", "w3a_ok", "w3q_ok"))
        dx_ok, mix_ok, kvr_ok, kv_ok, ra_ok, M_ok = map(
            sem, ("dx_ok", "mix_ok", "kvr_ok", "kv_ok", "ra_ok", "M_ok"))
        lag_ok, ar_ok, exps_ok, ea_ok, v2_ok, nd_ok, t1_ok = map(
            sem, ("lag_ok", "ar_ok", "exps_ok", "ea_ok", "v2_ok", "nd_ok", "t1_ok"))
        nd2_ok, qq_ok, ln_ok, arg_ok, sr_ok, y_ok, o1_ok = map(
            sem, ("nd2_ok", "qq_ok", "ln_ok", "arg_ok", "sr_ok", "y_ok", "o1_ok"))
        r_ok = [sem(f"r{i}_ok") for i in range(4)]
        st_ok = [sem(f"st{i}_ok") for i in range(4)]
        mv_ok = [sem(f"mv{i}_ok") for i in range(4)]
        ve_ok = [sem(f"ve{i}_ok") for i in range(4)]
        rs_ok = [sem(f"rs{i}_ok") for i in range(4)]
        x_ok = [sem(f"x{i}_ok") for i in range(4)]
        x1k_ok, x1Tp_ok, x1T_ok, x1h_ok, x1l_ok = map(sem, ("x1k_ok", "x1Tp_ok", "x1T_ok", "x1h_ok", "x1l_ok"))
        router_ok, lg_ok, mx_ok, ix_ok, gap_ok, tanh_ok, sel_ok, top_ok, twab_ok, twt_ok, twp_ok, tw_ok = map(
            sem, ("router_ok", "lg_ok", "mx_ok", "ix_ok", "gap_ok", "tanh_ok", "sel_ok", "top_ok", "twab_ok",
                  "twt_ok", "twp_ok", "tw_ok"))
        gu_ok, silu_ok, hu_ok, h_ok, hh_ok, hl_ok, down_ok = map(
            sem, ("gu_ok", "silu_ok", "hu_ok", "h_ok", "hh_ok", "hl_ok", "down_ok"))
        x2Tp_ok, x2T_ok, x2b_ok, q_ok, k_ok, v_ok = map(sem, ("x2Tp_ok", "x2T_ok", "x2b_ok", "q_ok", "k_ok", "v_ok"))
        qt_ok, qe_ok, qp_ok, kt_ok, kc_ok, ke_ok, kp_ok, vx_ok = map(
            sem, ("qt_ok", "qe_ok", "qp_ok", "kt_ok", "kc_ok", "ke_ok", "kp_ok", "vx_ok"))
        kvp_ok, kvm_ok, at_ok, ze_ok, zr_ok, an_ok, anTp_ok, anT_ok, o3_ok = map(
            sem, ("kvp_ok", "kvm_ok", "at_ok", "ze_ok", "zr_ok", "an_ok", "anTp_ok", "anT_ok", "o3_ok"))
        x3Tp_ok, x3h_ok, x3l_ok, f12_ok, th_ok, fx_ok, fh_ok, fl_ok, w3_ok = map(
            sem, ("x3Tp_ok", "x3h_ok", "x3l_ok", "f12_ok", "th_ok", "fx_ok", "fh_ok", "fl_ok", "w3_ok"))

        xT_v = xT.rearrange("(k p) (n t) -> n p k t", p=P, t=T)
        x_v = x.rearrange("n (t p) c -> n p t c", p=P)
        out_v = out.rearrange("n (t p) c -> n p t c", p=P)

        def batch_of(view, n):
            return view[bass.ds(n, 1)].rearrange("n p a b -> (n p) a b") if not isinstance(n, int) else view[n]

        def chunked(w):
            return w.rearrange("(k p) d -> p k d", p=P)

        LOOP = (2, B - 2)

        def slots(eng, slot):
            for b in range(-2, LOOP[0]):
                slot(b, 0 <= b, 1 <= b, -1 <= b, True)
            with eng.Fori(*LOOP) as b:
                slot(b, True, True, True, True)
            for b in range(LOOP[1], B + 1):
                slot(b, b < B, True, b + 1 < B, b + 2 < B)

        block = ctx.enter_context(nc.Block())

        @block.sync
        def _(sp):
            sp.dma_start(vec[:, :, :], vecs).then_inc(in_vec, 16)
            sp.dma_start(cst[:, :, :], consts).then_inc(in_vec, 16)
            sp.dma_start(xs[:, :, 1:], xT_v[0]).then_inc(in_xT, 16)
            for j, w in enumerate((Wk, Wv, Wr)):
                sp.dma_start(wkvr[:, j, :, :], chunked(w)).then_inc(in_wkvr, 16)
            sp.dma_start(stage[0], w_gate).then_inc(in_gate, 16)
            sp.dma_start(wo1[:, :, :], chunked(Wo)).then_inc(in_wo1, 16)
            sp.dma_start(stage[1], w_up).then_inc(in_up, 16)
            sp.dma_start(gw[:, :, :], chunked(gate_w)).then_inc(in_gw, 16)

            def slot(b, experts, attn, rwkv, proj):
                if proj:
                    if not (isinstance(b, int) and b == -2):
                        sp.wait_ge(mix_ok, b + 2)
                        sp.dma_start(xs[:, :, 1:], batch_of(xT_v, b + 2)).then_inc(in_xT, 16)
                if rwkv:
                    if experts:
                        sp.wait_ge(x1k_ok, b + 1)
                        sp.wait_ge(x1Tp_ok, b + 1)
                    sp.dma_start(x1[:, :, :], batch_of(x_v, b + 1)).then_inc(in_x, 16)
                if isinstance(b, int) and b == -2:
                    sp.dma_start(msk[:, :], mask).then_inc(in_msk, 16)
                    for i in range(3):
                        sp.dma_start(bias[:, i, :], rows[i:i + 1, :].broadcast_to([P, C])).then_inc(in_msk, 16)
                    sp.wait_ge(gate_hi_ok, 1)
                    sp.wait_ge(gate_lo_ok, 1)
                    sp.dma_start(stage[0], w_down).then_inc(in_down, 16)
                    sp.wait_ge(up_hi_ok, 1)
                    sp.wait_ge(up_lo_ok, 1)
                    for i, w in enumerate((W1, W2)):
                        sp.dma_start(stage[1][:, i * KC * HID:(i + 1) * KC * HID].rearrange("p (k n) -> p k n", k=KC),
                                     chunked(w)).then_inc(in_w12, 16)
                    for j, w in enumerate((Wq3, Wk3, Wv3)):
                        sp.dma_start(wqkv[:, j, :, :], chunked(w)).then_inc(in_wqkv, 16)
                    sp.dma_start(wo3[:, :, :], chunked(Wo3)).then_inc(in_wo3, 16)
                if isinstance(b, int) and b == -1:
                    sp.wait_ge(down_hi_ok, 1)
                    sp.wait_ge(down_lo_ok, 1)
                    full = HID // P
                    raw3 = stage[0][:, 0:NF * C].rearrange("p (k c) -> p k c", k=NF)
                    sp.dma_start(raw3[:, 0:full, :], chunked(W3[0:full * P, :])).then_inc(in_w3, 16)
                    sp.dma_start(raw3[0:HID - full * P, full, :], W3[full * P:HID, :]).then_inc(in_w3, 16)
                if attn:
                    sp.wait_ge(x_ok[3], b)
                    sp.dma_start(batch_of(out_v, b - 1), x4[:, :, :]).then_inc(out_x4, 16)

            slots(sp, slot)
            sp.wait_ge(out_x4, 16 * B)

        @block.tensor
        def _(pe):
            def f32_product(dst, pairs):
                for i, (l, r) in enumerate(pairs):
                    last = pe.matmul(dst, l, r, start=i == 0, stop=i == len(pairs) - 1)
                return last

            def transposes(src, dst):
                for t in range(NT):
                    for k in range(KC):
                        last = pe.transpose(dst[:, k, t * P:(t + 1) * P], src[:, t, k * P:(k + 1) * P], ident)
                return last

            def gate_up(b, c):
                if c == 0:
                    pe.wait_ge(x1h_ok, b + 1)
                    pe.wait_ge(x1l_ok, b + 1)
                past(pe, hu_ok, NCH * b + c - 1)
                cols = slice(c * P, (c + 1) * P)
                for i, (wh, wl) in enumerate(((gate_hi, gate_lo), (up_hi, up_lo))):
                    last = f32_product(G[:, c % 2, i, :], [
                        (w[:, k, cols], xx[:, k, :]) for k in range(KC)
                        for w, xx in ((wh, x1h), (wh, x1l), (wl, x1h))])
                last.then_inc(gu_ok, 1)

            def down(b, c):
                pe.wait_ge(hl_ok, NCH * b + c + 1)
                if c == 0:
                    if isinstance(b, int) and b == 0:
                        pe.wait_ge(down_hi_ok, 1)
                        pe.wait_ge(down_lo_ok, 1)
                    past(pe, r_ok[1], b)
                s = c % SDEPTH
                for t in range(NT):
                    tok = slice(t * P, (t + 1) * P)
                    for i, (l, r) in enumerate(((hh, down_hi), (hh, down_lo), (hl, down_hi))):
                        last = pe.matmul(D[:, t, :], l[:, s, tok], r[:, c, :], start=c == 0 and t == 0 and i == 0,
                                         stop=c == NCH - 1 and i == 2, skip_group_check=True)
                last.then_inc(down_ok, 1)

            def router(b):
                pe.wait_ge(x1T_ok, b + 1)
                for t in range(NT):
                    last = f32_product(O[:, 0, t * E:(t + 1) * E],
                                       [(x1T[:, k, t * P:(t + 1) * P], gw[:, k, :]) for k in range(KC)])
                last.then_inc(router_ok, 1)

            def ternary(b, f):
                if f == 0:
                    pe.wait_ge(x3h_ok, b)
                    pe.wait_ge(x3l_ok, b)
                    if isinstance(b, int) and b == 1:
                        pe.wait_ge(w12q_ok, 1)
                if f < 3:
                    if not isinstance(b, int) or b + 2 < B:
                        pe.wait_ge(kv_ok, b + 3)
                        pe.wait_ge(ra_ok, b + 3)
                else:
                    pe.wait_ge(fx_ok, NF * (b - 1) + f - 2)
                cols = slice(f * P, (f + 1) * P)
                for i, w in enumerate((w1q, w2q)):
                    last = f32_product(Q[:, f % 3, i * T:(i + 1) * T],
                                       [(w[:, k, cols], xx[:, k, :]) for k in range(KC) for xx in (x3h, x3l)])
                last.then_inc(f12_ok, 1)

            def ternary_out(b, f):
                pe.wait_ge(fl_ok, NF * (b - 1) + f + 1)
                if f == 0 and (not isinstance(b, int) or b + 1 < B):
                    pe.wait_ge(r_ok[0], b + 2)
                if f == 0 and isinstance(b, int) and b == 1:
                    pe.wait_ge(w3q_ok, 1)
                for t in range(NT):
                    tok = slice(t * P, (t + 1) * P)
                    for i, l in enumerate((fh, fl)):
                        last = pe.matmul(O[:, t, :], l[:, f % SDEPTH, tok], w3q[:, f, :],
                                         start=f == 0 and t == 0 and i == 0, stop=f == NF - 1 and i == 1,
                                         skip_group_check=True)
                last.then_inc(w3_ok, 1)

            def slot(b, experts, attn, rwkv, proj):
                first = isinstance(b, int) and b == 0
                if experts:
                    if first:
                        for s in (gate_hi_ok, gate_lo_ok, up_hi_ok, up_lo_ok):
                            pe.wait_ge(s, 1)
                    gate_up(b, 0)
                    gate_up(b, 1)
                if attn:
                    pe.wait_ge(x_ok[1], b)
                    if not isinstance(b, int) or b < B:
                        pe.wait_ge(x1T_ok, b + 1)
                    transposes(x2, Tb).then_inc(x2Tp_ok, 1)
                if experts:
                    if first:
                        pe.wait_ge(in_gw, 16)
                    router(b)
                if attn:
                    pe.wait_ge(x2T_ok, b)
                    if isinstance(b, int) and b == 1:
                        pe.wait_ge(in_wqkv, 48)
                    past(pe, fx_ok, NF * (b - 1))
                    for d in range(KC):
                        last = f32_product(Q[:, 0, d * T:(d + 1) * T],
                                           [(wqkv[:, 0, k, d * P:(d + 1) * P], xT2[:, k, :]) for k in range(KC)])
                    last.then_inc(q_ok, 1)
                    for j, s in ((1, k_ok), (2, v_ok)):
                        for t in range(NT):
                            last = f32_product(Q[:, j, t * C:(t + 1) * C],
                                               [(xT2[:, k, t * P:(t + 1) * P], wqkv[:, j, k, :]) for k in range(KC)])
                        last.then_inc(s, 1)
                if experts:
                    gate_up(b, 2)
                    pe.wait_ge(twt_ok, b + 1)
                    if attn:
                        pe.wait_ge(x2T_ok, b)
                    for t in range(NT):
                        last = pe.transpose(Tb[:, 0, t * P:(t + 1) * P], twt[:, t, :], ident)
                    last.then_inc(twp_ok, 1)
                    gate_up(b, 3)
                if attn:
                    pe.wait_ge(kp_ok, b)
                    pe.wait_ge(vx_ok, b)
                    pe.wait_ge(qp_ok, b)
                    for d in range(KC):
                        last = f32_product(Q[:, 0, d * C:(d + 1) * C],
                                           [(ke[:, t, d * P:(d + 1) * P], vx[:, t, d:d + 2, :]) for t in range(NT)])
                    last.then_inc(kvp_ok, 1)
                if experts:
                    gate_up(b, 4)
                    down(b, 0)
                    down(b, 1)
                if attn:
                    pe.wait_ge(kvm_ok, b)
                    for t in range(NT):
                        for d in range(KC):
                            last = pe.matmul(Q[:, 1 + t, d * C:(d + 1) * C], qS[:, d, t * P:(t + 1) * P],
                                             kvm[:, d, :], start=True, stop=True)
                    last.then_inc(at_ok, 1)
                if experts:
                    gate_up(b, 5)
                    down(b, 2)
                if proj:
                    pe.wait_ge(mix_ok, b + 3)
                    if isinstance(b, int) and b == -2:
                        pe.wait_ge(in_wkvr, 48)
                    if attn:
                        pe.wait_ge(an_ok, b)
                    elif isinstance(b, int) and b > -2:
                        for s in (kv_ok, ra_ok):
                            pe.wait_ge(s, b + 2)
                    for j in range(3):
                        for d in range(KC):
                            last = f32_product(Q[:, j, d * T:(d + 1) * T],
                                               [(wkvr[:, j, k, d * P:(d + 1) * P], mix[:, j, k, :])
                                                for k in range(KC)])
                    last.then_inc(kvr_ok, 1)
                if attn:
                    pe.wait_ge(an_ok, b)
                    if experts:
                        pe.wait_ge(tw_ok, b + 1)
                    transposes(an, Tb).then_inc(anTp_ok, 1)
                if experts:
                    gate_up(b, 6)
                    down(b, 3)
                if attn:
                    pe.wait_ge(anT_ok, b)
                    if isinstance(b, int) and b == 1:
                        pe.wait_ge(in_wo3, 16)
                    if experts:
                        pe.wait_ge(lg_ok, b + 1)
                    else:
                        pe.wait_ge(r_ok[3], b - 1)
                    for t in range(NT):
                        last = f32_product(O[:, t, :],
                                           [(anT[:, k, t * P:(t + 1) * P], wo3[:, k, :]) for k in range(KC)])
                    last.then_inc(o3_ok, 1)
                if first:
                    pe.wait_ge(wsum_ok, 3)
                    pe.wait_ge(lg_ok, 1)
                    pe.matmul(O[:, 0, 0:3], ones[:, :], wsum[:, :], start=True, stop=True).then_inc(gamma_ok, 1)
                if experts:
                    gate_up(b, 7)
                    down(b, 4)
                if rwkv:
                    pe.wait_ge(y_ok, b + 2)
                    if isinstance(b, int) and b == -1:
                        pe.wait_ge(in_wo1, 16)
                    if attn:
                        pe.wait_ge(r_ok[2], b)
                    elif first:
                        pe.wait_ge(thr_ok, 1)
                    for t in range(NT):
                        last = f32_product(O[:, t, :],
                                           [(y[:, k, t * P:(t + 1) * P], wo1[:, k, :]) for k in range(KC)])
                    last.then_inc(o1_ok, 1)
                if experts:
                    gate_up(b, 8)
                    down(b, 5)
                if attn:
                    pe.wait_ge(x_ok[2], b)
                    pe.wait_ge(anT_ok, b)
                    transposes(x3, Tb).then_inc(x3Tp_ok, 1)
                if experts:
                    gate_up(b, 9)
                    down(b, 6)
                if attn:
                    ternary(b, 0)
                    ternary(b, 1)
                if experts:
                    gate_up(b, 10)
                    down(b, 7)
                if attn:
                    ternary(b, 2)
                    ternary_out(b, 0)
                if rwkv:
                    pe.wait_ge(x_ok[0], b + 2)
                    if attn:
                        pe.wait_ge(x3l_ok, b)
                    elif experts:
                        pe.wait_ge(tw_ok, b + 1)
                    transposes(x1, Tb).then_inc(x1Tp_ok, 1)
                if attn:
                    ternary(b, 3)
                    ternary_out(b, 1)
                if experts:
                    down(b, 8)
                if attn:
                    ternary(b, 4)
                    ternary_out(b, 2)
                if experts:
                    down(b, 9)
                if attn:
                    ternary(b, 5)
                    ternary_out(b, 3)
                if experts:
                    down(b, 10)
                if attn:
                    ternary_out(b, 4)
                    ternary_out(b, 5)

            pe.wait_ge(in_vec, 32)
            pe.wait_ge(preset, 3)
            slots(pe, slot)

        @block.scalar
        def _(act):
            def copy(dst, src):
                return act.activation(dst, src, ACT.Copy)

            def silu(b, c):
                act.wait_ge(gu_ok, NCH * b + c + 1)
                past(act, hl_ok, NCH * b + c + 1 - rotating(c, HDEPTH))
                act.activation(hb[:, c % HDEPTH, :], G[:, c % 2, 0, :], ACT.Silu).then_inc(silu_ok, 1)

            def h_high(b, c):
                act.wait_ge(h_ok, NCH * b + c + 1)
                past(act, down_ok, NCH * b + c + 1 - rotating(c, SDEPTH))
                copy(hh[:, c % SDEPTH, :], hb[:, c % HDEPTH, :]).then_inc(hh_ok, 1)

            def tanh_half(b, f):
                act.wait_ge(f12_ok, NF * (b - 1) + f + 1)
                past(act, fl_ok, NF * (b - 1) + f + 1 - SDEPTH)
                act.activation(fb[:, f % SDEPTH, :], Q[:, f % 3, 0:T], ACT.Tanh, scale=0.5).then_inc(th_ok, 1)

            def f_high(b, f):
                act.wait_ge(fx_ok, NF * (b - 1) + f + 1)
                past(act, w3_ok, NF * (b - 1) + f + 1 - SDEPTH)
                copy(fh[:, f % SDEPTH, :], fb[:, f % SDEPTH, :]).then_inc(fh_ok, 1)

            def slot(b, experts, attn, rwkv, proj):
                if experts:
                    act.wait_ge(x_ok[0], b + 1)
                    past(act, r_ok[1], b)
                    copy(x1k[:, :, :], x1[:, :, :]).then_inc(x1k_ok, 1)
                    silu(b, 0)
                    silu(b, 1)
                if attn:
                    act.wait_ge(x2Tp_ok, b)
                    copy(xT2, Tb[:, :, :]).then_inc(x2T_ok, 1)
                if experts:
                    act.wait_ge(gap_ok, b + 1)
                    act.activation(gap[:, :], gap[:, :], ACT.Tanh, scale=0.5).then_inc(tanh_ok, 1)
                if rwkv:
                    act.wait_ge(ar_ok, b + 2)
                    act.activation(AR[:, :, :, :], AR[:, :, :, :], ACT.Exp).then_inc(exps_ok, 1)
                    act.wait_ge(ra_ok, b + 2)
                    act.activation(ra[:, :, :], ra[:, :, :], ACT.Exp, scale=-1.0).then_inc(ea_ok, 1)
                if attn:
                    act.wait_ge(qt_ok, b)
                    act.activation(qS, qS, ACT.Exp).then_inc(qe_ok, 1)
                    act.wait_ge(kc_ok, b)
                    act.activation(ke, ke, ACT.Exp).then_inc(ke_ok, 1)
                if experts:
                    silu(b, 2)
                    act.wait_ge(twp_ok, b + 1)
                    copy(TW[:, :], Tb[:, 0, :]).then_inc(tw_ok, 1)
                    h_high(b, 0)
                    silu(b, 3)
                    h_high(b, 1)
                    silu(b, 4)
                    h_high(b, 2)
                    silu(b, 5)
                    h_high(b, 3)
                if rwkv:
                    act.preload_act_table_set("natural_log_exp_and_others")
                    act.wait_ge(qq_ok, b + 2)
                    act.activation(AR[:, 2, :, :], AR[:, 2, :, :], ACT.Ln).then_inc(ln_ok, 1)
                    act.wait_ge(arg_ok, b + 2)
                    act.activation(AR[:, 3, :, :], AR[:, 3, :, :], ACT.Exp, scale=-1.0).then_inc(sr_ok, 1)
                if proj:
                    act.wait_ge(kvr_ok, b + 3)
                    if rwkv:
                        act.wait_ge(nd_ok, b + 2)
                        act.wait_ge(v2_ok, b + 2)
                    copy(kS[:, :, :], Q[:, 0, :].rearrange("p (k t) -> p k t", k=KC))
                    copy(vS[:, :, :], Q[:, 1, :].rearrange("p (k t) -> p k t", k=KC)).then_inc(kv_ok, 1)
                    r = Q[:, 2, :].rearrange("p (k t) -> p k t", k=KC)
                    act.activation(ra[:, :, :], r, ACT.Abs)
                    act.activation(rn[:, :, :], r, ACT.Relu, scale=-1.0).then_inc(ra_ok, 1)
                if attn:
                    act.wait_ge(anTp_ok, b)
                    copy(anT, Tb[:, :, :]).then_inc(anT_ok, 1)
                if experts:
                    silu(b, 6)
                    h_high(b, 4)
                    silu(b, 7)
                    h_high(b, 5)
                    silu(b, 8)
                    h_high(b, 6)
                if attn:
                    act.wait_ge(x3Tp_ok, b)
                    copy(x3h[:, :, :], Tb[:, :, :]).then_inc(x3h_ok, 1)
                if experts:
                    silu(b, 9)
                    h_high(b, 7)
                if attn:
                    tanh_half(b, 0)
                    tanh_half(b, 1)
                    f_high(b, 0)
                if experts:
                    silu(b, 10)
                    h_high(b, 8)
                if attn:
                    f_high(b, 1)
                    tanh_half(b, 2)
                if rwkv:
                    act.wait_ge(x1Tp_ok, b + 2)
                    copy(x1T[:, :, :], Tb[:, :, :]).then_inc(x1T_ok, 1)
                if attn:
                    f_high(b, 2)
                    tanh_half(b, 3)
                if experts:
                    h_high(b, 9)
                if attn:
                    f_high(b, 3)
                    tanh_half(b, 4)
                if experts:
                    h_high(b, 10)
                if attn:
                    f_high(b, 4)
                    tanh_half(b, 5)
                    f_high(b, 5)

            act.wait_ge(in_vec, 32)
            act.activation(wdec[:, :], vec[:, :, TD_COL], ACT.Exp).then_inc(decay_e, 1)
            slots(act, slot)

        @block.vector
        def _(dve):
            def add_residual(i, psum, res, dst, value):
                dve.tensor_tensor(dst, psum, res, ALU.add).then_inc(r_ok[i], 1)
                dve.wait_ge(r_ok[i], value)
                for t in range(NT):
                    last = dve.bn_stats(st[:, i, t, :], dst[:, t, :])
                last.then_inc(st_ok[i], 1)
                dve.wait_ge(preset, 4)
                dve.wait_ge(st_ok[i], value)
                for t in range(NT):
                    last = dve.bn_aggr(mv[:, i, t, :], st[:, i, t, :])
                last.then_inc(mv_ok[i], 1)

            def normalise(i, src, dst, value):
                dve.wait_ge(rs_ok[i], value)
                dve.wait_ge(mv_ok[i], value)
                for t in range(NT):
                    last = dve.tensor_scalar(dst[:, t, :], src[:, t, :], mv[:, i, t, 0:1], rs[:, i, t:t + 1],
                                             ALU.subtract, ALU.mult)
                last.then_inc(x_ok[i], 1)

            def gate_times_up(b, c):
                dve.wait_ge(silu_ok, NCH * b + c + 1)
                h = hb[:, c % HDEPTH, :]
                dve.tensor_tensor(h, h, G[:, c % 2, 1, :], ALU.mult).then_inc(hu_ok, 1)

            def ternary_gate(b, f):
                dve.wait_ge(th_ok, NF * (b - 1) + f + 1)
                h = fb[:, f % SDEPTH, :]
                dve.scalar_tensor_tensor(h, h, 1.0, Q[:, f % 3, T:2 * T], ALU.add, ALU.mult).then_inc(fx_ok, 1)

            def split_weights(raw, hi, lo, hi_ok, lo_ok):
                dve.tensor_copy(hi, raw).then_inc(hi_ok, 1)
                if lo_ok is not None:
                    dve.wait_ge(hi_ok, 1)
                    dve.tensor_tensor(lo, raw, hi.bitcast(F32), ALU.subtract).then_inc(lo_ok, 1)

            def flat(w):
                return w[:, :, :].rearrange("p a b -> p (a b)")

            raw12 = stage[1][:, 0:2 * KC * HID].rearrange("p (j k n) -> p j k n", j=2, k=KC)
            raw3 = stage[0][:, 0:NF * C].rearrange("p (k c) -> p k c", k=NF)

            def quantise_sums():
                dve.wait_ge(in_w12, 32)
                for j in range(2):
                    dve.tensor_reduce(wsum[:, j:j + 1], raw12[:, j, :, :], mybir.AxisListType.XY, ALU.add,
                                      apply_absolute_value=True).then_inc(wsum_ok, 1)
                dve.wait_ge(in_w3, 32)
                dve.wait_ge(pads_ok, 1)
                dve.tensor_reduce(wsum[:, 2:3], raw3, mybir.AxisListType.XY, ALU.add,
                                  apply_absolute_value=True).then_inc(wsum_ok, 1)

            def quantise_thresholds():
                dve.wait_ge(gamma_ok, 1)
                for i, s in enumerate((0.5, -0.5)):
                    last = dve.tensor_scalar(thr[:, i, :], O[:, 0, 0:3], s / (C * HID), s * GAMMA_EPS, ALU.mult,
                                             ALU.add)
                last.then_inc(thr_ok, 1)
                dve.wait_ge(thr_ok, 1)

            def quantise(j):
                tmp = mix[:, :, :, :].rearrange("p a b c -> p (a b c)")[:, 0:KC * HID].rearrange(
                    "p (k n) -> p k n", k=KC)
                w = (w1q, w2q)[j]
                dve.tensor_scalar(tmp, raw12[:, j, :, :], thr[:, 1, j:j + 1], None, ALU.is_lt).then_inc(w12a_ok, 1)
                dve.wait_ge(w12a_ok, j + 1)
                last = dve.scalar_tensor_tensor(w[:, :, 0:HID], raw12[:, j, :, :], thr[:, 0, j:j + 1], tmp,
                                                ALU.is_gt, ALU.subtract)
                if j:
                    last.then_inc(w12q_ok, 1)
                    dve.wait_ge(w12q_ok, 1)

            def quantise_out():
                a = mix[:, :, :, :].rearrange("p a b c -> p (a b c)")[:, 0:NF * C].rearrange("p (k c) -> p k c", k=NF)
                r3 = stage[0][:, 0:NF * C].rearrange("p (k c) -> p k c", k=NF)
                dve.tensor_scalar(a, r3, thr[:, 1, 2:3], 0.5, ALU.is_lt, ALU.mult).then_inc(w3a_ok, 1)
                dve.tensor_scalar(r3, r3, thr[:, 0, 2:3], 0.5, ALU.is_gt, ALU.mult).then_inc(w3a_ok, 1)
                dve.wait_ge(w3a_ok, 2)
                dve.tensor_tensor(w3q[:, :, :], r3, a, ALU.subtract).then_inc(w3q_ok, 1)
                dve.wait_ge(w3q_ok, 1)

            def slot(b, experts, attn, rwkv, proj):
                first = isinstance(b, int) and b == 0
                if experts:
                    gate_times_up(b, 0)
                    gate_times_up(b, 1)
                    dve.wait_ge(router_ok, b + 1)
                    dve.tensor_copy(lg[:, :, :], O[:, 0, 0:NT * E].rearrange("p (t e) -> p t e", t=NT))\
                       .then_inc(lg_ok, 1)
                    dve.wait_ge(preset, 4)
                    dve.wait_ge(lg_ok, b + 1)
                    for t in range(NT):
                        last = dve.max(mx8[:, t, :], lg[:, t, :])
                    last.then_inc(mx_ok, 1)
                    dve.wait_ge(mx_ok, b + 1)
                    past(dve, top_ok, b)
                    dve.tensor_tensor(gap[:, :], mx8[:, :, 1], mx8[:, :, 0], ALU.subtract).then_inc(gap_ok, 1)
                    for t in range(NT):
                        last = dve.max_index(ix8[:, t, :], mx8[:, t, :], lg[:, t, :])
                    last.then_inc(ix_ok, 1)
                    dve.wait_ge(ix_ok, b + 1)
                    dve.tensor_copy(sel[:, :, :], ix8[:, :, 0:2]).then_inc(sel_ok, 1)
                if attn:
                    if isinstance(b, int) and b == 1:
                        dve.wait_ge(in_msk, 64)
                    dve.wait_ge(q_ok, b)
                    for k in range(KC):
                        last = dve.tensor_scalar(qS[:, k, :], Q[:, 0, k * T:(k + 1) * T], vec[:, k, QB_COL:QB_COL + 1],
                                                 0.0, ALU.add, ALU.min)
                    last.then_inc(qt_ok, 1)
                    dve.wait_ge(k_ok, b)
                    dve.tensor_tensor(kt, Q[:, 1, :].rearrange("p (t c) -> p t c", t=NT),
                                      bias[:, 0:1, :].broadcast_to([P, NT, C]), ALU.add).then_inc(kt_ok, 1)
                    dve.wait_ge(kt_ok, b)
                    dve.tensor_scalar(ke, kt, 0.0, None, ALU.min).then_inc(kc_ok, 1)
                if experts:
                    dve.wait_ge(tanh_ok, b + 1)
                    for i, s in enumerate((-0.5, 0.5)):
                        last = dve.tensor_scalar(top[:, i, :], gap[:, :], s, 0.5, ALU.mult, ALU.add)
                    last.then_inc(top_ok, 1)
                    dve.wait_ge(top_ok, b + 1)
                    dve.wait_ge(sel_ok, b + 1)
                    past(dve, twp_ok, b)
                    for t in range(NT):
                        dve.tensor_scalar(twt[:, t, :], expert_of, sel[:, t, 0:1], top[:, 0, t:t + 1],
                                          ALU.is_equal, ALU.mult)
                        last = dve.tensor_scalar(twb[:, t, :], expert_of, sel[:, t, 1:2], top[:, 1, t:t + 1],
                                                 ALU.is_equal, ALU.mult)
                    last.then_inc(twab_ok, 1)
                    dve.wait_ge(twab_ok, b + 1)
                    dve.tensor_tensor(twt[:, :, :], twt[:, :, :], twb[:, :, :], ALU.add).then_inc(twt_ok, 1)
                if attn:
                    dve.wait_ge(v_ok, b)
                    dve.tensor_tensor(vx[:, :, 0:3:2, :], Q[:, 2, :].rearrange("p (t j c) -> p t j c", t=NT, j=2),
                                      bias[:, 1:2, :].rearrange("p t (j c) -> p t j c", j=2).broadcast_to(
                                          [P, NT, 2, P]), ALU.add).then_inc(vx_ok, 1)
                    dve.wait_ge(qe_ok, b)
                    for k in range(KC):
                        last = dve.scalar_tensor_tensor(qS[:, k, :], Q[:, 0, k * T:(k + 1) * T], qb1[:, k:k + 1],
                                                        qS[:, k, :], ALU.add, ALU.max)
                    last.then_inc(qp_ok, 1)
                    dve.wait_ge(ke_ok, b)
                    dve.scalar_tensor_tensor(ke, kt, 1.0, ke, ALU.add, ALU.max).then_inc(kp_ok, 1)
                if experts:
                    gate_times_up(b, 2)
                    if first:
                        quantise_sums()
                if rwkv:
                    dve.wait_ge(exps_ok, b + 2)
                    for k in range(KC):
                        dve.tensor_tensor_scan(ND[:, 1, k, 1:], AR[:, 0, k, :], AR[:, 1, k, :], 0.0, ALU.mult,
                                               ALU.add)
                if experts:
                    gate_times_up(b, 3)
                if rwkv:
                    dve.wait_ge(v2_ok, b + 2)
                    for k in range(KC):
                        last = dve.tensor_tensor_scan(ND[:, 0, k, 1:], AR[:, 0, k, :], V2[:, 0, k, :], 0.0,
                                                      ALU.mult, ALU.add)
                    last.then_inc(nd_ok, 1)
                if attn:
                    dve.wait_ge(kvp_ok, b)
                    dve.tensor_tensor(kvm, Q[:, 0, :].rearrange("p (k c) -> p k c", k=KC),
                                      msk[:, :].rearrange("p (k c) -> p k c", k=1).broadcast_to([P, KC, C]),
                                      ALU.mult).then_inc(kvm_ok, 1)
                if proj:
                    dve.wait_ge(dx_ok, b + 3)
                    if not (isinstance(b, int) and b == -2):
                        dve.wait_ge(kvr_ok, b + 2)
                    for j in range(3):
                        for k in range(KC):
                            last = dve.scalar_tensor_tensor(mix[:, j, k, :], dx[:, k, :],
                                                            vec[:, k, MIX + j:MIX + j + 1], xs[:, k, 0:T],
                                                            ALU.mult, ALU.add)
                    last.then_inc(mix_ok, 1)
                if experts:
                    gate_times_up(b, 4)
                if rwkv:
                    dve.wait_ge(nd_ok, b + 2)
                    for i in range(2):
                        last = dve.tensor_tensor(AR[:, i, :, :], ND[:, i, :, 0:T], AR[:, 2, :, :], ALU.mult)
                    last.then_inc(t1_ok, 1)
                    dve.wait_ge(t1_ok, b + 2)
                    dve.tensor_tensor(V2[:, 0, :, :], AR[:, 0, :, :], V2[:, 1, :, :], ALU.add)
                    dve.tensor_tensor(AR[:, 1, :, :], AR[:, 1, :, :], AR[:, 3, :, :], ALU.add).then_inc(nd2_ok, 1)
                    dve.wait_ge(nd2_ok, b + 2)
                    dve.wait_ge(ea_ok, b + 2)
                    dve.scalar_tensor_tensor(AR[:, 2, :, :], ra[:, :, :], 1.0, AR[:, 1, :, :], ALU.add,
                                             ALU.mult).then_inc(qq_ok, 1)
                if experts:
                    gate_times_up(b, 5)
                if attn:
                    dve.wait_ge(at_ok, b)
                    dve.tensor_scalar(zr[:, :, :], Q[:, 1:3, P:3 * P:HEAD], Z_EPS, None, ALU.add).then_inc(ze_ok, 1)
                    dve.wait_ge(ze_ok, b)
                    dve.reciprocal(zr[:, :, :], zr[:, :, :]).then_inc(zr_ok, 1)
                    dve.wait_ge(zr_ok, b)
                    for t in range(NT):
                        for k in range(KC):
                            src = Q[:, 1 + t, 3 * P * k:3 * P * k + P].rearrange("p (h e) -> p h e", e=HEAD)
                            dst = an[:, t, k * P:(k + 1) * P].rearrange("p (h e) -> p h e", e=HEAD)
                            hs = slice(k * NH // KC, (k + 1) * NH // KC)
                            last = dve.tensor_tensor(dst, src, zr[:, t, hs].unsqueeze(2).broadcast_to(
                                [P, NH // KC, HEAD]), ALU.mult)
                    last.then_inc(an_ok, 1)
                if rwkv:
                    dve.wait_ge(ln_ok, b + 2)
                    dve.tensor_tensor(AR[:, 3, :, :], rn[:, :, :], AR[:, 2, :, :], ALU.add).then_inc(arg_ok, 1)
                if experts:
                    gate_times_up(b, 6)
                if rwkv:
                    dve.wait_ge(sr_ok, b + 2)
                    past(dve, o1_ok, b + 1)
                    dve.tensor_tensor(y[:, :, :], V2[:, 0, :, :], AR[:, 3, :, :], ALU.mult).then_inc(y_ok, 1)
                if isinstance(b, int) and b == -2:
                    dve.wait_ge(in_gate, 16)
                    split_weights(stage[0], flat(gate_hi), None, gate_hi_ok, None)
                    dve.wait_ge(in_up, 16)
                    split_weights(stage[1], flat(up_hi), flat(up_lo), up_hi_ok, up_lo_ok)
                if isinstance(b, int) and b == -1:
                    dve.wait_ge(in_down, 16)
                    split_weights(stage[0], flat(down_hi), flat(down_lo), down_hi_ok, down_lo_ok)
                    dve.wait_ge(down_lo_ok, 1)
                    dve.memset(stage[0][HID % P:, (NF - 1) * C:NF * C], 0.0).then_inc(pads_ok, 1)
                if attn:
                    dve.wait_ge(o3_ok, b)
                    dve.wait_ge(x2b_ok, b)
                    add_residual(2, O[:, :, :], x2, x3, b)
                if first:
                    quantise_thresholds()
                    quantise(0)
                if experts:
                    gate_times_up(b, 7)
                if attn:
                    normalise(2, x3, x3, b)
                if rwkv:
                    dve.wait_ge(o1_ok, b + 2)
                    dve.wait_ge(in_x, 16 * (b + 2))
                    add_residual(0, O[:, :, :], x1[:, :, :], x1[:, :, :], b + 2)
                if experts:
                    gate_times_up(b, 8)
                if proj:
                    dve.wait_ge(kv_ok, b + 3)
                    for k in range(KC):
                        last = dve.tensor_tensor_scan(M[:, k, 1:], wdec[:, k:k + 1].broadcast_to([P, T]), kS[:, k, :],
                                                      LOW, ALU.add, ALU.max)
                    last.then_inc(M_ok, 1)
                if rwkv:
                    normalise(0, x1, x1, b + 2)
                if first:
                    quantise(1)
                    quantise_out()
                if experts:
                    gate_times_up(b, 9)
                if attn:
                    dve.wait_ge(x3h_ok, b)
                    dve.tensor_tensor(x3l[:, :, :], Tb[:, :, :], x3h[:, :, :].bitcast(F32), ALU.subtract)\
                       .then_inc(x3l_ok, 1)
                    ternary_gate(b, 0)
                    ternary_gate(b, 1)
                if experts:
                    gate_times_up(b, 10)
                if attn:
                    ternary_gate(b, 2)
                if rwkv:
                    dve.wait_ge(x1T_ok, b + 2)
                    if experts:
                        dve.wait_ge(gu_ok, NCH * (b + 1))
                    dve.tensor_copy(x1h[:, :, :], x1T[:, :, :]).then_inc(x1h_ok, 1)
                    dve.wait_ge(x1h_ok, b + 2)
                    dve.tensor_tensor(x1l[:, :, :], x1T[:, :, :], x1h[:, :, :].bitcast(F32), ALU.subtract)\
                       .then_inc(x1l_ok, 1)
                if attn:
                    ternary_gate(b, 3)
                if proj:
                    dve.wait_ge(M_ok, b + 3)
                    for k in range(KC):
                        dve.scalar_tensor_tensor(AR[:, 2, k, :], kS[:, k, :], vec[:, k, U_COL:U_COL + 1],
                                                 M[:, k, 0:T], ALU.add, ALU.subtract)
                        last = dve.scalar_tensor_tensor(AR[:, 0, k, :], M[:, k, 0:T], wdec[:, k:k + 1],
                                                        M[:, k, 1:], ALU.add, ALU.subtract)
                    last.then_inc(lag_ok, 1)
                    dve.tensor_tensor(AR[:, 1, :, :], kS[:, :, :], M[:, :, 1:], ALU.subtract)
                    dve.wait_ge(lag_ok, b + 3)
                    dve.tensor_scalar(AR[:, 3, :, :], AR[:, 2, :, :], 0.0, None, ALU.min)
                    dve.tensor_scalar(AR[:, 2, :, :], AR[:, 2, :, :], 0.0, -1.0, ALU.max, ALU.mult)\
                       .then_inc(ar_ok, 1)
                if attn:
                    ternary_gate(b, 4)
                    ternary_gate(b, 5)
                if experts:
                    dve.wait_ge(down_ok, NCH * (b + 1))
                    dve.wait_ge(x1k_ok, b + 1)
                    if attn:
                        dve.wait_ge(r_ok[2], b)
                    add_residual(1, D[:, :, :], x1k[:, :, :], x2, b + 1)
                if attn:
                    dve.wait_ge(w3_ok, NF * b)
                    past(dve, out_x4, 16 * (b - 1))
                    add_residual(3, O[:, :, :], x3, x4[:, :, :], b)
                if experts:
                    if first:
                        dve.memset(vx[:, :, 1, :], 1.0)
                    normalise(1, x2, x2, b + 1)
                if attn:
                    normalise(3, x4, x4, b)

            dve.memset(xs[:, :, 0:1], 0.0).then_inc(preset, 1)
            dve.memset(M[:, :, 0:1], LOW)
            dve.memset(ND[:, :, :, 0:1], 0.0).then_inc(preset, 1)
            dve.memset(ones[:, :], 1.0).then_inc(preset, 1)
            dve.memset(w1q[:, :, HID:].bitcast(F32), 0.0)
            dve.memset(w2q[:, :, HID:].bitcast(F32), 0.0)
            dve.memset(eps[:, :], LN_EPS)
            dve.memset(neghalf[:, :], -0.5).then_inc(preset, 1)
            dve.wait_ge(preset, 4)
            dve.wait_ge(in_vec, 32)
            dve.tensor_scalar(qb1[:, :], vec[:, :, QB_COL], 1.0, None, ALU.add)
            dve.wait_ge(decay_e, 1)
            dve.tensor_scalar(wdec[:, :], wdec[:, :], -1.0, None, ALU.mult).then_inc(wdec_ok, 1)
            dve.wait_ge(wdec_ok, 1)
            slots(dve, slot)

        @block.gpsimd
        def _(pool):
            def deviation(i, value):
                pool.wait_ge(mv_ok[i], value)
                pool.tensor_tensor(ve[:, i, :], mv[:, i, :, 1], eps[:, :], ALU.add).then_inc(ve_ok[i], 1)
                pool.wait_ge(ve_ok[i], value)
                pool.tensor_tensor(rs[:, i, :], ve[:, i, :], neghalf[:, :], ALU.pow).then_inc(rs_ok[i], 1)

            def weigh(b, c):
                pool.wait_ge(hu_ok, NCH * b + c + 1)
                if c == 0:
                    pool.wait_ge(tw_ok, b + 1)
                h = hb[:, c % HDEPTH, :]
                pool.tensor_tensor(h, h, TW[:, :], ALU.mult).then_inc(h_ok, 1)

            def h_low(b, c):
                pool.wait_ge(hh_ok, NCH * b + c + 1)
                pool.tensor_tensor(hl[:, c % SDEPTH, :], hb[:, c % HDEPTH, :], hh[:, c % SDEPTH, :].bitcast(F32),
                                   ALU.subtract).then_inc(hl_ok, 1)

            def f_low(b, f):
                pool.wait_ge(fh_ok, NF * (b - 1) + f + 1)
                pool.tensor_tensor(fl[:, f % SDEPTH, :], fb[:, f % SDEPTH, :], fh[:, f % SDEPTH, :].bitcast(F32),
                                   ALU.subtract).then_inc(fl_ok, 1)

            def slot(b, experts, attn, rwkv, proj):
                if rwkv:
                    pool.wait_ge(exps_ok, b + 2)
                    past(pool, y_ok, b + 1)
                    for i, e in ((0, 1), (1, 3)):
                        last = pool.tensor_tensor(V2[:, i, :, :], AR[:, e, :, :], vS[:, :, :], ALU.mult)
                    last.then_inc(v2_ok, 1)
                if proj:
                    pool.wait_ge(in_xT, 16 * (b + 3))
                    if not (isinstance(b, int) and b == -2):
                        pool.wait_ge(mix_ok, b + 2)
                    pool.tensor_tensor(dx[:, :, :], xs[:, :, 1:], xs[:, :, 0:T], ALU.subtract).then_inc(dx_ok, 1)
                if isinstance(b, int) and b == -2:
                    pool.wait_ge(gate_hi_ok, 1)
                    pool.tensor_tensor(gate_lo[:, :, :].rearrange("p a b -> p (a b)"), stage[0],
                                       gate_hi[:, :, :].rearrange("p a b -> p (a b)").bitcast(F32),
                                       ALU.subtract).then_inc(gate_lo_ok, 1)
                if attn:
                    pool.wait_ge(x2Tp_ok, b)
                    pool.tensor_tensor(x2, x2, bias[:, 2:3, :].broadcast_to([P, NT, C]), ALU.add)\
                        .then_inc(x2b_ok, 1)
                if experts:
                    weigh(b, 0)
                    weigh(b, 1)
                    h_low(b, 0)
                    weigh(b, 2)
                    h_low(b, 1)
                    weigh(b, 3)
                    h_low(b, 2)
                    weigh(b, 4)
                    h_low(b, 3)
                    weigh(b, 5)
                    h_low(b, 4)
                    weigh(b, 6)
                if attn:
                    deviation(2, b)
                if experts:
                    h_low(b, 5)
                    weigh(b, 7)
                if rwkv:
                    deviation(0, b + 2)
                if experts:
                    h_low(b, 6)
                    weigh(b, 8)
                    h_low(b, 7)
                    weigh(b, 9)
                if attn:
                    f_low(b, 0)
                if experts:
                    h_low(b, 8)
                    weigh(b, 10)
                if attn:
                    f_low(b, 1)
                    f_low(b, 2)
                if experts:
                    h_low(b, 9)
                if attn:
                    f_low(b, 3)
                if experts:
                    h_low(b, 10)
                if attn:
                    f_low(b, 4)
                    f_low(b, 5)
                if experts:
                    deviation(1, b + 1)
                if attn:
                    deviation(3, b)

            pool.wait_ge(preset, 4)
            slots(pool, slot)


def kernel(**inputs):
    import numpy as np
    import concourse.bacc as bacc
    from concourse.bass_utils import run_bass_kernel_spmd

    a = {k: np.asarray(v) for k, v in inputs.items()}
    f32 = np.float32

    def turned(w):
        return np.ascontiguousarray(w.T)

    def by_channel(w):
        t = w.reshape(E, NCH, FE, KC, P).transpose(4, 3, 1, 0, 2)
        return np.ascontiguousarray(t).reshape(P, KC * NCH * P)

    vec = np.stack([a["L0_attn_time_mix_k"], a["L0_attn_time_mix_v"], a["L0_attn_time_mix_r"],
                    a["L0_attn_time_first"], a["L0_attn_time_decay"], a["L1_attn_q_b"]], axis=-1)
    consts = np.zeros((P, 2, P), f32)
    consts[:, 0, :] = np.eye(P, dtype=f32)
    consts[:, 1, :] = np.repeat(np.arange(E, dtype=f32), FE)
    heads = np.arange(P) // HEAD
    mask = np.tile((heads[:, None] == heads[None, :]).astype(f32), (1, KC))
    arrays = {
        "xT": np.ascontiguousarray(a["L0_attn_x"].reshape(B * T, C).T),
        "x": a["L0_attn_x"],
        "vecs": np.ascontiguousarray(vec.reshape(KC, P, NVEC).transpose(1, 0, 2)),
        "rows": np.stack([a["L1_attn_k_b"], a["L1_attn_v_b"], a["L1_attn_o_b"]]),
        "consts": consts,
        "mask": mask,
        "Wk": turned(a["L0_attn_Wk"]), "Wv": turned(a["L0_attn_Wv"]), "Wr": turned(a["L0_attn_Wr"]),
        "Wo": turned(a["L0_attn_Wo"]),
        "gate_w": turned(a["L0_ffn_gate_w"]),
        "w_gate": by_channel(a["L0_ffn_gate_proj"]),
        "w_up": by_channel(a["L0_ffn_up_proj"]),
        "w_down": np.ascontiguousarray(
            a["L0_ffn_down_proj"].reshape(E, C, NCH, FE).transpose(0, 3, 2, 1)).reshape(P, NCH * C),
        "Wq3": turned(a["L1_attn_q_w"]), "Wk3": turned(a["L1_attn_k_w"]), "Wv3": turned(a["L1_attn_v_w"]),
        "Wo3": turned(a["L1_attn_o_w"]),
        "W1": turned(a["L1_ffn_w1"]), "W2": turned(a["L1_ffn_w2"]), "W3": turned(a["L1_ffn_w3"]),
    }
    nc = bacc.Bacc("TRN2", target_bir_lowering=False, num_devices=1)
    args = [nc.dram_tensor(f"in_{k}", v.shape, mybir.dt.from_np(v.dtype), kind="ExternalInput").ap()
            for k, v in arrays.items()]
    out = nc.dram_tensor("out_0", (B, T, C), F32, kind="ExternalOutput").ap()
    build(nc, *args, out)
    r = run_bass_kernel_spmd(nc, [{f"in_{k}": v for k, v in arrays.items()}], core_ids=[0])
    return r.results[0]["out_0"]
```

```python
from contextlib import ExitStack

import concourse.bass as bass
from concourse import mybir

P = 128
F32 = mybir.dt.float32
F32R = mybir.dt.float32r
U32 = mybir.dt.uint32
ALU = mybir.AluOpType
ACT = mybir.ActivationFunctionType
AX_X = mybir.AxisListType.X

B, T, C = 8, 256, 256
KC = C // P
NT = T // P
E, F = 8, 176
FE = P // E
NCH = F // FE
HID = 704
NF = -(-HID // P)
HEAD = 16
NH = C // HEAD
HK = NH // KC
KVW = P + HK
VW = C + HK
LN_EPS = 1e-5
Z_EPS = 1e-6
GAMMA_EPS = 1e-8
LOW = -1e38
MIX, U_COL, TD_COL, QB_COL = 0, 3, 4, 5
NVEC = 6
WARM = (10, 9, 9, 10, 5, 5, 4, 5, 12, 5)
HDEPTH = 4
SDEPTH = 3


def rotating(c, depth, per_batch=NCH):
    if c >= depth:
        return depth
    back = [x for x in range(per_batch) if x % depth == c % depth][-1]
    return per_batch - back + c


def past(eng, sem, value):
    if isinstance(value, int) and value < 1:
        return
    eng.wait_ge(sem, value)


def build(nc, xT, x, vecs, rows, consts, mask, Wk, Wv, Wr, Wo, gate_w, w_gate, w_up, w_down,
          Wq3, Wk3, Wv3, Wo3, W1, W2, W3, out):
    ctx = ExitStack()
    with ctx:
        def sb(name, shape, dt=F32):
            return ctx.enter_context(nc.sbuf_tensor(name, shape, dt))

        def pb(name, shape):
            return ctx.enter_context(nc.psum_tensor(name, shape, F32))

        def sem(name):
            return ctx.enter_context(nc.semaphore(name))

        wkvr = sb("wkvr", [P, 3, KC, C])
        wo1 = sb("wo1", [P, KC, C])
        att_hi = sb("att_hi", [P, 4, KC, C], F32R)
        att_lo = sb("att_lo", [P, 4, KC, C], F32R)
        gw = sb("gw", [P, KC, E])
        gate_hi = sb("gate_hi", [P, KC, NCH * P], F32R)
        gate_lo = sb("gate_lo", [P, KC, NCH * P], F32R)
        up_hi = sb("up_hi", [P, KC, NCH * P], F32R)
        up_lo = sb("up_lo", [P, KC, NCH * P], F32R)
        down_hi = sb("down_hi", [P, NCH, C], F32R)
        down_lo = sb("down_lo", [P, NCH, C], F32R)
        w1q = sb("w1q", [P, KC, NF * P], F32R)
        w2q = sb("w2q", [P, KC, NF * P], F32R)
        w3q = sb("w3q", [P, NF, C], F32R)
        vec = sb("vec", [P, KC, NVEC])
        wdec = sb("wdec", [P, KC])
        qb1 = sb("qb1", [P, KC])
        bias = sb("bias", [P, 3, C])
        cst = sb("cst", [P, 2, P])
        msk = sb("msk", [P, KC, KVW])
        ones = sb("ones", [P, P])
        neghalf = sb("neghalf", [P, NT])
        eps = sb("eps", [P, NT])
        ident = cst[:, 0, :]
        expert_of = cst[:, 1, :]

        xs = sb("xs", [P, KC, 1 + T])
        dx = sb("dx", [P, KC, T])
        mix = sb("mix", [P, 3, KC, T])
        vS = sb("vS", [P, KC, T])
        ra = sb("ra", [P, KC, T])
        rn = sb("rn", [P, KC, T])
        M = sb("M", [P, KC, 1 + T])
        AR = sb("AR", [P, 4, KC, T])
        V2 = sb("V2", [P, 2, KC, T])
        ND = sb("ND", [P, 2, KC, 1 + T])
        kS = ND[:, 0, :, 1:]
        y = V2[:, 1, :, :]
        x1 = sb("x1", [P, NT, C])
        x1k = sb("x1k", [P, NT, C])
        x1T = sb("x1T", [P, KC, T])
        x1h = sb("x1h", [P, KC, T], F32R)
        x1l = sb("x1l", [P, KC, T], F32R)
        hb = sb("hb", [P, HDEPTH, T])
        hh = sb("hh", [P, SDEPTH, T], F32R)
        hl = sb("hl", [P, SDEPTH, T], F32R)
        TW = sb("TW", [P, T])
        twt = sb("twt", [P, NT, P])
        twb = sb("twb", [P, NT, P])
        lg = sb("lg", [P, NT, E])
        mx8 = sb("mx8", [P, NT, 8])
        ix8 = sb("ix8", [P, NT, 8], U32)
        sel = sb("sel", [P, NT, 2])
        gap = sb("gap", [P, NT])
        top = sb("top", [P, 2, NT])
        STAGE = KC * NCH * P
        arena = sb("arena", [P, 2 * STAGE])
        stage = [arena[:, i * STAGE:(i + 1) * STAGE] for i in range(2)]
        raw_att = stage[1][:, 0:4 * KC * C].rearrange("p (j k n) -> p j k n", j=4, k=KC)
        raw12 = stage[1][:, 0:2 * KC * HID].rearrange("p (j k n) -> p j k n", j=2, k=KC)
        raw3 = stage[0][:, 0:NF * C].rearrange("p (k c) -> p k c", k=NF)
        U = KC * T
        x2 = arena[:, 0:U].rearrange("p (t c) -> p t c", t=NT)
        x3 = arena[:, U:2 * U].rearrange("p (t c) -> p t c", t=NT)
        qS = arena[:, 2 * U:3 * U].rearrange("p (k t) -> p k t", k=KC)
        kt = arena[:, 3 * U:4 * U].rearrange("p (t c) -> p t c", t=NT)
        ke = arena[:, 4 * U:5 * U].rearrange("p (t c) -> p t c", t=NT)
        an = arena[:, 5 * U:6 * U].rearrange("p (t c) -> p t c", t=NT)
        x4 = arena[:, 6 * U:7 * U].rearrange("p (t c) -> p t c", t=NT)
        VX, KV, FB = 7 * U, 7 * U + NT * VW, 7 * U + NT * VW + KC * KVW
        vx = arena[:, VX:KV].rearrange("p (t c) -> p t c", t=NT)
        kvm = arena[:, KV:FB].rearrange("p (k c) -> p k c", k=KC)
        fb = arena[:, FB:FB + SDEPTH * T].rearrange("p (s t) -> p s t", s=SDEPTH)
        assert FB + SDEPTH * T <= 2 * STAGE
        zr = sb("zr", [P, NT, NH])
        xh = sb("xh", [P, KC, T], F32R)
        xl = sb("xl", [P, KC, T], F32R)
        fh = sb("fh", [P, SDEPTH, T], F32R)
        fl = sb("fl", [P, SDEPTH, T], F32R)
        wsum = sb("wsum", [P, 3])
        thr = sb("thr", [P, 2, 3])
        st = sb("st", [P, 4, NT, 6])
        mv = sb("mv", [P, 4, NT, 2])
        ve = sb("ve", [P, 4, NT])
        rs = sb("rs", [P, 4, NT])

        G = pb("G", [P, 2, 2, T])
        D = pb("D", [P, NT, C])
        Tb = pb("Tb", [P, KC, T])
        Q = pb("Q", [P, 3, 2 * T])
        O = pb("O", [P, NT, C])

        in_vec, in_cst, in_msk, in_wo1, in_gw, in_xT, in_x = map(
            sem, ("in_vec", "in_cst", "in_msk", "in_wo1", "in_gw", "in_xT", "in_x"))
        in_kvr = [sem(f"in_w{j}") for j in "kvr"]
        in_gate, in_up, in_down, in_w12, in_w3 = map(sem, ("in_gate", "in_up", "in_down", "in_w12", "in_w3"))
        in_att, out_x4, att_hi_ok, att_lo_ok = map(sem, ("in_att", "out_x4", "att_hi_ok", "att_lo_ok"))
        preset, decay_e, wdec_ok, pads_ok = map(sem, ("preset", "decay_e", "wdec_ok", "pads_ok"))
        gate_hi_ok, gate_lo_ok = sem("gate_hi_ok"), sem("gate_lo_ok")
        up_hi_ok, up_lo_ok = sem("up_hi_ok"), sem("up_lo_ok")
        down_hi_ok, down_lo_ok = sem("down_hi_ok"), sem("down_lo_ok")
        wsum_ok, gamma_ok, thr_ok, w12a_ok, w12q_ok, w3a_ok, w3q_ok = map(
            sem, ("wsum_ok", "gamma_ok", "thr_ok", "w12a_ok", "w12q_ok", "w3a_ok", "w3q_ok"))
        dx_ok, mixk_ok, mix_ok, kp1_ok, kvr_ok, kS_ok, vS_ok, ra_ok, M_ok = map(
            sem, ("dx_ok", "mixk_ok", "mix_ok", "kp1_ok", "kvr_ok", "kS_ok", "vS_ok", "ra_ok", "M_ok"))
        lag_ok, ar_ok, exps_ok, ea_ok, nd_ok, t1_ok = map(
            sem, ("lag_ok", "ar_ok", "exps_ok", "ea_ok", "nd_ok", "t1_ok"))
        nd2_ok, qq_ok, ln_ok, arg_ok, sr_ok, y_ok, o1_ok = map(
            sem, ("nd2_ok", "qq_ok", "ln_ok", "arg_ok", "sr_ok", "y_ok", "o1_ok"))
        v2_ok = [sem("v2_next_ok"), sem("v2_out_ok")]
        r_ok = [sem(f"r{i}_ok") for i in range(4)]
        st_ok = [sem(f"st{i}_ok") for i in range(4)]
        mv_ok = [sem(f"mv{i}_ok") for i in range(4)]
        ve_ok = [sem(f"ve{i}_ok") for i in range(4)]
        rs_ok = [sem(f"rs{i}_ok") for i in range(4)]
        x_ok = [sem(f"x{i}_ok") for i in range(4)]
        x1k_ok, x1Tp_ok, x1T_ok, x1h_ok, x1l_ok = map(sem, ("x1k_ok", "x1Tp_ok", "x1T_ok", "x1h_ok", "x1l_ok"))
        router_ok, lg_ok, mx_ok, ix_ok, gap_ok, tanh_ok, sel_ok, top_ok, twab_ok, twt_ok, twp_ok, tw_ok = map(
            sem, ("router_ok", "lg_ok", "mx_ok", "ix_ok", "gap_ok", "tanh_ok", "sel_ok", "top_ok", "twab_ok",
                  "twt_ok", "twp_ok", "tw_ok"))
        gu_ok, silu_ok, hu_ok, h_ok, hh_ok, hl_ok, down_ok = map(
            sem, ("gu_ok", "silu_ok", "hu_ok", "h_ok", "hh_ok", "hl_ok", "down_ok"))
        x2Tp_ok, x2h_ok, x2l_ok, x2b_ok, q_ok, k_ok, v_ok = map(
            sem, ("x2Tp_ok", "x2h_ok", "x2l_ok", "x2b_ok", "q_ok", "k_ok", "v_ok"))
        qt_ok, qe_ok, qp_ok, kt_ok, kc_ok, ke_ok, kp_ok, vx_ok = map(
            sem, ("qt_ok", "qe_ok", "qp_ok", "kt_ok", "kc_ok", "ke_ok", "kp_ok", "vx_ok"))
        kvp_ok, kvm_ok, at_ok, ze_ok, zr_ok, an_ok, anTp_ok, anh_ok, anl_ok, o3_ok = map(
            sem, ("kvp_ok", "kvm_ok", "at_ok", "ze_ok", "zr_ok", "an_ok", "anTp_ok", "anh_ok", "anl_ok", "o3_ok"))
        x3Tp_ok, x3h_ok, x3l_ok, f12_ok, th_ok, fx_ok, fh_ok, fl_ok, w3_ok = map(
            sem, ("x3Tp_ok", "x3h_ok", "x3l_ok", "f12_ok", "th_ok", "fx_ok", "fh_ok", "fl_ok", "w3_ok"))

        xT_v = xT.rearrange("(k p) (n t) -> n p k t", p=P, t=T)
        x_v = x.rearrange("n (t p) c -> n p t c", p=P)
        out_v = out.rearrange("n (t p) c -> n p t c", p=P)

        def batch_of(view, n):
            return view[bass.ds(n, 1)].rearrange("n p a b -> (n p) a b") if not isinstance(n, int) else view[n]

        def flat(w):
            return w[:, :, :].rearrange("p a b -> p (a b)")

        def chunked(w):
            return w.rearrange("(k p) d -> p k d", p=P)

        LOOP = (2, B - 2)

        def slots(eng, slot):
            for b in range(-2, LOOP[0]):
                slot(b, 0 <= b, 1 <= b, -1 <= b, True)
            with eng.Fori(*LOOP) as b:
                slot(b, True, True, True, True)
            for b in range(LOOP[1], B + 1):
                slot(b, b < B, True, b + 1 < B, b + 2 < B)

        def difference(eng):
            eng.tensor_tensor(dx[:, :, :], xs[:, :, 1:], xs[:, :, 0:T], ALU.subtract).then_inc(dx_ok, 1)

        def value_product(eng, i):
            eng.tensor_tensor(V2[:, i, :, :], AR[:, 1 + 2 * i, :, :], vS[:, :, :], ALU.mult).then_inc(v2_ok[i], 1)

        block = ctx.enter_context(nc.Block())

        @block.sync
        def _(sp):
            sp.dma_start(xs[:, :, 1:], xT_v[0]).then_inc(in_xT, 16)
            sp.dma_start(vec[:, :, :], vecs).then_inc(in_vec, 16)
            for j, w in enumerate((Wk, Wv, Wr)):
                sp.dma_start(wkvr[:, j, :, :], chunked(w)).then_inc(in_kvr[j], 16)
            sp.dma_start(cst[:, :, :], consts).then_inc(in_cst, 16)
            sp.dma_start(stage[0], w_gate).then_inc(in_gate, 16)

            def slot(b, experts, attn, rwkv, proj):
                if isinstance(b, int) and b == -2:
                    sp.wait_ge(mix_ok, 1)
                    sp.dma_start(xs[:, :, 1:], xT_v[1]).then_inc(in_xT, 16)
                    sp.dma_start(stage[1], w_up).then_inc(in_up, 16)
                    sp.dma_start(wo1[:, :, :], chunked(Wo)).then_inc(in_wo1, 16)
                    return
                if proj and not (isinstance(b, int) and b == -1):
                    sp.wait_ge(mix_ok, b + 2)
                    sp.dma_start(xs[:, :, 1:], batch_of(xT_v, b + 2)).then_inc(in_xT, 16)
                if rwkv:
                    if experts:
                        sp.wait_ge(x1k_ok, b + 1)
                        sp.wait_ge(x1Tp_ok, b + 1)
                    sp.dma_start(x1[:, :, :], batch_of(x_v, b + 1)).then_inc(in_x, 16)
                if isinstance(b, int) and b == -1:
                    sp.dma_start(gw[:, :, :], chunked(gate_w)).then_inc(in_gw, 16)
                    sp.wait_ge(gate_hi_ok, 1)
                    sp.wait_ge(gate_lo_ok, 1)
                    sp.dma_start(stage[0], w_down).then_inc(in_down, 16)
                    sp.dma_start(msk[:, :, :], mask).then_inc(in_msk, 16)
                    for i in range(3):
                        sp.dma_start(bias[:, i, :], rows[i:i + 1, :].broadcast_to([P, C])).then_inc(in_msk, 16)
                    sp.wait_ge(up_hi_ok, 1)
                    sp.wait_ge(up_lo_ok, 1)
                    for j, w in enumerate((Wq3, Wk3, Wv3, Wo3)):
                        sp.dma_start(raw_att[:, j, :, :], chunked(w)).then_inc(in_att, 16)
                if isinstance(b, int) and b == 0:
                    sp.wait_ge(down_hi_ok, 1)
                    sp.wait_ge(down_lo_ok, 1)
                    full = HID // P
                    sp.dma_start(raw3[:, 0:full, :], chunked(W3[0:full * P, :])).then_inc(in_w3, 16)
                    sp.dma_start(raw3[0:HID - full * P, full, :], W3[full * P:HID, :]).then_inc(in_w3, 16)
                    sp.wait_ge(att_hi_ok, 1)
                    sp.wait_ge(att_lo_ok, 1)
                    for i, w in enumerate((W1, W2)):
                        sp.dma_start(raw12[:, i, :, :], chunked(w)).then_inc(in_w12, 16)
                if attn:
                    sp.wait_ge(x_ok[3], b)
                    sp.dma_start(batch_of(out_v, b - 1), x4[:, :, :]).then_inc(out_x4, 16)

            slots(sp, slot)
            sp.wait_ge(out_x4, 16 * B)

        @block.tensor
        def _(pe):
            def f32_product(dst, pairs):
                for i, (l, r) in enumerate(pairs):
                    last = pe.matmul(dst, l, r, start=i == 0, stop=i == len(pairs) - 1)
                return last

            def transposes(src, dst):
                for t in range(NT):
                    for k in range(KC):
                        last = pe.transpose(dst[:, k, t * P:(t + 1) * P], src[:, t, k * P:(k + 1) * P], ident)
                return last

            def split_product(dst, pairs):
                return f32_product(dst, [p for (lh, ll), (rh, rl) in pairs for p in ((lh, rh), (lh, rl), (ll, rh))])

            def keep_clock(n):
                for _ in range(n):
                    pe.matmul(G[:, 0, 0, 0:P], ones[:, :], ones[:, :], start=True, stop=True)

            def gate_up(b, c):
                if c == 0:
                    pe.wait_ge(x1h_ok, b + 1)
                    pe.wait_ge(x1l_ok, b + 1)
                past(pe, hu_ok, NCH * b + c - 1)
                cols = slice(c * P, (c + 1) * P)
                for i, (wh, wl) in enumerate(((gate_hi, gate_lo), (up_hi, up_lo))):
                    last = f32_product(G[:, c % 2, i, :], [
                        (w[:, k, cols], xx[:, k, :]) for k in range(KC)
                        for w, xx in ((wh, x1h), (wh, x1l), (wl, x1h))])
                last.then_inc(gu_ok, 1)

            def down(b, c):
                pe.wait_ge(hl_ok, NCH * b + c + 1)
                if c == 0:
                    if isinstance(b, int) and b == 0:
                        pe.wait_ge(down_hi_ok, 1)
                        pe.wait_ge(down_lo_ok, 1)
                    past(pe, r_ok[1], b)
                s = c % SDEPTH
                for t in range(NT):
                    tok = slice(t * P, (t + 1) * P)
                    for i, (l, r) in enumerate(((hh, down_hi), (hh, down_lo), (hl, down_hi))):
                        last = pe.matmul(D[:, t, :], l[:, s, tok], r[:, c, :], start=c == 0 and t == 0 and i == 0,
                                         stop=c == NCH - 1 and i == 2, skip_group_check=True)
                last.then_inc(down_ok, 1)

            def router(b):
                pe.wait_ge(x1T_ok, b + 1)
                for t in range(NT):
                    last = f32_product(O[:, 0, t * E:(t + 1) * E],
                                       [(x1T[:, k, t * P:(t + 1) * P], gw[:, k, :]) for k in range(KC)])
                last.then_inc(router_ok, 1)

            def by_token(dst, j, t):
                tok = slice(t * P, (t + 1) * P)
                return split_product(dst, [((xh[:, k, tok], xl[:, k, tok]), (att_hi[:, j, k, :], att_lo[:, j, k, :]))
                                           for k in range(KC)])

            def project(b, j):
                if isinstance(b, int) and b == -2:
                    pe.wait_ge(in_kvr[j], 16)
                for d in range(KC):
                    last = f32_product(Q[:, j, d * T:(d + 1) * T],
                                       [(wkvr[:, j, k, d * P:(d + 1) * P], mix[:, j, k, :]) for k in range(KC)])
                return last

            def ternary(b, f):
                if f == 0:
                    pe.wait_ge(x3h_ok, b)
                    pe.wait_ge(x3l_ok, b)
                    if isinstance(b, int) and b == 1:
                        pe.wait_ge(w12q_ok, 2)
                if f < 3:
                    if not isinstance(b, int) or b + 2 < B:
                        pe.wait_ge(kS_ok, b + 3)
                        pe.wait_ge(vS_ok, b + 3)
                        pe.wait_ge(ra_ok, b + 3)
                else:
                    pe.wait_ge(fx_ok, NF * (b - 1) + f - 2)
                cols = slice(f * P, (f + 1) * P)
                for i, w in enumerate((w1q, w2q)):
                    last = f32_product(Q[:, f % 3, i * T:(i + 1) * T],
                                       [(w[:, k, cols], xx[:, k, :]) for k in range(KC) for xx in (xh, xl)])
                last.then_inc(f12_ok, 1)

            def ternary_out(b, f):
                pe.wait_ge(fl_ok, NF * (b - 1) + f + 1)
                if f == 0 and (not isinstance(b, int) or b + 1 < B):
                    pe.wait_ge(r_ok[0], b + 2)
                if f == 0 and isinstance(b, int) and b == 1:
                    pe.wait_ge(w3q_ok, 1)
                for t in range(NT):
                    tok = slice(t * P, (t + 1) * P)
                    for i, l in enumerate((fh, fl)):
                        last = pe.matmul(O[:, t, :], l[:, f % SDEPTH, tok], w3q[:, f, :],
                                         start=f == 0 and t == 0 and i == 0, stop=f == NF - 1 and i == 1,
                                         skip_group_check=True)
                last.then_inc(w3_ok, 1)

            def slot(b, experts, attn, rwkv, proj):
                first = isinstance(b, int) and b == 0
                if not experts and attn:
                    pe.wait_ge(hu_ok, NCH * B)
                    keep_clock(WARM[3])
                if experts:
                    if first:
                        for s in (gate_hi_ok, gate_lo_ok, up_hi_ok, up_lo_ok):
                            pe.wait_ge(s, 1)
                    gate_up(b, 0)
                    gate_up(b, 1)
                    if first:
                        pe.wait_ge(in_gw, 16)
                    past(pe, r_ok[3], b - 1)
                    router(b)
                if attn:
                    pe.wait_ge(x_ok[1], b)
                    if experts:
                        pe.wait_ge(x1T_ok, b + 1)
                    transposes(x2, Tb).then_inc(x2Tp_ok, 1)
                if experts:
                    gate_up(b, 2)
                if attn and not experts:
                    keep_clock(WARM[4])
                if attn:
                    pe.wait_ge(x2h_ok, b)
                    pe.wait_ge(x2l_ok, b)
                    if isinstance(b, int) and b == 1:
                        pe.wait_ge(att_hi_ok, 1)
                        pe.wait_ge(att_lo_ok, 1)
                    past(pe, fx_ok, NF * (b - 1))
                    for j, s in ((1, k_ok), (2, v_ok)):
                        for t in range(NT):
                            last = by_token(Q[:, j, t * C:(t + 1) * C], j, t)
                        last.then_inc(s, 1)
                    for d in range(KC):
                        cols = slice(d * P, (d + 1) * P)
                        last = split_product(Q[:, 0, d * T:(d + 1) * T],
                                             [((att_hi[:, 0, k, cols], att_lo[:, 0, k, cols]),
                                               (xh[:, k, :], xl[:, k, :])) for k in range(KC)])
                    last.then_inc(q_ok, 1)
                if experts:
                    pe.wait_ge(twt_ok, b + 1)
                    for t in range(NT):
                        last = pe.transpose(Tb[:, 0, t * P:(t + 1) * P], twt[:, t, :], ident)
                    last.then_inc(twp_ok, 1)
                    gate_up(b, 3)
                if not experts:
                    keep_clock(WARM[5])
                if attn:
                    pe.wait_ge(kp_ok, b)
                    pe.wait_ge(vx_ok, b)
                    if experts:
                        pe.wait_ge(lg_ok, b + 1)
                    else:
                        pe.wait_ge(r_ok[3], b - 1)
                    for d in range(KC):
                        last = f32_product(O[:, d, 0:KVW], [(ke[:, t, d * P:(d + 1) * P], vx[:, t, d * P:d * P + KVW])
                                                            for t in range(NT)])
                    last.then_inc(kvp_ok, 1)
                if experts:
                    gate_up(b, 4)
                    down(b, 0)
                if attn:
                    pe.wait_ge(kvm_ok, b)
                    pe.wait_ge(qp_ok, b)
                    for t in range(NT):
                        for d in range(KC):
                            last = pe.matmul(Q[:, 1 + t, d * KVW:(d + 1) * KVW], qS[:, d, t * P:(t + 1) * P],
                                             kvm[:, d, :], start=True, stop=True)
                    last.then_inc(at_ok, 1)
                if proj:
                    pe.wait_ge(mixk_ok, b + 3)
                    if not attn:
                        past(pe, kS_ok, b + 2)
                    project(b, 0).then_inc(kp1_ok, 1)
                if experts:
                    down(b, 1)
                if attn:
                    if not experts:
                        keep_clock(WARM[6])
                    pe.wait_ge(an_ok, b)
                    if experts:
                        pe.wait_ge(tw_ok, b + 1)
                    transposes(an, Tb).then_inc(anTp_ok, 1)
                if experts:
                    gate_up(b, 5)
                    down(b, 2)
                if proj:
                    pe.wait_ge(mix_ok, b + 3)
                    if not attn:
                        past(pe, vS_ok, b + 2)
                        past(pe, ra_ok, b + 2)
                    project(b, 1)
                    project(b, 2).then_inc(kvr_ok, 1)
                if experts:
                    gate_up(b, 6)
                    down(b, 3)
                if attn:
                    if not experts:
                        keep_clock(WARM[7])
                    pe.wait_ge(anh_ok, b)
                    pe.wait_ge(anl_ok, b)
                    for t in range(NT):
                        last = by_token(O[:, t, :], 3, t)
                    last.then_inc(o3_ok, 1)
                if first:
                    pe.wait_ge(wsum_ok, 3)
                    pe.wait_ge(lg_ok, 1)
                    pe.matmul(O[:, 0, 0:3], ones[:, :], wsum[:, :], start=True, stop=True).then_inc(gamma_ok, 1)
                if experts:
                    gate_up(b, 7)
                    down(b, 4)
                if rwkv:
                    if not (experts or attn):
                        keep_clock(WARM[1])
                    pe.wait_ge(y_ok, b + 2)
                    if isinstance(b, int) and b == -1:
                        pe.wait_ge(in_wo1, 16)
                    if attn:
                        pe.wait_ge(r_ok[2], b)
                    elif first:
                        pe.wait_ge(thr_ok, 1)
                    for t in range(NT):
                        last = f32_product(O[:, t, :],
                                           [(y[:, k, t * P:(t + 1) * P], wo1[:, k, :]) for k in range(KC)])
                    last.then_inc(o1_ok, 1)
                if experts:
                    gate_up(b, 8)
                    down(b, 5)
                if attn and not experts:
                    keep_clock(WARM[8])
                if attn:
                    pe.wait_ge(x_ok[2], b)
                    transposes(x3, Tb).then_inc(x3Tp_ok, 1)
                if experts:
                    gate_up(b, 9)
                    down(b, 6)
                if attn and not experts:
                    keep_clock(WARM[9])
                if attn:
                    ternary(b, 0)
                    ternary(b, 1)
                if experts:
                    gate_up(b, 10)
                if attn:
                    ternary(b, 2)
                    ternary_out(b, 0)
                if experts:
                    down(b, 7)
                if rwkv:
                    if not (experts or attn):
                        keep_clock(WARM[2])
                    pe.wait_ge(x_ok[0], b + 2)
                    if attn:
                        pe.wait_ge(x3l_ok, b)
                    elif experts:
                        pe.wait_ge(tw_ok, b + 1)
                    if isinstance(b, int) and b == -1:
                        pe.wait_ge(in_cst, 16)
                    transposes(x1, Tb).then_inc(x1Tp_ok, 1)
                if attn:
                    ternary(b, 3)
                    ternary_out(b, 1)
                    ternary(b, 4)
                if experts:
                    down(b, 8)
                if attn:
                    ternary_out(b, 2)
                    ternary(b, 5)
                if experts:
                    down(b, 9)
                if attn:
                    ternary_out(b, 3)
                if experts:
                    down(b, 10)
                if attn:
                    ternary_out(b, 4)
                    ternary_out(b, 5)

            pe.wait_ge(preset, 3)
            keep_clock(WARM[0])
            slots(pe, slot)

        @block.scalar
        def _(act):
            def copy(dst, src):
                return act.activation(dst, src, ACT.Copy)

            def silu(b, c):
                act.wait_ge(gu_ok, NCH * b + c + 1)
                past(act, hl_ok, NCH * b + c + 1 - rotating(c, HDEPTH))
                act.activation(hb[:, c % HDEPTH, :], G[:, c % 2, 0, :], ACT.Silu).then_inc(silu_ok, 1)

            def h_high(b, c):
                act.wait_ge(h_ok, NCH * b + c + 1)
                past(act, down_ok, NCH * b + c + 1 - rotating(c, SDEPTH))
                copy(hh[:, c % SDEPTH, :], hb[:, c % HDEPTH, :]).then_inc(hh_ok, 1)

            def values_and_gate(b):
                act.wait_ge(kvr_ok, b + 3)
                past(act, v2_ok[0], b + 2)
                past(act, v2_ok[1], b + 2)
                copy(vS[:, :, :], Q[:, 1, :].rearrange("p (k t) -> p k t", k=KC)).then_inc(vS_ok, 1)
                r = Q[:, 2, :].rearrange("p (k t) -> p k t", k=KC)
                act.activation(ra[:, :, :], r, ACT.Abs)
                act.activation(rn[:, :, :], r, ACT.Relu, scale=-1.0).then_inc(ra_ok, 1)

            def exponentials(b):
                act.wait_ge(ar_ok, b + 2)
                act.activation(AR[:, :, :, :], AR[:, :, :, :], ACT.Exp).then_inc(exps_ok, 1)

            def gate_exponential(b):
                act.wait_ge(ra_ok, b + 2)
                act.activation(ra[:, :, :], ra[:, :, :], ACT.Exp, scale=-1.0).then_inc(ea_ok, 1)

            def tanh_half(b, f):
                act.wait_ge(f12_ok, NF * (b - 1) + f + 1)
                past(act, fl_ok, NF * (b - 1) + f + 1 - SDEPTH)
                act.activation(fb[:, f % SDEPTH, :], Q[:, f % 3, 0:T], ACT.Tanh, scale=0.5).then_inc(th_ok, 1)

            def f_high(b, f):
                act.wait_ge(fx_ok, NF * (b - 1) + f + 1)
                past(act, w3_ok, NF * (b - 1) + f + 1 - SDEPTH)
                copy(fh[:, f % SDEPTH, :], fb[:, f % SDEPTH, :]).then_inc(fh_ok, 1)

            def slot(b, experts, attn, rwkv, proj):
                first = isinstance(b, int) and b == 0
                if first:
                    exponentials(b)
                if experts:
                    act.wait_ge(x_ok[0], b + 1)
                    past(act, r_ok[1], b)
                    copy(x1k[:, :, :], x1[:, :, :]).then_inc(x1k_ok, 1)
                    silu(b, 0)
                    silu(b, 1)
                if attn:
                    act.wait_ge(x2Tp_ok, b)
                    copy(xh[:, :, :], Tb[:, :, :]).then_inc(x2h_ok, 1)
                if experts:
                    act.wait_ge(gap_ok, b + 1)
                    act.activation(gap[:, :], gap[:, :], ACT.Tanh, scale=0.5).then_inc(tanh_ok, 1)
                    silu(b, 2)
                if rwkv and not first:
                    exponentials(b)
                if rwkv:
                    if isinstance(b, int) and b == -1:
                        values_and_gate(b - 1)
                        gate_exponential(b)
                if isinstance(b, int) and b == -1:
                    act.wait_ge(in_up, 16)
                    copy(flat(up_hi), stage[1]).then_inc(up_hi_ok, 1)
                if attn:
                    act.wait_ge(kc_ok, b)
                    act.activation(ke, ke, ACT.Exp).then_inc(ke_ok, 1)
                if experts:
                    act.wait_ge(twp_ok, b + 1)
                    copy(TW[:, :], Tb[:, 0, :]).then_inc(tw_ok, 1)
                if rwkv and not (isinstance(b, int) and b == -1):
                    gate_exponential(b)
                if attn:
                    act.wait_ge(qt_ok, b)
                    act.activation(qS, qS, ACT.Exp).then_inc(qe_ok, 1)
                if experts:
                    h_high(b, 0)
                    silu(b, 3)
                    h_high(b, 1)
                    silu(b, 4)
                    h_high(b, 2)
                    h_high(b, 3)
                    silu(b, 5)
                    h_high(b, 4)
                if rwkv:
                    act.preload_act_table_set("natural_log_exp_and_others")
                    act.wait_ge(qq_ok, b + 2)
                    act.activation(AR[:, 2, :, :], AR[:, 2, :, :], ACT.Ln).then_inc(ln_ok, 1)
                if attn:
                    act.wait_ge(anTp_ok, b)
                    copy(xh[:, :, :], Tb[:, :, :]).then_inc(anh_ok, 1)
                if rwkv:
                    act.wait_ge(arg_ok, b + 2)
                    act.activation(AR[:, 3, :, :], AR[:, 3, :, :], ACT.Exp, scale=-1.0).then_inc(sr_ok, 1)
                if experts:
                    silu(b, 6)
                    h_high(b, 5)
                if proj:
                    act.wait_ge(kp1_ok, b + 3)
                    if rwkv:
                        act.wait_ge(t1_ok, b + 2)
                    copy(kS, Q[:, 0, :].rearrange("p (k t) -> p k t", k=KC)).then_inc(kS_ok, 1)
                    if not (isinstance(b, int) and b == -2):
                        values_and_gate(b)
                if isinstance(b, int) and b == -2:
                    act.wait_ge(in_gate, 16)
                    copy(flat(gate_hi), stage[0]).then_inc(gate_hi_ok, 1)
                if isinstance(b, int) and b == -1:
                    act.wait_ge(in_down, 16)
                    copy(flat(down_hi), stage[0]).then_inc(down_hi_ok, 1)
                if experts:
                    silu(b, 7)
                    h_high(b, 6)
                    silu(b, 8)
                    h_high(b, 7)
                if attn:
                    act.wait_ge(x3Tp_ok, b)
                    copy(xh[:, :, :], Tb[:, :, :]).then_inc(x3h_ok, 1)
                if experts:
                    silu(b, 9)
                    h_high(b, 8)
                if attn:
                    tanh_half(b, 0)
                    tanh_half(b, 1)
                    f_high(b, 0)
                if experts:
                    silu(b, 10)
                    h_high(b, 9)
                if attn:
                    f_high(b, 1)
                    tanh_half(b, 2)
                if rwkv:
                    act.wait_ge(x1Tp_ok, b + 2)
                    copy(x1T[:, :, :], Tb[:, :, :]).then_inc(x1T_ok, 1)
                if isinstance(b, int) and b == -1:
                    act.wait_ge(in_att, 64)
                    copy(att_hi[:, :, :, :], raw_att).then_inc(att_hi_ok, 1)
                if attn:
                    f_high(b, 2)
                    tanh_half(b, 3)
                if experts:
                    h_high(b, 10)
                if attn:
                    f_high(b, 3)
                    tanh_half(b, 4)
                    f_high(b, 4)
                    tanh_half(b, 5)
                    f_high(b, 5)

            act.wait_ge(in_vec, 16)
            act.activation(wdec[:, :], vec[:, :, TD_COL], ACT.Exp).then_inc(decay_e, 1)
            slots(act, slot)

        @block.vector
        def _(dve):
            def add_residual(i, psum, res, dst, value):
                dve.tensor_tensor(dst, psum, res, ALU.add).then_inc(r_ok[i], 1)
                dve.wait_ge(r_ok[i], value)
                for t in range(NT):
                    last = dve.bn_stats(st[:, i, t, :], dst[:, t, :])
                last.then_inc(st_ok[i], 1)
                dve.wait_ge(preset, 4)
                dve.wait_ge(st_ok[i], value)
                for t in range(NT):
                    last = dve.bn_aggr(mv[:, i, t, :], st[:, i, t, :])
                last.then_inc(mv_ok[i], 1)

            def normalise(i, src, dst, value):
                dve.wait_ge(rs_ok[i], value)
                dve.wait_ge(mv_ok[i], value)
                for t in range(NT):
                    last = dve.tensor_scalar(dst[:, t, :], src[:, t, :], mv[:, i, t, 0:1], rs[:, i, t:t + 1],
                                             ALU.subtract, ALU.mult)
                last.then_inc(x_ok[i], 1)

            def low_transposed(hi_ok, lo_ok, value):
                dve.wait_ge(hi_ok, value)
                dve.tensor_tensor(xl[:, :, :], Tb[:, :, :], xh[:, :, :].bitcast(F32), ALU.subtract).then_inc(lo_ok, 1)

            def maxima(b):
                dve.wait_ge(kS_ok, b + 3)
                for k in range(KC):
                    last = dve.tensor_tensor_scan(M[:, k, 1:], wdec[:, k:k + 1].broadcast_to([P, T]), kS[:, k, :],
                                                  LOW, ALU.add, ALU.max)
                last.then_inc(M_ok, 1)

            def divided(b):
                dve.wait_ge(at_ok, b)
                dve.tensor_scalar(zr[:, :, :], Q[:, 1:3, P:P + NH], Z_EPS, None, ALU.add).then_inc(ze_ok, 1)
                dve.wait_ge(ze_ok, b)
                dve.reciprocal(zr[:, :, :], zr[:, :, :]).then_inc(zr_ok, 1)
                dve.wait_ge(zr_ok, b)
                for t in range(NT):
                    src = Q[:, 1 + t, 0:KC * (P + NH)].rearrange("p (k c) -> p k c", k=KC)[:, :, 0:P].rearrange(
                        "p k (h e) -> p k h e", e=HEAD)
                    last = dve.tensor_tensor(
                        an[:, t, :].rearrange("p (k h e) -> p k h e", k=KC, e=HEAD), src,
                        zr[:, t, :].rearrange("p (k h) -> p k h", k=KC).unsqueeze(3).broadcast_to(
                            [P, KC, HK, HEAD]), ALU.mult)
                last.then_inc(an_ok, 1)

            def exponents(b, part):
                if part == 0:
                    dve.wait_ge(M_ok, b + 3)
                if part < KC:
                    k = part
                    dve.scalar_tensor_tensor(AR[:, 2, k, :], kS[:, k, :], vec[:, k, U_COL:U_COL + 1],
                                             M[:, k, 0:T], ALU.add, ALU.subtract)
                    last = dve.scalar_tensor_tensor(AR[:, 0, k, :], M[:, k, 0:T], wdec[:, k:k + 1],
                                                    M[:, k, 1:], ALU.add, ALU.subtract)
                    if part == KC - 1:
                        last.then_inc(lag_ok, 1)
                        dve.tensor_tensor(AR[:, 1, :, :], kS[:, :, :], M[:, :, 1:], ALU.subtract)
                else:
                    dve.wait_ge(lag_ok, b + 3)
                    dve.tensor_scalar(AR[:, 3, :, :], AR[:, 2, :, :], 0.0, None, ALU.min)
                    dve.tensor_scalar(AR[:, 2, :, :], AR[:, 2, :, :], 0.0, -1.0, ALU.max, ALU.mult)\
                       .then_inc(ar_ok, 1)

            def mixed(j):
                for k in range(KC):
                    last = dve.scalar_tensor_tensor(mix[:, j, k, :], dx[:, k, :], vec[:, k, MIX + j:MIX + j + 1],
                                                    xs[:, k, 0:T], ALU.mult, ALU.add)
                return last

            def gate_times_up(b, c):
                dve.wait_ge(silu_ok, NCH * b + c + 1)
                h = hb[:, c % HDEPTH, :]
                dve.tensor_tensor(h, h, G[:, c % 2, 1, :], ALU.mult).then_inc(hu_ok, 1)

            def ternary_gate(b, f):
                dve.wait_ge(th_ok, NF * (b - 1) + f + 1)
                h = fb[:, f % SDEPTH, :]
                dve.scalar_tensor_tensor(h, h, 1.0, Q[:, f % 3, T:2 * T], ALU.add, ALU.mult).then_inc(fx_ok, 1)

            def low_part(raw, hi, lo):
                return dve.tensor_tensor(lo, raw, hi.bitcast(F32), ALU.subtract)

            def quantise_sum(j):
                if j == 2:
                    dve.wait_ge(down_lo_ok, 1)
                    dve.memset(stage[0][HID % P:, (NF - 1) * C:NF * C], 0.0).then_inc(pads_ok, 1)
                    dve.wait_ge(in_w3, 32)
                    dve.wait_ge(pads_ok, 1)
                else:
                    dve.wait_ge(in_w12, 32)
                dve.tensor_reduce(wsum[:, j:j + 1], raw3 if j == 2 else raw12[:, j, :, :], mybir.AxisListType.XY,
                                  ALU.add, apply_absolute_value=True).then_inc(wsum_ok, 1)

            flat_mix = mix[:, :, :, :].rearrange("p a b c -> p (a b c)")

            def quantise_thresholds():
                dve.wait_ge(kvr_ok, 3)
                dve.wait_ge(gamma_ok, 1)
                for i, s in enumerate((0.5, -0.5)):
                    last = dve.tensor_scalar(thr[:, i, :], O[:, 0, 0:3], s / (C * HID), s * GAMMA_EPS, ALU.mult,
                                             ALU.add)
                last.then_inc(thr_ok, 1)
                dve.wait_ge(thr_ok, 1)

            def quantise(j, step):
                tmp = flat_mix[:, 0:KC * HID].rearrange("p (k n) -> p k n", k=KC)
                w = (w1q, w2q)[j]
                if step == 0:
                    if j:
                        dve.wait_ge(w12q_ok, 1)
                    dve.tensor_scalar(tmp, raw12[:, j, :, :], thr[:, 1, j:j + 1], None, ALU.is_lt).then_inc(w12a_ok, 1)
                else:
                    dve.wait_ge(w12a_ok, j + 1)
                    dve.scalar_tensor_tensor(w[:, :, 0:HID], raw12[:, j, :, :], thr[:, 0, j:j + 1], tmp,
                                             ALU.is_gt, ALU.subtract).then_inc(w12q_ok, 1)

            def quantise_out(step):
                below = flat_mix[:, 0:NF * C].rearrange("p (k c) -> p k c", k=NF)
                if step == 0:
                    dve.wait_ge(w12q_ok, 2)
                    dve.tensor_scalar(below, raw3, thr[:, 1, 2:3], 0.5, ALU.is_lt, ALU.mult).then_inc(w3a_ok, 1)
                elif step == 1:
                    dve.wait_ge(w3a_ok, 1)
                    dve.tensor_scalar(raw3, raw3, thr[:, 0, 2:3], 0.5, ALU.is_gt, ALU.mult).then_inc(w3a_ok, 1)
                else:
                    dve.wait_ge(w3a_ok, 2)
                    dve.tensor_tensor(w3q[:, :, :], raw3, below, ALU.subtract).then_inc(w3q_ok, 1)
                    dve.wait_ge(w3q_ok, 1)

            def slot(b, experts, attn, rwkv, proj):
                first = isinstance(b, int) and b == 0
                if experts:
                    gate_times_up(b, 0)
                if attn and not (isinstance(b, int) and b == 1):
                    normalise(3, x4, x4, b - 1)
                if experts:
                    gate_times_up(b, 1)
                if attn:
                    low_transposed(x2h_ok, x2l_ok, b)
                if experts:
                    dve.wait_ge(router_ok, b + 1)
                    dve.tensor_copy(lg[:, :, :], O[:, 0, 0:NT * E].rearrange("p (t e) -> p t e", t=NT))\
                       .then_inc(lg_ok, 1)
                    dve.wait_ge(preset, 4)
                    dve.wait_ge(lg_ok, b + 1)
                    for t in range(NT):
                        last = dve.max(mx8[:, t, :], lg[:, t, :])
                    last.then_inc(mx_ok, 1)
                    dve.wait_ge(mx_ok, b + 1)
                    past(dve, top_ok, b)
                    dve.tensor_tensor(gap[:, :], mx8[:, :, 1], mx8[:, :, 0], ALU.subtract).then_inc(gap_ok, 1)
                    for t in range(NT):
                        last = dve.max_index(ix8[:, t, :], mx8[:, t, :], lg[:, t, :])
                    last.then_inc(ix_ok, 1)
                    dve.wait_ge(ix_ok, b + 1)
                    dve.tensor_copy(sel[:, :, :], ix8[:, :, 0:2]).then_inc(sel_ok, 1)
                    if first:
                        dve.wait_ge(in_cst, 16)
                    dve.wait_ge(tanh_ok, b + 1)
                    for i, s in enumerate((-0.5, 0.5)):
                        last = dve.tensor_scalar(top[:, i, :], gap[:, :], s, 0.5, ALU.mult, ALU.add)
                    last.then_inc(top_ok, 1)
                    dve.wait_ge(top_ok, b + 1)
                    dve.wait_ge(sel_ok, b + 1)
                    past(dve, twp_ok, b)
                    for t in range(NT):
                        dve.tensor_scalar(twt[:, t, :], expert_of, sel[:, t, 0:1], top[:, 0, t:t + 1],
                                          ALU.is_equal, ALU.mult)
                        last = dve.tensor_scalar(twb[:, t, :], expert_of, sel[:, t, 1:2], top[:, 1, t:t + 1],
                                                 ALU.is_equal, ALU.mult)
                    last.then_inc(twab_ok, 1)
                    dve.wait_ge(twab_ok, b + 1)
                    dve.tensor_tensor(twt[:, :, :], twt[:, :, :], twb[:, :, :], ALU.add).then_inc(twt_ok, 1)
                    gate_times_up(b, 2)
                if attn:
                    if isinstance(b, int) and b == 1:
                        dve.wait_ge(in_msk, 64)
                    dve.wait_ge(k_ok, b)
                    dve.tensor_tensor(kt, Q[:, 1, :].rearrange("p (t c) -> p t c", t=NT),
                                      bias[:, 0:1, :].broadcast_to([P, NT, C]), ALU.add).then_inc(kt_ok, 1)
                    dve.wait_ge(kt_ok, b)
                    dve.tensor_scalar(ke, kt, 0.0, None, ALU.min).then_inc(kc_ok, 1)
                    dve.wait_ge(v_ok, b)
                    v = Q[:, 2, :].rearrange("p (t c) -> p t c", t=NT)
                    for k in range(KC):
                        last = dve.tensor_tensor(vx[:, :, k * KVW:k * KVW + P], v[:, :, k * P:(k + 1) * P],
                                                 bias[:, 1:2, k * P:(k + 1) * P].broadcast_to([P, NT, P]), ALU.add)
                    last.then_inc(vx_ok, 1)
                    dve.wait_ge(ke_ok, b)
                    dve.scalar_tensor_tensor(ke, kt, 1.0, ke, ALU.add, ALU.max).then_inc(kp_ok, 1)
                    dve.wait_ge(q_ok, b)
                    for k in range(KC):
                        last = dve.tensor_scalar(qS[:, k, :], Q[:, 0, k * T:(k + 1) * T], vec[:, k, QB_COL:QB_COL + 1],
                                                 0.0, ALU.add, ALU.min)
                    last.then_inc(qt_ok, 1)
                if proj:
                    dve.wait_ge(dx_ok, b + 3)
                    if not (isinstance(b, int) and b == -2):
                        dve.wait_ge(kvr_ok, b + 2)
                    mixed(0).then_inc(mixk_ok, 1)
                if first:
                    dve.wait_ge(att_hi_ok, 1)
                    low_part(raw_att, att_hi[:, :, :, :], att_lo[:, :, :, :]).then_inc(att_lo_ok, 1)
                    quantise_sum(2)
                if attn:
                    dve.wait_ge(qe_ok, b)
                    for k in range(KC):
                        last = dve.scalar_tensor_tensor(qS[:, k, :], Q[:, 0, k * T:(k + 1) * T], qb1[:, k:k + 1],
                                                        qS[:, k, :], ALU.add, ALU.max)
                    last.then_inc(qp_ok, 1)
                if attn:
                    dve.wait_ge(kvp_ok, b)
                    dve.tensor_tensor(kvm, O[:, :, 0:KVW], msk[:, :, :], ALU.mult).then_inc(kvm_ok, 1)
                if proj:
                    mixed(1)
                if experts:
                    gate_times_up(b, 3)
                if proj:
                    mixed(2).then_inc(mix_ok, 1)
                if attn:
                    divided(b)
                if rwkv:
                    dve.wait_ge(exps_ok, b + 2)
                    for k in range(KC):
                        dve.tensor_tensor_scan(ND[:, 1, k, 1:], AR[:, 0, k, :], AR[:, 1, k, :], 0.0, ALU.mult,
                                               ALU.add)
                    if isinstance(b, int) and b == -1:
                        dve.wait_ge(vS_ok, 1)
                        value_product(dve, 0)
                        value_product(dve, 1)
                    dve.wait_ge(v2_ok[0], b + 2)
                    for k in range(KC):
                        last = dve.tensor_tensor_scan(ND[:, 0, k, 1:], AR[:, 0, k, :], V2[:, 0, k, :], 0.0,
                                                      ALU.mult, ALU.add)
                    last.then_inc(nd_ok, 1)
                if experts:
                    gate_times_up(b, 4)
                if rwkv:
                    dve.wait_ge(nd_ok, b + 2)
                    for i in range(2):
                        last = dve.tensor_tensor(AR[:, i, :, :], ND[:, i, :, 0:T], AR[:, 2, :, :], ALU.mult)
                    last.then_inc(t1_ok, 1)
                    dve.wait_ge(t1_ok, b + 2)
                    dve.wait_ge(v2_ok[1], b + 2)
                    dve.tensor_tensor(V2[:, 0, :, :], AR[:, 0, :, :], V2[:, 1, :, :], ALU.add)
                    dve.tensor_tensor(AR[:, 1, :, :], AR[:, 1, :, :], AR[:, 3, :, :], ALU.add).then_inc(nd2_ok, 1)
                    dve.wait_ge(nd2_ok, b + 2)
                    dve.wait_ge(ea_ok, b + 2)
                    dve.scalar_tensor_tensor(AR[:, 2, :, :], ra[:, :, :], 1.0, AR[:, 1, :, :], ALU.add,
                                             ALU.mult).then_inc(qq_ok, 1)
                if first:
                    quantise_sum(0)
                if experts:
                    gate_times_up(b, 5)
                if attn:
                    low_transposed(anh_ok, anl_ok, b)
                if rwkv:
                    dve.wait_ge(ln_ok, b + 2)
                    dve.tensor_tensor(AR[:, 3, :, :], rn[:, :, :], AR[:, 2, :, :], ALU.add).then_inc(arg_ok, 1)
                if first:
                    quantise_sum(1)
                if experts:
                    gate_times_up(b, 6)
                if rwkv:
                    dve.wait_ge(sr_ok, b + 2)
                    dve.tensor_tensor(y, V2[:, 0, :, :], AR[:, 3, :, :], ALU.mult).then_inc(y_ok, 1)
                if attn:
                    dve.wait_ge(o3_ok, b)
                    dve.wait_ge(x2b_ok, b)
                    add_residual(2, O[:, :, :], x2, x3, b)
                if first:
                    quantise_thresholds()
                    quantise(0, 0)
                if experts:
                    gate_times_up(b, 7)
                if first:
                    quantise(0, 1)
                if attn:
                    normalise(2, x3, x3, b)
                if rwkv:
                    dve.wait_ge(o1_ok, b + 2)
                    dve.wait_ge(in_x, 16 * (b + 2))
                    add_residual(0, O[:, :, :], x1[:, :, :], x1[:, :, :], b + 2)
                if experts:
                    gate_times_up(b, 8)
                if proj and not attn:
                    maxima(b)
                if rwkv:
                    normalise(0, x1, x1, b + 2)
                if first:
                    quantise(1, 0)
                if attn:
                    low_transposed(x3h_ok, x3l_ok, b)
                if experts:
                    gate_times_up(b, 9)
                if first:
                    quantise(1, 1)
                    quantise_out(0)
                if attn:
                    if proj:
                        maxima(b)
                    ternary_gate(b, 0)
                if proj:
                    exponents(b, 0)
                if attn:
                    ternary_gate(b, 1)
                if experts:
                    gate_times_up(b, 10)
                if first:
                    quantise_out(1)
                if proj:
                    exponents(b, 1)
                if attn:
                    ternary_gate(b, 2)
                if rwkv:
                    dve.wait_ge(x1T_ok, b + 2)
                    if experts:
                        dve.wait_ge(gu_ok, NCH * (b + 1))
                    dve.tensor_copy(x1h[:, :, :], x1T[:, :, :]).then_inc(x1h_ok, 1)
                    dve.wait_ge(x1h_ok, b + 2)
                    dve.tensor_tensor(x1l[:, :, :], x1T[:, :, :], x1h[:, :, :].bitcast(F32), ALU.subtract)\
                       .then_inc(x1l_ok, 1)
                if first:
                    quantise_out(2)
                if attn:
                    ternary_gate(b, 3)
                if proj:
                    exponents(b, 2)
                if attn:
                    ternary_gate(b, 4)
                    ternary_gate(b, 5)
                if experts:
                    dve.wait_ge(down_ok, NCH * (b + 1))
                    dve.wait_ge(x1k_ok, b + 1)
                    if attn:
                        dve.wait_ge(r_ok[2], b)
                    add_residual(1, D[:, :, :], x1k[:, :, :], x2, b + 1)
                if attn:
                    dve.wait_ge(w3_ok, NF * b)
                    past(dve, out_x4, 16 * (b - 1))
                    add_residual(3, O[:, :, :], x3, x4[:, :, :], b)
                if experts:
                    if first:
                        dve.memset(vx[:, :, P:KVW], 1.0)
                    normalise(1, x2, x2, b + 1)
                if attn and not experts:
                    normalise(3, x4, x4, b)

            dve.memset(xs[:, :, 0:1], 0.0).then_inc(preset, 1)
            dve.memset(M[:, :, 0:1], LOW)
            dve.memset(ND[:, :, :, 0:1], 0.0).then_inc(preset, 1)
            dve.memset(ones[:, :], 1.0).then_inc(preset, 1)
            dve.memset(w1q[:, :, HID:].bitcast(F32), 0.0)
            dve.memset(w2q[:, :, HID:].bitcast(F32), 0.0)
            dve.memset(eps[:, :], LN_EPS)
            dve.memset(neghalf[:, :], -0.5).then_inc(preset, 1)
            dve.wait_ge(preset, 4)
            dve.wait_ge(in_xT, 16)
            difference(dve)
            dve.wait_ge(in_vec, 16)
            dve.tensor_scalar(qb1[:, :], vec[:, :, QB_COL], 1.0, None, ALU.add)
            dve.wait_ge(decay_e, 1)
            dve.tensor_scalar(wdec[:, :], wdec[:, :], -1.0, None, ALU.mult).then_inc(wdec_ok, 1)
            dve.wait_ge(wdec_ok, 1)
            slots(dve, slot)

        @block.gpsimd
        def _(pool):
            def deviation(i, value):
                pool.wait_ge(mv_ok[i], value)
                pool.tensor_tensor(ve[:, i, :], mv[:, i, :, 1], eps[:, :], ALU.add).then_inc(ve_ok[i], 1)
                pool.wait_ge(ve_ok[i], value)
                pool.tensor_tensor(rs[:, i, :], ve[:, i, :], neghalf[:, :], ALU.pow).then_inc(rs_ok[i], 1)

            def low_part(hi_ok, raw, hi, lo, lo_ok):
                pool.wait_ge(hi_ok, 1)
                pool.tensor_tensor(flat(lo), raw, flat(hi).bitcast(F32), ALU.subtract).then_inc(lo_ok, 1)

            def next_difference(b):
                pool.wait_ge(in_xT, 16 * (b + 3))
                pool.wait_ge(mix_ok, b + 2)
                difference(pool)

            def weigh(b, c):
                pool.wait_ge(hu_ok, NCH * b + c + 1)
                if c == 0:
                    pool.wait_ge(tw_ok, b + 1)
                h = hb[:, c % HDEPTH, :]
                pool.tensor_tensor(h, h, TW[:, :], ALU.mult).then_inc(h_ok, 1)

            def h_low(b, c):
                pool.wait_ge(hh_ok, NCH * b + c + 1)
                pool.tensor_tensor(hl[:, c % SDEPTH, :], hb[:, c % HDEPTH, :], hh[:, c % SDEPTH, :].bitcast(F32),
                                   ALU.subtract).then_inc(hl_ok, 1)

            def f_low(b, f):
                pool.wait_ge(fh_ok, NF * (b - 1) + f + 1)
                pool.tensor_tensor(fl[:, f % SDEPTH, :], fb[:, f % SDEPTH, :], fh[:, f % SDEPTH, :].bitcast(F32),
                                   ALU.subtract).then_inc(fl_ok, 1)

            def slot(b, experts, attn, rwkv, proj):
                if isinstance(b, int) and b == -1:
                    next_difference(b)
                if attn:
                    pool.wait_ge(x2Tp_ok, b)
                    pool.tensor_tensor(x2, x2, bias[:, 2:3, :].broadcast_to([P, NT, C]), ALU.add)\
                        .then_inc(x2b_ok, 1)
                if proj and not (isinstance(b, int) and b < 0):
                    next_difference(b)
                if rwkv and not (isinstance(b, int) and b == -1):
                    pool.wait_ge(exps_ok, b + 2)
                    pool.wait_ge(vS_ok, b + 2)
                    pool.wait_ge(o1_ok, b + 1)
                    value_product(pool, 0)
                if isinstance(b, int) and b == -1:
                    low_part(gate_hi_ok, stage[0], gate_hi, gate_lo, gate_lo_ok)
                    low_part(up_hi_ok, stage[1], up_hi, up_lo, up_lo_ok)
                if experts:
                    weigh(b, 0)
                    weigh(b, 1)
                    h_low(b, 0)
                if rwkv and not (isinstance(b, int) and b == -1):
                    value_product(pool, 1)
                if experts:
                    weigh(b, 2)
                    h_low(b, 1)
                    weigh(b, 3)
                    h_low(b, 2)
                    weigh(b, 4)
                    h_low(b, 3)
                    weigh(b, 5)
                    h_low(b, 4)
                    weigh(b, 6)
                if attn:
                    deviation(2, b)
                if experts:
                    h_low(b, 5)
                    weigh(b, 7)
                if rwkv:
                    deviation(0, b + 2)
                if isinstance(b, int) and b == -1:
                    low_part(down_hi_ok, stage[0], down_hi, down_lo, down_lo_ok)
                if experts:
                    h_low(b, 6)
                    weigh(b, 8)
                    h_low(b, 7)
                    weigh(b, 9)
                if attn:
                    f_low(b, 0)
                if experts:
                    h_low(b, 8)
                    weigh(b, 10)
                if attn:
                    f_low(b, 1)
                    f_low(b, 2)
                if experts:
                    h_low(b, 9)
                if attn:
                    f_low(b, 3)
                if experts:
                    h_low(b, 10)
                if attn:
                    f_low(b, 4)
                    f_low(b, 5)
                if experts:
                    deviation(1, b + 1)
                if attn:
                    deviation(3, b)

            pool.wait_ge(preset, 4)
            slots(pool, slot)


def kernel(**inputs):
    import numpy as np
    import concourse.bacc as bacc
    from concourse.bass_utils import run_bass_kernel_spmd

    a = {k: np.asarray(v) for k, v in inputs.items()}
    f32 = np.float32

    def turned(w):
        return np.ascontiguousarray(w.T)

    def by_channel(w):
        t = w.reshape(E, NCH, FE, KC, P).transpose(4, 3, 1, 0, 2)
        return np.ascontiguousarray(t).reshape(P, KC * NCH * P)

    vec = np.stack([a["L0_attn_time_mix_k"], a["L0_attn_time_mix_v"], a["L0_attn_time_mix_r"],
                    a["L0_attn_time_first"], a["L0_attn_time_decay"], a["L1_attn_q_b"]], axis=-1)
    consts = np.zeros((P, 2, P), f32)
    consts[:, 0, :] = np.eye(P, dtype=f32)
    consts[:, 1, :] = np.repeat(np.arange(E, dtype=f32), FE)
    heads = np.arange(P) // HEAD
    share = (heads[:, None] == heads[None, :]).astype(f32)
    own = (heads[:, None] == np.arange(HK)[None, :]).astype(f32)
    mask = np.stack([np.concatenate([share, own], 1), np.concatenate([own, share], 1)], 1)
    arrays = {
        "xT": np.ascontiguousarray(a["L0_attn_x"].reshape(B * T, C).T),
        "x": a["L0_attn_x"],
        "vecs": np.ascontiguousarray(vec.reshape(KC, P, NVEC).transpose(1, 0, 2)),
        "rows": np.stack([a["L1_attn_k_b"], a["L1_attn_v_b"], a["L1_attn_o_b"]]),
        "consts": consts,
        "mask": mask,
        "Wk": turned(a["L0_attn_Wk"]), "Wv": turned(a["L0_attn_Wv"]), "Wr": turned(a["L0_attn_Wr"]),
        "Wo": turned(a["L0_attn_Wo"]),
        "gate_w": turned(a["L0_ffn_gate_w"]),
        "w_gate": by_channel(a["L0_ffn_gate_proj"]),
        "w_up": by_channel(a["L0_ffn_up_proj"]),
        "w_down": np.ascontiguousarray(
            a["L0_ffn_down_proj"].reshape(E, C, NCH, FE).transpose(0, 3, 2, 1)).reshape(P, NCH * C),
        "Wq3": turned(a["L1_attn_q_w"]), "Wk3": turned(a["L1_attn_k_w"]), "Wv3": turned(a["L1_attn_v_w"]),
        "Wo3": turned(a["L1_attn_o_w"]),
        "W1": turned(a["L1_ffn_w1"]), "W2": turned(a["L1_ffn_w2"]), "W3": turned(a["L1_ffn_w3"]),
    }
    nc = bacc.Bacc("TRN2", target_bir_lowering=False, num_devices=1)
    args = [nc.dram_tensor(f"in_{k}", v.shape, mybir.dt.from_np(v.dtype), kind="ExternalInput").ap()
            for k, v in arrays.items()]
    out = nc.dram_tensor("out_0", (B, T, C), F32, kind="ExternalOutput").ap()
    build(nc, *args, out)
    r = run_bass_kernel_spmd(nc, [{f"in_{k}": v for k, v in arrays.items()}], core_ids=[0])
    return r.results[0]["out_0"]
```

```python
from contextlib import ExitStack

import concourse.bass as bass
from concourse import mybir

P = 128
F32 = mybir.dt.float32
F32R = mybir.dt.float32r
U32 = mybir.dt.uint32
ALU = mybir.AluOpType
ACT = mybir.ActivationFunctionType

B, T, C = 8, 256, 256
KC = C // P
NT = T // P
E, F = 8, 176
FE = P // E
NCH = F // FE
HID = 704
NF = -(-HID // P)
HEAD = 16
NH = C // HEAD
HK = NH // KC
KVW = P + HK
VW = C + HK
LN_EPS = 1e-5
Z_EPS = 1e-6
GAMMA_EPS = 1e-8
LOW = -1e38
MIX, U_COL, TD_COL, QB_COL = 0, 3, 4, 5
NVEC = 6
WARM = (10, 9, 9, 10, 5, 5, 4, 5, 12, 5)
HDEPTH = 4
SDEPTH = 3


def rotating(c, depth, per_batch=NCH):
    if c >= depth:
        return depth
    back = [x for x in range(per_batch) if x % depth == c % depth][-1]
    return per_batch - back + c


def past(eng, sem, value):
    if isinstance(value, int) and value < 1:
        return
    eng.wait_ge(sem, value)


def build(nc, xT, x, vecs, rows, consts, mask, Wk, Wv, Wr, Wo, gate_w, w_gate, w_up, w_down,
          Wq3, Wk3, Wv3, Wo3, W1, W2, W3, out):
    ctx = ExitStack()
    with ctx:
        def sb(name, shape, dt=F32):
            return ctx.enter_context(nc.sbuf_tensor(name, shape, dt))

        def pb(name, shape):
            return ctx.enter_context(nc.psum_tensor(name, shape, F32))

        def sem(name):
            return ctx.enter_context(nc.semaphore(name))

        kvr_hi = sb("kvr_hi", [P, 3, KC, C], F32R)
        kvr_lo = sb("kvr_lo", [P, 3, KC, C], F32R)
        wo1 = sb("wo1", [P, KC, C])
        att_hi = sb("att_hi", [P, 4, KC, C], F32R)
        att_lo = sb("att_lo", [P, 4, KC, C], F32R)
        gw = sb("gw", [P, KC, E])
        gw_hi = sb("gw_hi", [P, KC, E], F32R)
        gw_lo = sb("gw_lo", [P, KC, E], F32R)
        gate_hi = sb("gate_hi", [P, KC, NCH * P], F32R)
        gate_lo = sb("gate_lo", [P, KC, NCH * P], F32R)
        up_hi = sb("up_hi", [P, KC, NCH * P], F32R)
        up_lo = sb("up_lo", [P, KC, NCH * P], F32R)
        down_hi = sb("down_hi", [P, NCH, C], F32R)
        down_lo = sb("down_lo", [P, NCH, C], F32R)
        w1q = sb("w1q", [P, KC, NF * P], F32R)
        w2q = sb("w2q", [P, KC, NF * P], F32R)
        w3q = sb("w3q", [P, NF, C], F32R)
        vec = sb("vec", [P, KC, NVEC])
        wdec = sb("wdec", [P, KC])
        qb1 = sb("qb1", [P, KC])
        bias_o = sb("bias_o", [P, C])
        cst = sb("cst", [P, 2, P])
        msk = sb("msk", [P, KC, KVW])
        ones = sb("ones", [P, P])
        neghalf = sb("neghalf", [P, NT])
        eps = sb("eps", [P, NT])
        ident = cst[:, 0, :]
        expert_of = cst[:, 1, :]

        xs = sb("xs", [P, KC, 1 + T])
        dx = sb("dx", [P, KC, T])
        mix = sb("mix", [P, 2, 2, KC, T], F32R)
        vS = sb("vS", [P, KC, T])
        ra = sb("ra", [P, KC, T])
        rn = sb("rn", [P, KC, T])
        M = sb("M", [P, KC, 1 + T])
        AR = sb("AR", [P, 4, KC, T])
        V2 = sb("V2", [P, 2, KC, T])
        ND = sb("ND", [P, 2, KC, 1 + T])
        kS = ND[:, 0, :, 1:]
        y = V2[:, 1, :, :]
        x1 = sb("x1", [P, NT, C])
        x1k = sb("x1k", [P, NT, C])
        x1h = sb("x1h", [P, KC, T], F32R)
        x1l = sb("x1l", [P, KC, T], F32R)
        hb = sb("hb", [P, HDEPTH, T])
        hh = sb("hh", [P, SDEPTH, T], F32R)
        hl = sb("hl", [P, SDEPTH, T], F32R)
        TW = sb("TW", [P, T])
        twt = sb("twt", [P, NT, P])
        twb = sb("twb", [P, NT, P])
        lg = sb("lg", [P, NT, E])
        mx8 = sb("mx8", [P, NT, 8])
        ix8 = sb("ix8", [P, NT, 8], U32)
        sel = sb("sel", [P, NT, 2])
        gap = sb("gap", [P, NT])
        top = sb("top", [P, 2, NT])
        STAGE = KC * NCH * P
        arena = sb("arena", [P, 2 * STAGE])
        stage = [arena[:, i * STAGE:(i + 1) * STAGE] for i in range(2)]
        raw_kvr = stage[1][:, 0:3 * KC * C].rearrange("p (j k n) -> p j k n", j=3, k=KC)
        raw_att = stage[1][:, 0:4 * KC * C].rearrange("p (j k n) -> p j k n", j=4, k=KC)
        raw12 = stage[1][:, 0:2 * KC * HID].rearrange("p (j k n) -> p j k n", j=2, k=KC)
        raw3 = stage[0][:, 0:NF * C].rearrange("p (k c) -> p k c", k=NF)
        U = KC * T
        x2 = arena[:, 0:U].rearrange("p (t c) -> p t c", t=NT)
        x3 = arena[:, U:2 * U].rearrange("p (t c) -> p t c", t=NT)
        qS = arena[:, 2 * U:3 * U].rearrange("p (k t) -> p k t", k=KC)
        x4 = arena[:, 3 * U:4 * U].rearrange("p (t c) -> p t c", t=NT)
        kt = x4
        ke = arena[:, 4 * U:5 * U].rearrange("p (t c) -> p t c", t=NT)
        an = arena[:, 5 * U:6 * U].rearrange("p (t c) -> p t c", t=NT)
        bias = arena[:, 6 * U:6 * U + 2 * C].rearrange("p (j c) -> p j c", j=2)
        VX = 6 * U + 2 * C
        KV, FB = VX + NT * VW, VX + NT * VW + KC * KVW
        vx = arena[:, VX:KV].rearrange("p (t c) -> p t c", t=NT)
        kvm = arena[:, KV:FB].rearrange("p (k c) -> p k c", k=KC)
        fb = arena[:, FB:FB + SDEPTH * T].rearrange("p (s t) -> p s t", s=SDEPTH)
        assert FB + SDEPTH * T <= 2 * STAGE
        zr = sb("zr", [P, NT, NH])
        xh = sb("xh", [P, KC, T], F32R)
        xl = sb("xl", [P, KC, T], F32R)
        fh = sb("fh", [P, SDEPTH, T], F32R)
        fl = sb("fl", [P, SDEPTH, T], F32R)
        wsum = sb("wsum", [P, 3])
        thr = sb("thr", [P, 2, 3])
        st = sb("st", [P, 4, NT, 6])
        mv = sb("mv", [P, 4, NT, 2])
        ve = sb("ve", [P, 4, NT])
        rs = sb("rs", [P, 4, NT])

        G = pb("G", [P, 2, 2, T])
        D = pb("D", [P, NT, C])
        Tb = pb("Tb", [P, KC, T])
        Q = pb("Q", [P, 3, 2 * T])
        O = pb("O", [P, NT, C])

        in_vec, in_cst, in_msk, in_wo1, in_gw, in_xT, in_x = map(
            sem, ("in_vec", "in_cst", "in_msk", "in_wo1", "in_gw", "in_xT", "in_x"))
        in_kvr = [sem(f"in_w{j}") for j in "kvr"]
        kvr_hi_ok, k_lo_ok, vr_lo_ok, in_bias = map(sem, ("kvr_hi_ok", "k_lo_ok", "vr_lo_ok", "in_bias"))
        mixf_ok, mixh_ok, mixl_ok = map(sem, ("mixf_ok", "mixh_ok", "mixl_ok"))
        in_gate, in_up, in_down, in_w12, in_w3 = map(sem, ("in_gate", "in_up", "in_down", "in_w12", "in_w3"))
        in_att, out_x4, att_hi_ok, att_lo_ok = map(sem, ("in_att", "out_x4", "att_hi_ok", "att_lo_ok"))
        preset, decay_e, wdec_ok, pads_ok = map(sem, ("preset", "decay_e", "wdec_ok", "pads_ok"))
        gate_hi_ok, gate_lo_ok = sem("gate_hi_ok"), sem("gate_lo_ok")
        up_hi_ok, up_lo_ok = sem("up_hi_ok"), sem("up_lo_ok")
        down_hi_ok, down_lo_ok = sem("down_hi_ok"), sem("down_lo_ok")
        wsum_ok, gamma_ok, thr_ok, w12a_ok, w12q_ok, w3a_ok, w3q_ok = map(
            sem, ("wsum_ok", "gamma_ok", "thr_ok", "w12a_ok", "w12q_ok", "w3a_ok", "w3q_ok"))
        dx_ok, kp1_ok, vp1_ok, kvr_ok, kS_ok, vS_ok, ra_ok, M_ok = map(
            sem, ("dx_ok", "kp1_ok", "vp1_ok", "kvr_ok", "kS_ok", "vS_ok", "ra_ok", "M_ok"))
        lag_ok, ar_ok, exps_ok, ea_ok, nd_ok, t1_ok = map(
            sem, ("lag_ok", "ar_ok", "exps_ok", "ea_ok", "nd_ok", "t1_ok"))
        nd2_ok, qq_ok, ln_ok, arg_ok, sr_ok, y_ok, o1_ok = map(
            sem, ("nd2_ok", "qq_ok", "ln_ok", "arg_ok", "sr_ok", "y_ok", "o1_ok"))
        v2_ok = [sem("v2_next_ok"), sem("v2_out_ok")]
        r_ok = [sem(f"r{i}_ok") for i in range(4)]
        st_ok = [sem(f"st{i}_ok") for i in range(4)]
        mv_ok = [sem(f"mv{i}_ok") for i in range(4)]
        ve_ok = [sem(f"ve{i}_ok") for i in range(4)]
        rs_ok = [sem(f"rs{i}_ok") for i in range(4)]
        x_ok = [sem(f"x{i}_ok") for i in range(4)]
        x1k_ok, x1Tp_ok, x1h_ok, x1l_ok, gw_hi_ok, gw_lo_ok = map(
            sem, ("x1k_ok", "x1Tp_ok", "x1h_ok", "x1l_ok", "gw_hi_ok", "gw_lo_ok"))
        router_ok, lg_ok, mx_ok, ix_ok, gap_ok, tanh_ok, sel_ok, top_ok, twab_ok, twt_ok, twp_ok, tw_ok = map(
            sem, ("router_ok", "lg_ok", "mx_ok", "ix_ok", "gap_ok", "tanh_ok", "sel_ok", "top_ok", "twab_ok",
                  "twt_ok", "twp_ok", "tw_ok"))
        gu_ok, silu_ok, hu_ok, h_ok, hh_ok, hl_ok, down_ok = map(
            sem, ("gu_ok", "silu_ok", "hu_ok", "h_ok", "hh_ok", "hl_ok", "down_ok"))
        x2Tp_ok, x2h_ok, x2l_ok, x2b_ok, q_ok, k_ok, v_ok = map(
            sem, ("x2Tp_ok", "x2h_ok", "x2l_ok", "x2b_ok", "q_ok", "k_ok", "v_ok"))
        qt_ok, qe_ok, qp_ok, kt_ok, kc_ok, ke_ok, kp_ok, vx_ok = map(
            sem, ("qt_ok", "qe_ok", "qp_ok", "kt_ok", "kc_ok", "ke_ok", "kp_ok", "vx_ok"))
        kvp_ok, kvm_ok, at_ok, ze_ok, zr_ok, an_ok, anTp_ok, anh_ok, anl_ok, o3_ok = map(
            sem, ("kvp_ok", "kvm_ok", "at_ok", "ze_ok", "zr_ok", "an_ok", "anTp_ok", "anh_ok", "anl_ok", "o3_ok"))
        x3Tp_ok, x3h_ok, x3l_ok, f12_ok, th_ok, fx_ok, fh_ok, fl_ok, w3_ok = map(
            sem, ("x3Tp_ok", "x3h_ok", "x3l_ok", "f12_ok", "th_ok", "fx_ok", "fh_ok", "fl_ok", "w3_ok"))

        xT_v = xT.rearrange("(k p) (n t) -> n p k t", p=P, t=T)
        x_v = x.rearrange("n (t p) c -> n p t c", p=P)
        out_v = out.rearrange("n (t p) c -> n p t c", p=P)

        def batch_of(view, n):
            return view[bass.ds(n, 1)].rearrange("n p a b -> (n p) a b") if not isinstance(n, int) else view[n]

        def flat(w):
            return w[:, :, :].rearrange("p a b -> p (a b)")

        def chunked(w):
            return w.rearrange("(k p) d -> p k d", p=P)

        LOOP = (2, B - 2)

        def slots(eng, slot):
            for b in range(-2, LOOP[0]):
                slot(b, 0 <= b, 1 <= b, -1 <= b, True)
            with eng.Fori(*LOOP) as b:
                slot(b, True, True, True, True)
            for b in range(LOOP[1], B + 1):
                slot(b, b < B, True, b + 1 < B, b + 2 < B)

        def difference(eng):
            eng.tensor_tensor(dx[:, :, :], xs[:, :, 1:], xs[:, :, 0:T], ALU.subtract).then_inc(dx_ok, 1)

        mix_full = (M[:, :, 1:], M[:, :, 1:], dx[:, :, :])

        def mix_low(eng, j):
            eng.tensor_tensor(mix[:, 1, j % 2, :, :], mix_full[j], mix[:, 0, j % 2, :, :].bitcast(F32),
                              ALU.subtract).then_inc(mixl_ok, 1)

        def value_product(eng, i):
            eng.tensor_tensor(V2[:, i, :, :], AR[:, 1 + 2 * i, :, :], vS[:, :, :], ALU.mult).then_inc(v2_ok[i], 1)

        block = ctx.enter_context(nc.Block())

        @block.sync
        def _(sp):
            sp.dma_start(xs[:, :, 1:], xT_v[0]).then_inc(in_xT, 16)
            sp.dma_start(vec[:, :, :], vecs).then_inc(in_vec, 16)
            for j, w in enumerate((Wk, Wv, Wr)):
                sp.dma_start(raw_kvr[:, j, :, :], chunked(w)).then_inc(in_kvr[j], 16)
            sp.dma_start(cst[:, :, :], consts).then_inc(in_cst, 16)
            sp.dma_start(stage[0], w_gate).then_inc(in_gate, 16)

            def slot(b, experts, attn, rwkv, proj):
                if isinstance(b, int) and b == -2:
                    sp.wait_ge(kvr_hi_ok, 3)
                    sp.wait_ge(k_lo_ok, 1)
                    sp.wait_ge(vr_lo_ok, 2)
                    sp.dma_start(stage[1], w_up).then_inc(in_up, 16)
                    sp.wait_ge(mixf_ok, 3)
                    sp.dma_start(xs[:, :, 1:], xT_v[1]).then_inc(in_xT, 16)
                    sp.dma_start(wo1[:, :, :], chunked(Wo)).then_inc(in_wo1, 16)
                    return
                if proj and not (isinstance(b, int) and b == -1):
                    sp.wait_ge(mixf_ok, 3 * (b + 2))
                    sp.dma_start(xs[:, :, 1:], batch_of(xT_v, b + 2)).then_inc(in_xT, 16)
                if rwkv:
                    if experts:
                        sp.wait_ge(x1k_ok, b + 1)
                        sp.wait_ge(x1Tp_ok, b + 1)
                    sp.dma_start(x1[:, :, :], batch_of(x_v, b + 1)).then_inc(in_x, 16)
                if isinstance(b, int) and b == -1:
                    sp.dma_start(gw[:, :, :], chunked(gate_w)).then_inc(in_gw, 16)
                    sp.wait_ge(gate_hi_ok, 1)
                    sp.wait_ge(gate_lo_ok, 1)
                    sp.dma_start(stage[0], w_down).then_inc(in_down, 16)
                    sp.dma_start(msk[:, :, :], mask).then_inc(in_msk, 16)
                    sp.dma_start(bias_o[:, :], rows[2:3, :].broadcast_to([P, C])).then_inc(in_msk, 16)
                    sp.wait_ge(up_hi_ok, 1)
                    sp.wait_ge(up_lo_ok, 1)
                    for j, w in enumerate((Wq3, Wk3, Wv3, Wo3)):
                        sp.dma_start(raw_att[:, j, :, :], chunked(w)).then_inc(in_att, 16)
                if isinstance(b, int) and b == 0:
                    sp.wait_ge(down_hi_ok, 1)
                    sp.wait_ge(down_lo_ok, 1)
                    full = HID // P
                    sp.dma_start(raw3[:, 0:full, :], chunked(W3[0:full * P, :])).then_inc(in_w3, 16)
                    sp.dma_start(raw3[0:HID - full * P, full, :], W3[full * P:HID, :]).then_inc(in_w3, 16)
                    sp.wait_ge(att_hi_ok, 1)
                    sp.wait_ge(att_lo_ok, 1)
                    for i, w in enumerate((W1, W2)):
                        sp.dma_start(raw12[:, i, :, :], chunked(w)).then_inc(in_w12, 16)
                    sp.wait_ge(w12q_ok, 2)
                    for i in range(2):
                        sp.dma_start(bias[:, i, :], rows[i:i + 1, :].broadcast_to([P, C])).then_inc(in_bias, 16)
                if attn:
                    sp.wait_ge(x_ok[3], b)
                    sp.dma_start(batch_of(out_v, b - 1), x4[:, :, :]).then_inc(out_x4, 16)

            slots(sp, slot)
            sp.wait_ge(out_x4, 16 * B)

        @block.tensor
        def _(pe):
            def f32_product(dst, pairs):
                for i, (l, r) in enumerate(pairs):
                    last = pe.matmul(dst, l, r, start=i == 0, stop=i == len(pairs) - 1)
                return last

            def transposes(src, dst):
                for t in range(NT):
                    for k in range(KC):
                        last = pe.transpose(dst[:, k, t * P:(t + 1) * P], src[:, t, k * P:(k + 1) * P], ident)
                return last

            def split_product(dst, pairs):
                return f32_product(dst, [p for (lh, ll), (rh, rl) in pairs for p in ((lh, rh), (lh, rl), (ll, rh))])

            def keep_clock(n):
                for _ in range(n):
                    pe.matmul(G[:, 0, 0, 0:P], ones[:, :], ones[:, :], start=True, stop=True)

            def gate_up(b, c):
                if c == 0:
                    pe.wait_ge(x1h_ok, b + 1)
                    pe.wait_ge(x1l_ok, b + 1)
                past(pe, hu_ok, NCH * b + c - 1)
                cols = slice(c * P, (c + 1) * P)
                for i, (wh, wl) in enumerate(((gate_hi, gate_lo), (up_hi, up_lo))):
                    last = f32_product(G[:, c % 2, i, :], [
                        (w[:, k, cols], xx[:, k, :]) for k in range(KC)
                        for w, xx in ((wh, x1h), (wh, x1l), (wl, x1h))])
                last.then_inc(gu_ok, 1)

            def down(b, c):
                pe.wait_ge(hl_ok, NCH * b + c + 1)
                if c == 0:
                    if isinstance(b, int) and b == 0:
                        pe.wait_ge(down_hi_ok, 1)
                        pe.wait_ge(down_lo_ok, 1)
                    past(pe, r_ok[1], b)
                s = c % SDEPTH
                for t in range(NT):
                    tok = slice(t * P, (t + 1) * P)
                    for i, (l, r) in enumerate(((hh, down_hi), (hh, down_lo), (hl, down_hi))):
                        last = pe.matmul(D[:, t, :], l[:, s, tok], r[:, c, :], start=c == 0 and t == 0 and i == 0,
                                         stop=c == NCH - 1 and i == 2, skip_group_check=True)
                last.then_inc(down_ok, 1)

            def router(b):
                for t in range(NT):
                    tok = slice(t * P, (t + 1) * P)
                    last = split_product(O[:, 0, t * E:(t + 1) * E],
                                         [((x1h[:, k, tok], x1l[:, k, tok]), (gw_hi[:, k, :], gw_lo[:, k, :]))
                                          for k in range(KC)])
                last.then_inc(router_ok, 1)

            def by_token(dst, j, t):
                tok = slice(t * P, (t + 1) * P)
                return split_product(dst, [((xh[:, k, tok], xl[:, k, tok]), (att_hi[:, j, k, :], att_lo[:, j, k, :]))
                                           for k in range(KC)])

            def project(b, j):
                pe.wait_ge(mixl_ok, 3 * (b + 2) + j + 1)
                if isinstance(b, int) and b in (-1, 0):
                    pe.wait_ge((kS_ok, vS_ok, ra_ok)[j], b + 2)
                if isinstance(b, int) and b == -2:
                    pe.wait_ge(*((k_lo_ok, 1) if j == 0 else (vr_lo_ok, j)))
                for d in range(KC):
                    cols = slice(d * P, (d + 1) * P)
                    last = split_product(Q[:, j, d * T:(d + 1) * T],
                                         [((kvr_hi[:, j, k, cols], kvr_lo[:, j, k, cols]),
                                           (mix[:, 0, j % 2, k, :], mix[:, 1, j % 2, k, :])) for k in range(KC)])
                last.then_inc((kp1_ok, vp1_ok, kvr_ok)[j], 1)

            def ternary(b, f):
                if f == 0:
                    pe.wait_ge(x3h_ok, b)
                    pe.wait_ge(x3l_ok, b)
                    if isinstance(b, int) and b == 1:
                        pe.wait_ge(w12q_ok, 2)
                if f < 3:
                    if not isinstance(b, int) or b + 2 < B:
                        pe.wait_ge(kS_ok, b + 3)
                        pe.wait_ge(vS_ok, b + 3)
                        pe.wait_ge(ra_ok, b + 3)
                else:
                    pe.wait_ge(fx_ok, NF * (b - 1) + f - 2)
                cols = slice(f * P, (f + 1) * P)
                for i, w in enumerate((w1q, w2q)):
                    last = f32_product(Q[:, f % 3, i * T:(i + 1) * T],
                                       [(w[:, k, cols], xx[:, k, :]) for k in range(KC) for xx in (xh, xl)])
                last.then_inc(f12_ok, 1)

            def ternary_out(b, f):
                pe.wait_ge(fl_ok, NF * (b - 1) + f + 1)
                if f == 0 and (not isinstance(b, int) or b + 1 < B):
                    pe.wait_ge(r_ok[0], b + 2)
                if f == 0 and isinstance(b, int) and b == 1:
                    pe.wait_ge(w3q_ok, 1)
                for t in range(NT):
                    tok = slice(t * P, (t + 1) * P)
                    for i, l in enumerate((fh, fl)):
                        last = pe.matmul(O[:, t, :], l[:, f % SDEPTH, tok], w3q[:, f, :],
                                         start=f == 0 and t == 0 and i == 0, stop=f == NF - 1 and i == 1,
                                         skip_group_check=True)
                last.then_inc(w3_ok, 1)

            def slot(b, experts, attn, rwkv, proj):
                first = isinstance(b, int) and b == 0
                after_output = isinstance(b, int) and b == -1
                if not experts and attn:
                    pe.wait_ge(hu_ok, NCH * B)
                    keep_clock(WARM[3])
                if experts:
                    if first:
                        for s in (gate_hi_ok, gate_lo_ok, up_hi_ok, up_lo_ok):
                            pe.wait_ge(s, 1)
                    gate_up(b, 0)
                    gate_up(b, 1)
                    if first:
                        pe.wait_ge(gw_lo_ok, 1)
                    past(pe, r_ok[3], b - 1)
                    router(b)
                if attn:
                    pe.wait_ge(x_ok[1], b)
                    transposes(x2, Tb).then_inc(x2Tp_ok, 1)
                if experts:
                    gate_up(b, 2)
                if attn and not experts:
                    keep_clock(WARM[4])
                if attn:
                    pe.wait_ge(x2h_ok, b)
                    pe.wait_ge(x2l_ok, b)
                    if isinstance(b, int) and b == 1:
                        pe.wait_ge(att_hi_ok, 1)
                        pe.wait_ge(att_lo_ok, 1)
                    past(pe, fx_ok, NF * (b - 1))
                    for j, s in ((1, k_ok), (2, v_ok)):
                        for t in range(NT):
                            last = by_token(Q[:, j, t * C:(t + 1) * C], j, t)
                        last.then_inc(s, 1)
                    for d in range(KC):
                        cols = slice(d * P, (d + 1) * P)
                        last = split_product(Q[:, 0, d * T:(d + 1) * T],
                                             [((att_hi[:, 0, k, cols], att_lo[:, 0, k, cols]),
                                               (xh[:, k, :], xl[:, k, :])) for k in range(KC)])
                    last.then_inc(q_ok, 1)
                if first:
                    project(b - 1, 1)
                    project(b - 1, 2)
                if experts:
                    pe.wait_ge(twt_ok, b + 1)
                    for t in range(NT):
                        last = pe.transpose(Tb[:, 0, t * P:(t + 1) * P], twt[:, t, :], ident)
                    last.then_inc(twp_ok, 1)
                    gate_up(b, 3)
                if not experts:
                    keep_clock(WARM[5])
                if attn:
                    pe.wait_ge(kp_ok, b)
                    pe.wait_ge(vx_ok, b)
                    if experts:
                        pe.wait_ge(lg_ok, b + 1)
                    else:
                        pe.wait_ge(r_ok[3], b - 1)
                    for d in range(KC):
                        last = f32_product(O[:, d, 0:KVW], [(ke[:, t, d * P:(d + 1) * P], vx[:, t, d * P:d * P + KVW])
                                                            for t in range(NT)])
                    last.then_inc(kvp_ok, 1)
                if experts:
                    gate_up(b, 4)
                    down(b, 0)
                if attn:
                    pe.wait_ge(kvm_ok, b)
                    pe.wait_ge(qp_ok, b)
                    for t in range(NT):
                        for d in range(KC):
                            last = pe.matmul(Q[:, 1 + t, d * KVW:(d + 1) * KVW], qS[:, d, t * P:(t + 1) * P],
                                             kvm[:, d, :], start=True, stop=True)
                    last.then_inc(at_ok, 1)
                if experts:
                    gate_up(b, 5)
                    down(b, 1)
                if attn:
                    if not experts:
                        keep_clock(WARM[6])
                    pe.wait_ge(an_ok, b)
                    if experts:
                        pe.wait_ge(tw_ok, b + 1)
                    transposes(an, Tb).then_inc(anTp_ok, 1)
                if experts:
                    down(b, 2)
                if proj and not after_output:
                    project(b, 0)
                if attn:
                    if not experts:
                        keep_clock(WARM[7])
                    pe.wait_ge(anh_ok, b)
                    pe.wait_ge(anl_ok, b)
                    for t in range(NT):
                        last = by_token(O[:, t, :], 3, t)
                    last.then_inc(o3_ok, 1)
                if experts:
                    gate_up(b, 6)
                    down(b, 3)
                if proj and not after_output:
                    project(b, 1)
                if experts:
                    gate_up(b, 7)
                    down(b, 4)
                if proj and not after_output:
                    project(b, 2)
                if first:
                    pe.wait_ge(wsum_ok, 3)
                    pe.wait_ge(lg_ok, 1)
                    pe.matmul(O[:, 0, 0:3], ones[:, :], wsum[:, :], start=True, stop=True).then_inc(gamma_ok, 1)
                if rwkv:
                    if not (experts or attn):
                        keep_clock(WARM[1])
                    pe.wait_ge(y_ok, b + 2)
                    if isinstance(b, int) and b == -1:
                        pe.wait_ge(in_wo1, 16)
                    if attn:
                        pe.wait_ge(r_ok[2], b)
                    elif first:
                        pe.wait_ge(thr_ok, 1)
                    for t in range(NT):
                        last = f32_product(O[:, t, :],
                                           [(y[:, k, t * P:(t + 1) * P], wo1[:, k, :]) for k in range(KC)])
                    last.then_inc(o1_ok, 1)
                if after_output:
                    project(b, 0)
                if experts:
                    gate_up(b, 8)
                    down(b, 5)
                if attn and not experts:
                    keep_clock(WARM[8])
                if attn:
                    pe.wait_ge(x_ok[2], b)
                    transposes(x3, Tb).then_inc(x3Tp_ok, 1)
                if experts:
                    gate_up(b, 9)
                    down(b, 6)
                if attn and not experts:
                    keep_clock(WARM[9])
                if attn:
                    ternary(b, 0)
                    ternary(b, 1)
                if experts:
                    gate_up(b, 10)
                if attn:
                    ternary(b, 2)
                    ternary_out(b, 0)
                if experts:
                    down(b, 7)
                if rwkv:
                    if not (experts or attn):
                        keep_clock(WARM[2])
                    pe.wait_ge(x_ok[0], b + 2)
                    if attn:
                        pe.wait_ge(x3l_ok, b)
                    elif experts:
                        pe.wait_ge(tw_ok, b + 1)
                    if isinstance(b, int) and b == -1:
                        pe.wait_ge(in_cst, 16)
                    transposes(x1, Tb).then_inc(x1Tp_ok, 1)
                if attn:
                    ternary(b, 3)
                    ternary_out(b, 1)
                    ternary(b, 4)
                if experts:
                    down(b, 8)
                if attn:
                    ternary_out(b, 2)
                    ternary(b, 5)
                if experts:
                    down(b, 9)
                if attn:
                    ternary_out(b, 3)
                if experts:
                    down(b, 10)
                if attn:
                    ternary_out(b, 4)
                    ternary_out(b, 5)

            pe.wait_ge(preset, 3)
            keep_clock(WARM[0])
            slots(pe, slot)

        @block.scalar
        def _(act):
            def copy(dst, src):
                return act.activation(dst, src, ACT.Copy)

            def silu(b, c):
                act.wait_ge(gu_ok, NCH * b + c + 1)
                past(act, hl_ok, NCH * b + c + 1 - rotating(c, HDEPTH))
                act.activation(hb[:, c % HDEPTH, :], G[:, c % 2, 0, :], ACT.Silu).then_inc(silu_ok, 1)

            def h_high(b, c):
                act.wait_ge(h_ok, NCH * b + c + 1)
                past(act, down_ok, NCH * b + c + 1 - rotating(c, SDEPTH))
                copy(hh[:, c % SDEPTH, :], hb[:, c % HDEPTH, :]).then_inc(hh_ok, 1)

            def keys(b, rwkv):
                act.wait_ge(kp1_ok, b + 3)
                if rwkv:
                    act.wait_ge(t1_ok, b + 2)
                copy(kS, Q[:, 0, :].rearrange("p (k t) -> p k t", k=KC)).then_inc(kS_ok, 1)

            def mix_high(b, j):
                n = 3 * (b + 2) + j + 1
                act.wait_ge(mixf_ok, n)
                if j == 2:
                    act.wait_ge(kp1_ok, b + 3)
                copy(mix[:, 0, j % 2, :, :], mix_full[j]).then_inc(mixh_ok, 1)

            def values(b):
                act.wait_ge(vp1_ok, b + 3)
                past(act, v2_ok[0], b + 2)
                past(act, v2_ok[1], b + 2)
                copy(vS[:, :, :], Q[:, 1, :].rearrange("p (k t) -> p k t", k=KC)).then_inc(vS_ok, 1)

            def gates(b):
                act.wait_ge(kvr_ok, b + 3)
                r = Q[:, 2, :].rearrange("p (k t) -> p k t", k=KC)
                act.activation(ra[:, :, :], r, ACT.Abs)
                act.activation(rn[:, :, :], r, ACT.Relu, scale=-1.0).then_inc(ra_ok, 1)

            def exponentials(b):
                act.wait_ge(ar_ok, b + 2)
                act.activation(AR[:, :, :, :], AR[:, :, :, :], ACT.Exp).then_inc(exps_ok, 1)

            def gate_exponential(b):
                act.wait_ge(ra_ok, b + 2)
                act.activation(ra[:, :, :], ra[:, :, :], ACT.Exp, scale=-1.0).then_inc(ea_ok, 1)

            def tanh_half(b, f):
                act.wait_ge(f12_ok, NF * (b - 1) + f + 1)
                past(act, fl_ok, NF * (b - 1) + f + 1 - SDEPTH)
                act.activation(fb[:, f % SDEPTH, :], Q[:, f % 3, 0:T], ACT.Tanh, scale=0.5).then_inc(th_ok, 1)

            def f_high(b, f):
                act.wait_ge(fx_ok, NF * (b - 1) + f + 1)
                past(act, w3_ok, NF * (b - 1) + f + 1 - SDEPTH)
                copy(fh[:, f % SDEPTH, :], fb[:, f % SDEPTH, :]).then_inc(fh_ok, 1)

            def slot(b, experts, attn, rwkv, proj):
                first = isinstance(b, int) and b == 0
                if experts:
                    act.wait_ge(x_ok[0], b + 1)
                    past(act, r_ok[1], b)
                    copy(x1k[:, :, :], x1[:, :, :]).then_inc(x1k_ok, 1)
                    silu(b, 0)
                    silu(b, 1)
                if attn:
                    act.wait_ge(x2Tp_ok, b)
                    copy(xh[:, :, :], Tb[:, :, :]).then_inc(x2h_ok, 1)
                if experts:
                    act.wait_ge(gap_ok, b + 1)
                    act.activation(gap[:, :], gap[:, :], ACT.Tanh, scale=0.5).then_inc(tanh_ok, 1)
                    silu(b, 2)
                if rwkv and not first:
                    exponentials(b)
                if isinstance(b, int) and b == -1:
                    values(b - 1)
                    act.wait_ge(in_up, 16)
                    copy(flat(up_hi), stage[1]).then_inc(up_hi_ok, 1)
                    gates(b - 1)
                    gate_exponential(b)
                if attn:
                    act.wait_ge(kc_ok, b)
                    act.activation(ke, ke, ACT.Exp).then_inc(ke_ok, 1)
                if experts:
                    act.wait_ge(twp_ok, b + 1)
                    copy(TW[:, :], Tb[:, 0, :]).then_inc(tw_ok, 1)
                if rwkv and not (isinstance(b, int) and b < 1):
                    gate_exponential(b)
                if attn:
                    act.wait_ge(qt_ok, b)
                    act.activation(qS, qS, ACT.Exp).then_inc(qe_ok, 1)
                if experts:
                    h_high(b, 0)
                    h_high(b, 1)
                    silu(b, 3)
                if first:
                    silu(b, 4)
                    h_high(b, 2)
                    exponentials(b)
                    values(b - 1)
                    gates(b - 1)
                    gate_exponential(b)
                if proj and not (isinstance(b, int) and b < 1):
                    mix_high(b, 0)
                if experts:
                    if not first:
                        silu(b, 4)
                        h_high(b, 2)
                    h_high(b, 3)
                if attn:
                    act.wait_ge(anTp_ok, b)
                    copy(xh[:, :, :], Tb[:, :, :]).then_inc(anh_ok, 1)
                if proj and not (isinstance(b, int) and b < 0):
                    mix_high(b, 1)
                if experts:
                    silu(b, 5)
                    h_high(b, 4)
                if rwkv:
                    act.preload_act_table_set("natural_log_exp_and_others")
                    act.wait_ge(qq_ok, b + 2)
                    act.activation(AR[:, 2, :, :], AR[:, 2, :, :], ACT.Ln).then_inc(ln_ok, 1)
                if proj and not (isinstance(b, int) and b < 0):
                    mix_high(b, 2)
                if rwkv:
                    act.wait_ge(arg_ok, b + 2)
                    act.activation(AR[:, 3, :, :], AR[:, 3, :, :], ACT.Exp, scale=-1.0).then_inc(sr_ok, 1)
                if experts:
                    silu(b, 6)
                    h_high(b, 5)
                if proj and not (isinstance(b, int) and b == -1):
                    keys(b, rwkv)
                    if not (isinstance(b, int) and b < 0):
                        values(b)
                if isinstance(b, int) and b == -2:
                    act.wait_ge(in_gate, 16)
                    copy(flat(gate_hi), stage[0]).then_inc(gate_hi_ok, 1)
                if isinstance(b, int) and b == -1:
                    act.wait_ge(in_down, 16)
                    copy(flat(down_hi), stage[0]).then_inc(down_hi_ok, 1)
                if experts:
                    silu(b, 7)
                    h_high(b, 6)
                if proj and not (isinstance(b, int) and b < 0):
                    gates(b)
                if experts:
                    silu(b, 8)
                    h_high(b, 7)
                if attn:
                    act.wait_ge(x3Tp_ok, b)
                    copy(xh[:, :, :], Tb[:, :, :]).then_inc(x3h_ok, 1)
                if experts:
                    silu(b, 9)
                    h_high(b, 8)
                if attn:
                    tanh_half(b, 0)
                    tanh_half(b, 1)
                    f_high(b, 0)
                if experts:
                    silu(b, 10)
                    h_high(b, 9)
                if attn:
                    f_high(b, 1)
                    tanh_half(b, 2)
                if rwkv:
                    act.wait_ge(x1Tp_ok, b + 2)
                    copy(x1h[:, :, :], Tb[:, :, :]).then_inc(x1h_ok, 1)
                if isinstance(b, int) and b == -1:
                    keys(b, True)
                    act.wait_ge(in_att, 64)
                    copy(att_hi[:, :, :, :], raw_att).then_inc(att_hi_ok, 1)
                if attn:
                    f_high(b, 2)
                    tanh_half(b, 3)
                if experts:
                    h_high(b, 10)
                if attn:
                    f_high(b, 3)
                    tanh_half(b, 4)
                    f_high(b, 4)
                    tanh_half(b, 5)
                    f_high(b, 5)

            act.wait_ge(in_vec, 16)
            act.activation(wdec[:, :], vec[:, :, TD_COL], ACT.Exp).then_inc(decay_e, 1)
            for j in range(3):
                act.wait_ge(in_kvr[j], 16)
                copy(kvr_hi[:, j, :, :], raw_kvr[:, j, :, :]).then_inc(kvr_hi_ok, 1)
            slots(act, slot)

        @block.vector
        def _(dve):
            def add_residual(i, psum, res, dst, value):
                dve.tensor_tensor(dst, psum, res, ALU.add).then_inc(r_ok[i], 1)
                dve.wait_ge(r_ok[i], value)
                for t in range(NT):
                    last = dve.bn_stats(st[:, i, t, :], dst[:, t, :])
                last.then_inc(st_ok[i], 1)
                dve.wait_ge(preset, 4)
                dve.wait_ge(st_ok[i], value)
                for t in range(NT):
                    last = dve.bn_aggr(mv[:, i, t, :], st[:, i, t, :])
                last.then_inc(mv_ok[i], 1)

            def normalise(i, src, dst, value):
                dve.wait_ge(rs_ok[i], value)
                dve.wait_ge(mv_ok[i], value)
                for t in range(NT):
                    last = dve.tensor_scalar(dst[:, t, :], src[:, t, :], mv[:, i, t, 0:1], rs[:, i, t:t + 1],
                                             ALU.subtract, ALU.mult)
                last.then_inc(x_ok[i], 1)

            def low_transposed(hi_ok, lo_ok, value):
                dve.wait_ge(hi_ok, value)
                dve.tensor_tensor(xl[:, :, :], Tb[:, :, :], xh[:, :, :].bitcast(F32), ALU.subtract).then_inc(lo_ok, 1)

            def maxima(b):
                dve.wait_ge(mixl_ok, 3 * (b + 2) + 2)
                dve.wait_ge(kS_ok, b + 3)
                for k in range(KC):
                    last = dve.tensor_tensor_scan(M[:, k, 1:], wdec[:, k:k + 1].broadcast_to([P, T]), kS[:, k, :],
                                                  LOW, ALU.add, ALU.max)
                last.then_inc(M_ok, 1)

            def divided(b):
                dve.wait_ge(at_ok, b)
                dve.tensor_scalar(zr[:, :, :], Q[:, 1:3, P:P + NH], Z_EPS, None, ALU.add).then_inc(ze_ok, 1)
                dve.wait_ge(ze_ok, b)
                dve.reciprocal(zr[:, :, :], zr[:, :, :]).then_inc(zr_ok, 1)
                dve.wait_ge(zr_ok, b)
                for t in range(NT):
                    src = Q[:, 1 + t, 0:KC * (P + NH)].rearrange("p (k c) -> p k c", k=KC)[:, :, 0:P].rearrange(
                        "p k (h e) -> p k h e", e=HEAD)
                    last = dve.tensor_tensor(
                        an[:, t, :].rearrange("p (k h e) -> p k h e", k=KC, e=HEAD), src,
                        zr[:, t, :].rearrange("p (k h) -> p k h", k=KC).unsqueeze(3).broadcast_to(
                            [P, KC, HK, HEAD]), ALU.mult)
                last.then_inc(an_ok, 1)

            def exponents(b, part):
                if part == 0:
                    dve.wait_ge(M_ok, b + 3)
                if part < KC:
                    k = part
                    dve.scalar_tensor_tensor(AR[:, 2, k, :], kS[:, k, :], vec[:, k, U_COL:U_COL + 1],
                                             M[:, k, 0:T], ALU.add, ALU.subtract)
                    last = dve.scalar_tensor_tensor(AR[:, 0, k, :], M[:, k, 0:T], wdec[:, k:k + 1],
                                                    M[:, k, 1:], ALU.add, ALU.subtract)
                    if part == KC - 1:
                        last.then_inc(lag_ok, 1)
                        dve.tensor_tensor(AR[:, 1, :, :], kS[:, :, :], M[:, :, 1:], ALU.subtract)
                else:
                    dve.wait_ge(lag_ok, b + 3)
                    dve.tensor_scalar(AR[:, 3, :, :], AR[:, 2, :, :], 0.0, None, ALU.min)
                    dve.tensor_scalar(AR[:, 2, :, :], AR[:, 2, :, :], 0.0, -1.0, ALU.max, ALU.mult)\
                       .then_inc(ar_ok, 1)

            def mixed(b, j):
                full = mix_full[j]
                n = 3 * (b + 2) + j + 1
                if j == 0:
                    dve.wait_ge(dx_ok, b + 3)
                    past(dve, kvr_ok, b + 2)
                    past(dve, ar_ok, b + 2)
                elif j == 1:
                    dve.wait_ge(mixl_ok, n - 1)
                else:
                    dve.wait_ge(mixf_ok, n - 1)
                for k in range(KC):
                    last = dve.scalar_tensor_tensor(full[:, k, :], dx[:, k, :], vec[:, k, MIX + j:MIX + j + 1],
                                                    xs[:, k, 0:T], ALU.mult, ALU.add)
                last.then_inc(mixf_ok, 1)
                if isinstance(b, int) and 3 * b + j < 1:
                    if j == 2:
                        dve.wait_ge(kp1_ok, b + 3)
                    dve.wait_ge(mixf_ok, n)
                    dve.tensor_copy(mix[:, 0, j % 2, :, :], full).then_inc(mixh_ok, 1)
                    dve.wait_ge(mixh_ok, n)
                    mix_low(dve, j)

            def gate_times_up(b, c):
                dve.wait_ge(silu_ok, NCH * b + c + 1)
                h = hb[:, c % HDEPTH, :]
                dve.tensor_tensor(h, h, G[:, c % 2, 1, :], ALU.mult).then_inc(hu_ok, 1)

            def ternary_gate(b, f):
                dve.wait_ge(th_ok, NF * (b - 1) + f + 1)
                h = fb[:, f % SDEPTH, :]
                dve.scalar_tensor_tensor(h, h, 1.0, Q[:, f % 3, T:2 * T], ALU.add, ALU.mult).then_inc(fx_ok, 1)

            def low_part(raw, hi, lo):
                return dve.tensor_tensor(lo, raw, hi.bitcast(F32), ALU.subtract)

            def quantise_sum(j):
                if j == 2:
                    dve.wait_ge(down_lo_ok, 1)
                    dve.memset(stage[0][HID % P:, (NF - 1) * C:NF * C], 0.0).then_inc(pads_ok, 1)
                    dve.wait_ge(in_w3, 32)
                    dve.wait_ge(pads_ok, 1)
                else:
                    dve.wait_ge(in_w12, 32)
                dve.tensor_reduce(wsum[:, j:j + 1], raw3 if j == 2 else raw12[:, j, :, :], mybir.AxisListType.XY,
                                  ALU.add, apply_absolute_value=True).then_inc(wsum_ok, 1)

            flat_ar = AR[:, :, :, :].rearrange("p a b c -> p (a b c)")

            def quantise_thresholds():
                dve.wait_ge(gamma_ok, 1)
                for i, s in enumerate((0.5, -0.5)):
                    last = dve.tensor_scalar(thr[:, i, :], O[:, 0, 0:3], s / (C * HID), s * GAMMA_EPS, ALU.mult,
                                             ALU.add)
                last.then_inc(thr_ok, 1)
                dve.wait_ge(thr_ok, 1)

            def quantise(j, step):
                tmp = flat_ar[:, 0:KC * HID].rearrange("p (k n) -> p k n", k=KC)
                w = (w1q, w2q)[j]
                if step == 0:
                    if j:
                        dve.wait_ge(w12q_ok, 1)
                    dve.tensor_scalar(tmp, raw12[:, j, :, :], thr[:, 1, j:j + 1], None, ALU.is_lt).then_inc(w12a_ok, 1)
                else:
                    dve.wait_ge(w12a_ok, j + 1)
                    dve.scalar_tensor_tensor(w[:, :, 0:HID], raw12[:, j, :, :], thr[:, 0, j:j + 1], tmp,
                                             ALU.is_gt, ALU.subtract).then_inc(w12q_ok, 1)

            def quantise_out(step):
                below = flat_ar[:, 0:NF * C].rearrange("p (k c) -> p k c", k=NF)
                if step == 0:
                    dve.wait_ge(w12q_ok, 2)
                    dve.tensor_scalar(below, raw3, thr[:, 1, 2:3], 0.5, ALU.is_lt, ALU.mult).then_inc(w3a_ok, 1)
                elif step == 1:
                    dve.wait_ge(w3a_ok, 1)
                    dve.tensor_scalar(raw3, raw3, thr[:, 0, 2:3], 0.5, ALU.is_gt, ALU.mult).then_inc(w3a_ok, 1)
                else:
                    dve.wait_ge(w3a_ok, 2)
                    dve.tensor_tensor(w3q[:, :, :], raw3, below, ALU.subtract).then_inc(w3q_ok, 1)
                    dve.wait_ge(w3q_ok, 1)

            def slot(b, experts, attn, rwkv, proj):
                first = isinstance(b, int) and b == 0
                unsettled = isinstance(b, int) and b in (-1, 0)
                if experts:
                    gate_times_up(b, 0)
                if attn and not (isinstance(b, int) and b == 1):
                    normalise(3, x4, x4, b - 1)
                if experts:
                    gate_times_up(b, 1)
                if attn:
                    low_transposed(x2h_ok, x2l_ok, b)
                if experts:
                    dve.wait_ge(router_ok, b + 1)
                    dve.tensor_copy(lg[:, :, :], O[:, 0, 0:NT * E].rearrange("p (t e) -> p t e", t=NT))\
                       .then_inc(lg_ok, 1)
                    dve.wait_ge(preset, 4)
                    dve.wait_ge(lg_ok, b + 1)
                    for t in range(NT):
                        last = dve.max(mx8[:, t, :], lg[:, t, :])
                    last.then_inc(mx_ok, 1)
                    dve.wait_ge(mx_ok, b + 1)
                    past(dve, top_ok, b)
                    dve.tensor_tensor(gap[:, :], mx8[:, :, 1], mx8[:, :, 0], ALU.subtract).then_inc(gap_ok, 1)
                    for t in range(NT):
                        last = dve.max_index(ix8[:, t, :], mx8[:, t, :], lg[:, t, :])
                    last.then_inc(ix_ok, 1)
                    dve.wait_ge(ix_ok, b + 1)
                    dve.tensor_copy(sel[:, :, :], ix8[:, :, 0:2]).then_inc(sel_ok, 1)
                    if first:
                        dve.wait_ge(in_cst, 16)
                    dve.wait_ge(tanh_ok, b + 1)
                    for i, s in enumerate((-0.5, 0.5)):
                        last = dve.tensor_scalar(top[:, i, :], gap[:, :], s, 0.5, ALU.mult, ALU.add)
                    last.then_inc(top_ok, 1)
                    dve.wait_ge(top_ok, b + 1)
                    dve.wait_ge(sel_ok, b + 1)
                    past(dve, twp_ok, b)
                    for t in range(NT):
                        dve.tensor_scalar(twt[:, t, :], expert_of, sel[:, t, 0:1], top[:, 0, t:t + 1],
                                          ALU.is_equal, ALU.mult)
                        last = dve.tensor_scalar(twb[:, t, :], expert_of, sel[:, t, 1:2], top[:, 1, t:t + 1],
                                                 ALU.is_equal, ALU.mult)
                    last.then_inc(twab_ok, 1)
                    dve.wait_ge(twab_ok, b + 1)
                    dve.tensor_tensor(twt[:, :, :], twt[:, :, :], twb[:, :, :], ALU.add).then_inc(twt_ok, 1)
                    gate_times_up(b, 2)
                if first:
                    maxima(b - 1)
                    for part in range(KC + 1):
                        exponents(b - 1, part)
                    gate_times_up(b, 3)
                if attn:
                    if isinstance(b, int) and b == 1:
                        dve.wait_ge(in_msk, 32)
                        dve.wait_ge(in_bias, 32)
                    dve.wait_ge(k_ok, b)
                    past(dve, out_x4, 16 * (b - 1))
                    dve.tensor_tensor(kt, Q[:, 1, :].rearrange("p (t c) -> p t c", t=NT),
                                      bias[:, 0:1, :].broadcast_to([P, NT, C]), ALU.add).then_inc(kt_ok, 1)
                    dve.wait_ge(kt_ok, b)
                    dve.tensor_scalar(ke, kt, 0.0, None, ALU.min).then_inc(kc_ok, 1)
                    dve.wait_ge(v_ok, b)
                    v = Q[:, 2, :].rearrange("p (t c) -> p t c", t=NT)
                    for k in range(KC):
                        last = dve.tensor_tensor(vx[:, :, k * KVW:k * KVW + P], v[:, :, k * P:(k + 1) * P],
                                                 bias[:, 1:2, k * P:(k + 1) * P].broadcast_to([P, NT, P]), ALU.add)
                    last.then_inc(vx_ok, 1)
                    dve.wait_ge(ke_ok, b)
                    dve.scalar_tensor_tensor(ke, kt, 1.0, ke, ALU.add, ALU.max).then_inc(kp_ok, 1)
                    dve.wait_ge(q_ok, b)
                    for k in range(KC):
                        last = dve.tensor_scalar(qS[:, k, :], Q[:, 0, k * T:(k + 1) * T], vec[:, k, QB_COL:QB_COL + 1],
                                                 0.0, ALU.add, ALU.min)
                    last.then_inc(qt_ok, 1)
                if isinstance(b, int) and b == -2:
                    mixed(b, 0)
                    mixed(b, 1)
                elif proj and not (isinstance(b, int) and b < 0):
                    mixed(b, 0)
                if first:
                    gate_times_up(b, 4)
                    dve.wait_ge(att_hi_ok, 1)
                    low_part(raw_att, att_hi[:, :, :, :], att_lo[:, :, :, :]).then_inc(att_lo_ok, 1)
                    quantise_sum(2)
                if attn:
                    dve.wait_ge(qe_ok, b)
                    for k in range(KC):
                        last = dve.scalar_tensor_tensor(qS[:, k, :], Q[:, 0, k * T:(k + 1) * T], qb1[:, k:k + 1],
                                                        qS[:, k, :], ALU.add, ALU.max)
                    last.then_inc(qp_ok, 1)
                if attn:
                    dve.wait_ge(kvp_ok, b)
                    dve.tensor_tensor(kvm, O[:, :, 0:KVW], msk[:, :, :], ALU.mult).then_inc(kvm_ok, 1)
                if experts and not first:
                    gate_times_up(b, 3)
                if attn:
                    divided(b)
                if proj and not (isinstance(b, int) and b < 0):
                    mixed(b, 1)
                if rwkv:
                    dve.wait_ge(exps_ok, b + 2)
                    for k in range(KC):
                        dve.tensor_tensor_scan(ND[:, 1, k, 1:], AR[:, 0, k, :], AR[:, 1, k, :], 0.0, ALU.mult,
                                               ALU.add)
                    if isinstance(b, int) and b == -1:
                        dve.wait_ge(vS_ok, 1)
                        value_product(dve, 0)
                        value_product(dve, 1)
                    dve.wait_ge(v2_ok[0], b + 2)
                    for k in range(KC):
                        last = dve.tensor_tensor_scan(ND[:, 0, k, 1:], AR[:, 0, k, :], V2[:, 0, k, :], 0.0,
                                                      ALU.mult, ALU.add)
                    last.then_inc(nd_ok, 1)
                if experts and not first:
                    gate_times_up(b, 4)
                if attn:
                    low_transposed(anh_ok, anl_ok, b)
                if rwkv:
                    dve.wait_ge(nd_ok, b + 2)
                    for i in range(2):
                        last = dve.tensor_tensor(AR[:, i, :, :], ND[:, i, :, 0:T], AR[:, 2, :, :], ALU.mult)
                    last.then_inc(t1_ok, 1)
                    dve.wait_ge(t1_ok, b + 2)
                    dve.wait_ge(v2_ok[1], b + 2)
                    dve.tensor_tensor(V2[:, 0, :, :], AR[:, 0, :, :], V2[:, 1, :, :], ALU.add)
                    dve.tensor_tensor(AR[:, 1, :, :], AR[:, 1, :, :], AR[:, 3, :, :], ALU.add).then_inc(nd2_ok, 1)
                    dve.wait_ge(nd2_ok, b + 2)
                    dve.wait_ge(ea_ok, b + 2)
                    dve.scalar_tensor_tensor(AR[:, 2, :, :], ra[:, :, :], 1.0, AR[:, 1, :, :], ALU.add,
                                             ALU.mult).then_inc(qq_ok, 1)
                if first:
                    quantise_sum(0)
                if experts:
                    gate_times_up(b, 5)
                if proj and not (isinstance(b, int) and b < 0):
                    mixed(b, 2)
                if rwkv:
                    dve.wait_ge(ln_ok, b + 2)
                    dve.tensor_tensor(AR[:, 3, :, :], rn[:, :, :], AR[:, 2, :, :], ALU.add).then_inc(arg_ok, 1)
                if attn:
                    dve.wait_ge(o3_ok, b)
                    dve.wait_ge(x2b_ok, b)
                    add_residual(2, O[:, :, :], x2, x3, b)
                if first:
                    quantise_sum(1)
                if experts:
                    gate_times_up(b, 6)
                if rwkv:
                    dve.wait_ge(sr_ok, b + 2)
                    dve.tensor_tensor(y, V2[:, 0, :, :], AR[:, 3, :, :], ALU.mult).then_inc(y_ok, 1)
                if isinstance(b, int) and b == -1:
                    mixed(b, 0)
                if first:
                    quantise_thresholds()
                    quantise(0, 0)
                if experts:
                    gate_times_up(b, 7)
                if first:
                    quantise(0, 1)
                if attn:
                    normalise(2, x3, x3, b)
                if rwkv:
                    dve.wait_ge(o1_ok, b + 2)
                    dve.wait_ge(in_x, 16 * (b + 2))
                    add_residual(0, O[:, :, :], x1[:, :, :], x1[:, :, :], b + 2)
                if experts:
                    gate_times_up(b, 8)
                if proj and not attn and not (isinstance(b, int) and b < 0):
                    maxima(b)
                if rwkv:
                    normalise(0, x1, x1, b + 2)
                if isinstance(b, int) and b == -2:
                    maxima(b)
                if first:
                    quantise(1, 0)
                if attn:
                    low_transposed(x3h_ok, x3l_ok, b)
                if experts:
                    gate_times_up(b, 9)
                if first:
                    quantise(1, 1)
                    quantise_out(0)
                if attn:
                    if proj:
                        maxima(b)
                    ternary_gate(b, 0)
                if proj and not unsettled:
                    exponents(b, 0)
                if attn:
                    ternary_gate(b, 1)
                if experts:
                    gate_times_up(b, 10)
                if first:
                    quantise_out(1)
                if proj and not unsettled:
                    exponents(b, 1)
                if attn:
                    ternary_gate(b, 2)
                if rwkv:
                    dve.wait_ge(x1h_ok, b + 2)
                    dve.tensor_tensor(x1l[:, :, :], Tb[:, :, :], x1h[:, :, :].bitcast(F32), ALU.subtract)\
                       .then_inc(x1l_ok, 1)
                if isinstance(b, int) and b == -1:
                    dve.wait_ge(in_gw, 16)
                    dve.tensor_copy(gw_hi[:, :, :], gw[:, :, :]).then_inc(gw_hi_ok, 1)
                    dve.wait_ge(gw_hi_ok, 1)
                    low_part(gw[:, :, :], gw_hi[:, :, :], gw_lo[:, :, :]).then_inc(gw_lo_ok, 1)
                    mixed(b, 1)
                    mixed(b, 2)
                if first:
                    quantise_out(2)
                if attn:
                    ternary_gate(b, 3)
                if proj and not unsettled:
                    exponents(b, 2)
                if isinstance(b, int) and b == -2:
                    mixed(b, 2)
                if attn:
                    ternary_gate(b, 4)
                    ternary_gate(b, 5)
                if experts:
                    dve.wait_ge(down_ok, NCH * (b + 1))
                    dve.wait_ge(x1k_ok, b + 1)
                    if attn:
                        dve.wait_ge(r_ok[2], b)
                    add_residual(1, D[:, :, :], x1k[:, :, :], x2, b + 1)
                if attn:
                    dve.wait_ge(w3_ok, NF * b)
                    past(dve, out_x4, 16 * (b - 1))
                    add_residual(3, O[:, :, :], x3, x4[:, :, :], b)
                if experts:
                    if first:
                        dve.memset(vx[:, :, P:KVW], 1.0)
                        exponents(b, 0)
                    normalise(1, x2, x2, b + 1)
                    if first:
                        exponents(b, 1)
                        exponents(b, 2)
                if attn and not experts:
                    normalise(3, x4, x4, b)

            dve.memset(xs[:, :, 0:1], 0.0).then_inc(preset, 1)
            dve.memset(M[:, :, 0:1], LOW)
            dve.memset(ND[:, :, :, 0:1], 0.0).then_inc(preset, 1)
            dve.memset(ones[:, :], 1.0).then_inc(preset, 1)
            dve.memset(w1q[:, :, HID:].bitcast(F32), 0.0)
            dve.memset(w2q[:, :, HID:].bitcast(F32), 0.0)
            dve.memset(eps[:, :], LN_EPS)
            dve.memset(neghalf[:, :], -0.5).then_inc(preset, 1)
            dve.wait_ge(preset, 4)
            dve.wait_ge(in_xT, 16)
            difference(dve)
            dve.wait_ge(in_vec, 16)
            dve.tensor_scalar(qb1[:, :], vec[:, :, QB_COL], 1.0, None, ALU.add)
            dve.wait_ge(decay_e, 1)
            dve.tensor_scalar(wdec[:, :], wdec[:, :], -1.0, None, ALU.mult).then_inc(wdec_ok, 1)
            dve.wait_ge(wdec_ok, 1)
            dve.wait_ge(kvr_hi_ok, 1)
            low_part(raw_kvr[:, 0, :, :], kvr_hi[:, 0, :, :], kvr_lo[:, 0, :, :]).then_inc(k_lo_ok, 1)
            slots(dve, slot)

        @block.gpsimd
        def _(pool):
            def deviation(i, value):
                pool.wait_ge(mv_ok[i], value)
                pool.tensor_tensor(ve[:, i, :], mv[:, i, :, 1], eps[:, :], ALU.add).then_inc(ve_ok[i], 1)
                pool.wait_ge(ve_ok[i], value)
                pool.tensor_tensor(rs[:, i, :], ve[:, i, :], neghalf[:, :], ALU.pow).then_inc(rs_ok[i], 1)

            def low_part(hi_ok, raw, hi, lo, lo_ok):
                pool.wait_ge(hi_ok, 1)
                pool.tensor_tensor(flat(lo), raw, flat(hi).bitcast(F32), ALU.subtract).then_inc(lo_ok, 1)

            def next_mix_low(b, j):
                pool.wait_ge(mixh_ok, 3 * (b + 2) + j + 1)
                mix_low(pool, j)

            def next_values(b):
                pool.wait_ge(exps_ok, b + 2)
                pool.wait_ge(vS_ok, b + 2)
                pool.wait_ge(o1_ok, b + 1)
                value_product(pool, 0)

            def next_difference(b):
                pool.wait_ge(in_xT, 16 * (b + 3))
                pool.wait_ge(mixl_ok, 3 * (b + 2))
                difference(pool)

            def weigh(b, c):
                pool.wait_ge(hu_ok, NCH * b + c + 1)
                if c == 0:
                    pool.wait_ge(tw_ok, b + 1)
                h = hb[:, c % HDEPTH, :]
                pool.tensor_tensor(h, h, TW[:, :], ALU.mult).then_inc(h_ok, 1)

            def h_low(b, c):
                pool.wait_ge(hh_ok, NCH * b + c + 1)
                pool.tensor_tensor(hl[:, c % SDEPTH, :], hb[:, c % HDEPTH, :], hh[:, c % SDEPTH, :].bitcast(F32),
                                   ALU.subtract).then_inc(hl_ok, 1)

            def f_low(b, f):
                pool.wait_ge(fh_ok, NF * (b - 1) + f + 1)
                pool.tensor_tensor(fl[:, f % SDEPTH, :], fb[:, f % SDEPTH, :], fh[:, f % SDEPTH, :].bitcast(F32),
                                   ALU.subtract).then_inc(fl_ok, 1)

            def slot(b, experts, attn, rwkv, proj):
                if attn:
                    pool.wait_ge(x2Tp_ok, b)
                    pool.tensor_tensor(x2, x2, bias_o[:, :].unsqueeze(1).broadcast_to([P, NT, C]), ALU.add)\
                        .then_inc(x2b_ok, 1)
                if proj and not (isinstance(b, int) and b < 0):
                    next_difference(b)
                if attn and rwkv:
                    next_values(b)
                if isinstance(b, int) and b == -1:
                    low_part(gate_hi_ok, stage[0], gate_hi, gate_lo, gate_lo_ok)
                    next_difference(b)
                    low_part(up_hi_ok, stage[1], up_hi, up_lo, up_lo_ok)
                if experts:
                    weigh(b, 0)
                    weigh(b, 1)
                    h_low(b, 0)
                    weigh(b, 2)
                    h_low(b, 1)
                if proj and not (isinstance(b, int) and b < 1):
                    next_mix_low(b, 0)
                if experts:
                    weigh(b, 3)
                    h_low(b, 2)
                if isinstance(b, int) and b == 0:
                    next_values(b)
                if rwkv and not (isinstance(b, int) and b == -1):
                    value_product(pool, 1)
                if proj and not (isinstance(b, int) and b < 0):
                    next_mix_low(b, 1)
                if experts:
                    weigh(b, 4)
                    h_low(b, 3)
                    weigh(b, 5)
                    h_low(b, 4)
                if proj and not (isinstance(b, int) and b < 0):
                    next_mix_low(b, 2)
                if experts:
                    weigh(b, 6)
                if attn:
                    deviation(2, b)
                if experts:
                    h_low(b, 5)
                    weigh(b, 7)
                if rwkv:
                    deviation(0, b + 2)
                if isinstance(b, int) and b == -1:
                    low_part(down_hi_ok, stage[0], down_hi, down_lo, down_lo_ok)
                if experts:
                    h_low(b, 6)
                    weigh(b, 8)
                    h_low(b, 7)
                    weigh(b, 9)
                if attn:
                    f_low(b, 0)
                if experts:
                    h_low(b, 8)
                    weigh(b, 10)
                if attn:
                    f_low(b, 1)
                    f_low(b, 2)
                if experts:
                    h_low(b, 9)
                if attn:
                    f_low(b, 3)
                if experts:
                    h_low(b, 10)
                if attn:
                    f_low(b, 4)
                    f_low(b, 5)
                if experts:
                    deviation(1, b + 1)
                if attn:
                    deviation(3, b)

            for j in (1, 2):
                pool.wait_ge(kvr_hi_ok, j + 1)
                pool.tensor_tensor(kvr_lo[:, j, :, :], raw_kvr[:, j, :, :], kvr_hi[:, j, :, :].bitcast(F32),
                                   ALU.subtract).then_inc(vr_lo_ok, 1)
            pool.wait_ge(preset, 4)
            slots(pool, slot)


def kernel(**inputs):
    import numpy as np
    import concourse.bacc as bacc
    from concourse.bass_utils import run_bass_kernel_spmd

    a = {k: np.asarray(v) for k, v in inputs.items()}
    f32 = np.float32

    def turned(w):
        return np.ascontiguousarray(w.T)

    def by_channel(w):
        t = w.reshape(E, NCH, FE, KC, P).transpose(4, 3, 1, 0, 2)
        return np.ascontiguousarray(t).reshape(P, KC * NCH * P)

    vec = np.stack([a["L0_attn_time_mix_k"], a["L0_attn_time_mix_v"], a["L0_attn_time_mix_r"],
                    a["L0_attn_time_first"], a["L0_attn_time_decay"], a["L1_attn_q_b"]], axis=-1)
    consts = np.zeros((P, 2, P), f32)
    consts[:, 0, :] = np.eye(P, dtype=f32)
    consts[:, 1, :] = np.repeat(np.arange(E, dtype=f32), FE)
    heads = np.arange(P) // HEAD
    share = (heads[:, None] == heads[None, :]).astype(f32)
    own = (heads[:, None] == np.arange(HK)[None, :]).astype(f32)
    mask = np.stack([np.concatenate([share, own], 1), np.concatenate([own, share], 1)], 1)
    arrays = {
        "xT": np.ascontiguousarray(a["L0_attn_x"].reshape(B * T, C).T),
        "x": a["L0_attn_x"],
        "vecs": np.ascontiguousarray(vec.reshape(KC, P, NVEC).transpose(1, 0, 2)),
        "rows": np.stack([a["L1_attn_k_b"], a["L1_attn_v_b"], a["L1_attn_o_b"]]),
        "consts": consts,
        "mask": mask,
        "Wk": turned(a["L0_attn_Wk"]), "Wv": turned(a["L0_attn_Wv"]), "Wr": turned(a["L0_attn_Wr"]),
        "Wo": turned(a["L0_attn_Wo"]),
        "gate_w": turned(a["L0_ffn_gate_w"]),
        "w_gate": by_channel(a["L0_ffn_gate_proj"]),
        "w_up": by_channel(a["L0_ffn_up_proj"]),
        "w_down": np.ascontiguousarray(
            a["L0_ffn_down_proj"].reshape(E, C, NCH, FE).transpose(0, 3, 2, 1)).reshape(P, NCH * C),
        "Wq3": turned(a["L1_attn_q_w"]), "Wk3": turned(a["L1_attn_k_w"]), "Wv3": turned(a["L1_attn_v_w"]),
        "Wo3": turned(a["L1_attn_o_w"]),
        "W1": turned(a["L1_ffn_w1"]), "W2": turned(a["L1_ffn_w2"]), "W3": turned(a["L1_ffn_w3"]),
    }
    nc = bacc.Bacc("TRN2", target_bir_lowering=False, num_devices=1)
    args = [nc.dram_tensor(f"in_{k}", v.shape, mybir.dt.from_np(v.dtype), kind="ExternalInput").ap()
            for k, v in arrays.items()]
    out = nc.dram_tensor("out_0", (B, T, C), F32, kind="ExternalOutput").ap()
    build(nc, *args, out)
    r = run_bass_kernel_spmd(nc, [{f"in_{k}": v for k, v in arrays.items()}], core_ids=[0])
    return r.results[0]["out_0"]
```
